# Optimizing a Trainium2 kernel written in Bass

```python
import numpy as np
import jax
import jax.numpy as jnp

def _softmax(x, axis=-1):
    return jax.nn.softmax(x, axis=axis)

def _gelu(x):
    return jax.nn.gelu(x, approximate=True)

def _silu(x):
    return jax.nn.silu(x)

def _sigmoid(x):
    return jax.nn.sigmoid(x)

def _layernorm(x, axis=-1, eps=1e-05):
    m = jnp.mean(x, axis=axis, keepdims=True)
    v = jnp.var(x, axis=axis, keepdims=True)
    return (x - m) / jnp.sqrt(v + eps)

def _scatter_add(tgt, idx, src, axis=0):
    return tgt.at[idx].add(src)

def _segment_sum(src, seg, n):
    return jax.ops.segment_sum(src, seg, n)
kernel_name = 'mk_flamingo_gated_d2_seqx_r8_271824'

def setup_inputs(seed: int=0):
    np.random.seed(seed)
    _w = jnp.asarray

    def _rec_inputs():
        import jax
        import jax.numpy as jnp
        _rk = jax.random.key(seed)
        x = -0.0002928 + 1 * jax.random.normal(jax.random.fold_in(_rk, 1), (32, 56, 128), jnp.float32)
        _lenS = 56 - jax.random.randint(jax.random.fold_in(_rk, 7), (32,), 0, max(1, 56 // 4) + 1, jnp.int32)
        _lenS2 = 1500 - jax.random.randint(jax.random.fold_in(_rk, 8), (32,), 0, max(1, 1500 // 4) + 1, jnp.int32)
        _ctx_1024P = jax.random.normal(jax.random.fold_in(_rk, 11), (32, 16, 128), jnp.float32)
        _ctx_1024c = jax.random.dirichlet(jax.random.fold_in(_rk, 511), 0.3 * jnp.ones((16,), jnp.float32), (32, 1500))
        _ctx_1024t = jnp.einsum('bsk,bkd->bsd', _ctx_1024c, _ctx_1024P)
        _ctx_1024t = _ctx_1024t * jax.lax.rsqrt(jnp.mean(jnp.square(_ctx_1024t)) + 1e-12) * 0.953939
        ctx_1024 = -1.39393e-06 + 0.999914 * (_ctx_1024t + 0.3 * jax.random.normal(jax.random.fold_in(_rk, 611), (32, 1500, 128), jnp.float32))
        _validS = jnp.arange(56)[None, :] < _lenS[:, None]
        _validS2 = jnp.arange(1500)[None, :] < _lenS2[:, None]
        _causal = jnp.tril(jnp.ones((56, 56), dtype=bool))
        mask_BxSxS2_bk1 = jnp.broadcast_to(_validS2[:, None, :], (32, 56, 1500))
        _g = jax.random.normal(jax.random.fold_in(_rk, 9001), (2, 2), jnp.float32)
        _g = jnp.sign(_g) * jnp.maximum(jnp.abs(_g), 1.0) + (_g == 0) * 1.0
        g_xattn = _g[0]
        g_ffn = _g[1]
        return (x, ctx_1024, mask_BxSxS2_bk1, g_xattn, g_ffn)
    x, ctx_1024, mask_BxSxS2_bk1, g_xattn, g_ffn = _rec_inputs()

    def _L0_xattn_setup():
        import jax, jax.numpy as jnp
        import numpy as np
        import math
        DIM = 128
        H = 16
        HD = DIM // H // 2
        DEPTH = 4
        LAMBDA_INIT = 0.8 - 0.6 * math.exp(-0.3 * DEPTH)
        SCALE = HD ** (-0.5)
        EPS = 1e-05

        def _sdpa(q, k, v):
            scores = jnp.einsum('bhqd,bhkd->bhqk', q * SCALE, k)
            p = jax.nn.softmax(scores, axis=-1)
            return jnp.einsum('bhqk,bhkd->bhqd', p, v)
        key = jax.random.key(seed)
        ks = jax.random.split(key, 12)
        B, Nq, Nk = (2, 256, 256)
        s = DIM ** (-0.5)
        return {'query': jax.random.normal(ks[0], (B, Nq, DIM), jnp.float32), 'key_': jax.random.normal(ks[1], (B, Nk, DIM), jnp.float32), 'value': jax.random.normal(ks[2], (B, Nk, DIM), jnp.float32), 'Wq': jax.random.normal(ks[3], (DIM, DIM), jnp.float32) * s, 'Wk': jax.random.normal(ks[4], (DIM, DIM), jnp.float32) * s, 'Wv': jax.random.normal(ks[5], (DIM, DIM), jnp.float32) * s, 'Wp': jax.random.normal(ks[6], (DIM, DIM), jnp.float32) * s, 'bp': jnp.zeros((DIM,), jnp.float32), 'lq1': jax.random.normal(ks[7], (HD,), jnp.float32) * 0.1, 'lk1': jax.random.normal(ks[8], (HD,), jnp.float32) * 0.1, 'lq2': jax.random.normal(ks[9], (HD,), jnp.float32) * 0.1, 'lk2': jax.random.normal(ks[10], (HD,), jnp.float32) * 0.1, 'subln_w': jnp.ones((2 * HD,), jnp.float32)}
    _L0_xattn_all = _L0_xattn_setup()
    _L0_xattn_in = {k: v for k, v in _L0_xattn_all.items() if k in ('Wq', 'Wk', 'Wv', 'Wp', 'bp', 'lq1', 'lk1', 'lq2', 'lk2', 'subln_w')}
    del _L0_xattn_all

    def _L0_ffn_setup():
        import jax, jax.numpy as jnp
        import numpy as np
        QMAX = 127.0

        def _quant_dequant(w):
            scale = jnp.max(jnp.abs(w), axis=-1, keepdims=True) / QMAX
            scale = jnp.maximum(scale, 1e-08)
            q = jnp.clip(jnp.round(w / scale), -QMAX, QMAX)
            return q * scale
        key = jax.random.key(seed)
        ks = jax.random.split(key, 7)
        B, S, D, F, E, NS = (2, 256, 128, 256, 8, 1)
        std = 1.0 / np.sqrt(D)
        x = jax.random.normal(ks[0], (B, S, D), dtype=jnp.float32)
        router_w = _quant_dequant(jax.random.normal(ks[1], (E, D), dtype=jnp.float32) * std)
        router_b = jnp.zeros((E,), dtype=jnp.float32)
        w_up = _quant_dequant(jax.random.normal(ks[2], (E, F, D), dtype=jnp.float32) * std)
        w_down = _quant_dequant(jax.random.normal(ks[3], (E, D, F), dtype=jnp.float32) / np.sqrt(F))
        shared_w_up = _quant_dequant(jax.random.normal(ks[4], (NS, F, D), dtype=jnp.float32) * std)
        shared_w_down = _quant_dequant(jax.random.normal(ks[5], (NS, D, F), dtype=jnp.float32) / np.sqrt(F))
        return {'x': x, 'router_w': router_w, 'router_b': router_b, 'w_up': w_up, 'w_down': w_down, 'shared_w_up': shared_w_up, 'shared_w_down': shared_w_down}
    _L0_ffn_all = _L0_ffn_setup()
    _L0_ffn_in = {k: v for k, v in _L0_ffn_all.items() if k in ('router_w', 'router_b', 'w_up', 'w_down', 'shared_w_up', 'shared_w_down')}
    del _L0_ffn_all

    def _L1_xattn_setup():
        import jax, jax.numpy as jnp
        import numpy as np
        B, S, D, H = (2, 256, 128, 16)
        HD = D // H

        def _split_heads(x):
            b, s, _ = x.shape
            return x.reshape(b, s, H, HD).transpose(0, 2, 1, 3)
        key = jax.random.key(seed)
        ks = jax.random.split(key, 12)
        scale = 1.0 / np.sqrt(D)
        inp = {'query': jax.random.normal(ks[0], (B, S, D), jnp.float32), 'key': jax.random.normal(ks[1], (B, S, D), jnp.float32), 'value': jax.random.normal(ks[2], (B, S, D), jnp.float32), 'mask': jnp.broadcast_to(jnp.triu(jnp.ones((S, S), jnp.bool_), k=1), (B, S, S)), 'Wq': jax.random.normal(ks[3], (D, D), jnp.float32) * scale, 'bq': jnp.zeros((D,), jnp.float32), 'Wk': jax.random.normal(ks[4], (D, D), jnp.float32) * scale, 'bk': jnp.zeros((D,), jnp.float32), 'Wv': jax.random.normal(ks[5], (D, D), jnp.float32) * scale, 'bv': jnp.zeros((D,), jnp.float32), 'Wo': jax.random.normal(ks[6], (D, D), jnp.float32) * scale, 'bo': jnp.zeros((D,), jnp.float32)}
        return inp
    _L1_xattn_all = _L1_xattn_setup()
    _L1_xattn_in = {k: v for k, v in _L1_xattn_all.items() if k in ('Wq', 'bq', 'Wk', 'bk', 'Wv', 'bv', 'Wo', 'bo')}
    del _L1_xattn_all

    def _L1_ffn_setup():
        import jax, jax.numpy as jnp
        import numpy as np
        TOP_K = 2
        key = jax.random.key(seed)
        k1, k2, k3, k4 = jax.random.split(key, 4)
        B, T, D, H, E = (2, 256, 128, 256, 8)
        x = jax.random.normal(k1, (B, T, D), dtype=jnp.float32)
        w12 = jax.random.normal(k2, (E, 2 * H, D), dtype=jnp.float32) * D ** (-0.5)
        w3 = jax.random.normal(k3, (E, D, H), dtype=jnp.float32) * H ** (-0.5)
        gate_w = jax.random.normal(k4, (E, D), dtype=jnp.float32) * D ** (-0.5)
        return {'x': x, 'w12': w12, 'w3': w3, 'gate_w': gate_w}
    _L1_ffn_all = _L1_ffn_setup()
    _L1_ffn_in = {k: v for k, v in _L1_ffn_all.items() if k in ('w12', 'w3', 'gate_w')}
    del _L1_ffn_all
    return {'x': x, 'ctx_1024': ctx_1024, 'mask_BxSxS2_bk1': mask_BxSxS2_bk1, 'g_xattn': g_xattn, 'g_ffn': g_ffn, 'L0_xattn_Wq': _L0_xattn_in['Wq'], 'L0_xattn_Wk': _L0_xattn_in['Wk'], 'L0_xattn_Wv': _L0_xattn_in['Wv'], 'L0_xattn_Wp': _L0_xattn_in['Wp'], 'L0_xattn_bp': _L0_xattn_in['bp'], 'L0_xattn_lq1': _L0_xattn_in['lq1'], 'L0_xattn_lk1': _L0_xattn_in['lk1'], 'L0_xattn_lq2': _L0_xattn_in['lq2'], 'L0_xattn_lk2': _L0_xattn_in['lk2'], 'L0_xattn_subln_w': _L0_xattn_in['subln_w'], 'L0_ffn_router_w': _L0_ffn_in['router_w'], 'L0_ffn_router_b': _L0_ffn_in['router_b'], 'L0_ffn_w_up': _L0_ffn_in['w_up'], 'L0_ffn_w_down': _L0_ffn_in['w_down'], 'L0_ffn_shared_w_up': _L0_ffn_in['shared_w_up'], 'L0_ffn_shared_w_down': _L0_ffn_in['shared_w_down'], 'L1_xattn_Wq': _L1_xattn_in['Wq'], 'L1_xattn_bq': _L1_xattn_in['bq'], 'L1_xattn_Wk': _L1_xattn_in['Wk'], 'L1_xattn_bk': _L1_xattn_in['bk'], 'L1_xattn_Wv': _L1_xattn_in['Wv'], 'L1_xattn_bv': _L1_xattn_in['bv'], 'L1_xattn_Wo': _L1_xattn_in['Wo'], 'L1_xattn_bo': _L1_xattn_in['bo'], 'L1_ffn_w12': _L1_ffn_in['w12'], 'L1_ffn_w3': _L1_ffn_in['w3'], 'L1_ffn_gate_w': _L1_ffn_in['gate_w']}

def reference(x, ctx_1024, mask_BxSxS2_bk1, g_xattn, g_ffn, L0_xattn_Wq, L0_xattn_Wk, L0_xattn_Wv, L0_xattn_Wp, L0_xattn_bp, L0_xattn_lq1, L0_xattn_lk1, L0_xattn_lq2, L0_xattn_lk2, L0_xattn_subln_w, L0_ffn_router_w, L0_ffn_router_b, L0_ffn_w_up, L0_ffn_w_down, L0_ffn_shared_w_up, L0_ffn_shared_w_down, L1_xattn_Wq, L1_xattn_bq, L1_xattn_Wk, L1_xattn_bk, L1_xattn_Wv, L1_xattn_bv, L1_xattn_Wo, L1_xattn_bo, L1_ffn_w12, L1_ffn_w3, L1_ffn_gate_w):
    import jax
    import jax.numpy as jnp

    def _L0_xattn_ref(query, key_, value, Wq, Wk, Wv, Wp, bp, lq1, lk1, lq2, lk2, subln_w):
        import jax, jax.numpy as jnp
        import numpy as np
        import math
        DIM = 128
        H = 16
        HD = DIM // H // 2
        DEPTH = 4
        LAMBDA_INIT = 0.8 - 0.6 * math.exp(-0.3 * DEPTH)
        SCALE = HD ** (-0.5)
        EPS = 1e-05

        def _sdpa(q, k, v):
            scores = jnp.einsum('bhqd,bhkd->bhqk', q * SCALE, k)
            p = jax.nn.softmax(scores, axis=-1)
            return jnp.einsum('bhqk,bhkd->bhqd', p, v)
        B, Nq, C = query.shape
        Nk = key_.shape[1]
        q = (query @ Wq.T).reshape(B, Nq, 2 * H, HD).transpose(0, 2, 1, 3)
        k = (key_ @ Wk.T).reshape(B, Nk, 2 * H, HD).transpose(0, 2, 1, 3)
        v = (value @ Wv.T).reshape(B, Nk, H, 2 * HD).transpose(0, 2, 1, 3)
        q1, q2 = (q[:, :H], q[:, H:])
        k1, k2 = (k[:, :H], k[:, H:])
        a1 = _sdpa(q1, k1, v)
        a2 = _sdpa(q2, k2, v)
        lam1 = jnp.exp(jnp.sum(lq1 * lk1))
        lam2 = jnp.exp(jnp.sum(lq2 * lk2))
        lam = lam1 - lam2 + LAMBDA_INIT
        attn = a1 - lam * a2
        attn = attn.transpose(0, 2, 1, 3)
        attn = attn * jax.lax.rsqrt(jnp.mean(attn * attn, axis=-1, keepdims=True) + EPS)
        attn = attn * subln_w
        attn = attn * (1.0 - LAMBDA_INIT)
        attn = attn.reshape(B, Nq, C)
        return attn @ Wp.T + bp

    def _L0_ffn_ref(x, router_w, router_b, w_up, w_down, shared_w_up, shared_w_down):
        import jax, jax.numpy as jnp
        import numpy as np
        QMAX = 127.0

        def _quant_dequant(w):
            scale = jnp.max(jnp.abs(w), axis=-1, keepdims=True) / QMAX
            scale = jnp.maximum(scale, 1e-08)
            q = jnp.clip(jnp.round(w / scale), -QMAX, QMAX)
            return q * scale
        B, S, D = x.shape
        E = router_w.shape[0]
        TOPK = 2
        xt = x.reshape(-1, D)
        logits = xt @ router_w.T + router_b
        probs = jax.nn.softmax(logits, axis=-1)
        top_vals, top_idx = jax.lax.top_k(probs, TOPK)
        top_vals = top_vals / jnp.sum(top_vals, axis=-1, keepdims=True)
        combine = jnp.sum(jax.nn.one_hot(top_idx, E, dtype=xt.dtype) * top_vals[..., None], axis=1)
        h = jnp.einsum('td,efd->tef', xt, w_up)
        y = jnp.einsum('tef,edf->ted', jax.nn.silu(h), w_down)
        out = jnp.einsum('ted,te->td', y, combine)
        hs = jnp.einsum('td,sfd->tsf', xt, shared_w_up)
        out = out + jnp.einsum('tsf,sdf->td', jax.nn.silu(hs), shared_w_down)
        return out.reshape(B, S, D)

    def _L1_xattn_ref(query, key, value, mask, Wq, bq, Wk, bk, Wv, bv, Wo, bo):
        import jax, jax.numpy as jnp
        import numpy as np
        B, S, D, H = (2, 256, 128, 16)
        HD = D // H

        def _split_heads(x):
            b, s, _ = x.shape
            return x.reshape(b, s, H, HD).transpose(0, 2, 1, 3)
        q = _split_heads(query @ Wq.T + bq)
        k = _split_heads(key @ Wk.T + bk)
        v = _split_heads(value @ Wv.T + bv)
        scores = jnp.einsum('bhqd,bhkd->bhqk', q, k) / jnp.sqrt(jnp.float32(HD))
        scores = jnp.where(mask[:, None, :, :], jnp.finfo(scores.dtype).min, scores)
        attn = jax.nn.softmax(scores, axis=-1)
        ctx = jnp.einsum('bhqk,bhkd->bhqd', attn, v)
        merged = ctx.transpose(0, 2, 1, 3).reshape(query.shape[0], -1, D)
        out = merged @ Wo.T + bo
        return out

    def _L1_ffn_ref(x, w12, w3, gate_w):
        import jax, jax.numpy as jnp
        import numpy as np
        TOP_K = 2
        E = gate_w.shape[0]
        H = w3.shape[-1]
        scores = jnp.einsum('btd,ed->bte', x, gate_w)
        topk_scores, topk_idx = jax.lax.top_k(scores, TOP_K)
        topk_probs = jax.nn.softmax(topk_scores, axis=-1)
        total_probs = jnp.sum(jax.nn.one_hot(topk_idx, E, dtype=topk_probs.dtype) * topk_probs[..., None], axis=-2)
        h12 = jnp.einsum('btd,ehd->bteh', x, w12)
        h1, h2 = (h12[..., :H], h12[..., H:])
        hidden = jax.nn.silu(h1) * h2
        expert_out = jnp.einsum('bteh,edh->bted', hidden, w3)
        y = jnp.sum(total_probs[..., None] * expert_out, axis=-2)
        return y
    x = x + jnp.tanh(g_xattn[0]) * _L0_xattn_ref(_layernorm(x, axis=-1), ctx_1024, ctx_1024, L0_xattn_Wq, L0_xattn_Wk, L0_xattn_Wv, L0_xattn_Wp, L0_xattn_bp, L0_xattn_lq1, L0_xattn_lk1, L0_xattn_lq2, L0_xattn_lk2, L0_xattn_subln_w)
    x = x + jnp.tanh(g_ffn[0]) * _L0_ffn_ref(_layernorm(x, axis=-1), L0_ffn_router_w, L0_ffn_router_b, L0_ffn_w_up, L0_ffn_w_down, L0_ffn_shared_w_up, L0_ffn_shared_w_down)
    x = x + jnp.tanh(g_xattn[1]) * _L1_xattn_ref(_layernorm(x, axis=-1), ctx_1024, ctx_1024, mask_BxSxS2_bk1, L1_xattn_Wq, L1_xattn_bq, L1_xattn_Wk, L1_xattn_bk, L1_xattn_Wv, L1_xattn_bv, L1_xattn_Wo, L1_xattn_bo)
    x = x + jnp.tanh(g_ffn[1]) * _L1_ffn_ref(_layernorm(x, axis=-1), L1_ffn_w12, L1_ffn_w3, L1_ffn_gate_w)
    return x

_drawn_inputs = setup_inputs


def setup_inputs(seed=0):
    import zlib

    import numpy as np

    out = dict(_drawn_inputs(seed))
    spreads = {'g_ffn': (-1.0, 0.591),
     'L0_xattn_bp': (0.0, 0.1),
     'L0_xattn_subln_w': (1.0, 0.2),
     'L0_ffn_router_b': (0.0, 0.1),
     'L1_xattn_bq': (0.0, 0.1),
     'L1_xattn_bk': (0.0, 0.8),
     'L1_xattn_bv': (0.0, 0.1),
     'L1_xattn_bo': (0.0, 0.1)}
    factors = {'L0_xattn_lq2': 3.038, 'L0_xattn_lk2': 3.038}
    for name, (base, spread) in spreads.items():
        noise = np.random.default_rng([zlib.crc32(name.encode()), seed]).standard_normal(out[name].shape)
        drawn = base * np.exp(spread * noise) if base else spread * noise
        out[name] = jnp.asarray(drawn.astype(out[name].dtype))
    for name, factor in factors.items():
        out[name] = (out[name] * factor).astype(out[name].dtype)
    return out
```

```python
import math
from contextlib import ExitStack

import numpy as np
import concourse.bass as bass
from concourse import mybir

F32 = mybir.dt.float32
F16 = mybir.dt.float16
U8 = mybir.dt.uint8
ALU = mybir.AluOpType
ACT = mybir.ActivationFunctionType
AX = mybir.AxisListType

B, SQ, D, SK = 32, 56, 128, 1500
TOKENS = B * SQ
TT = 2 * SQ
NTT = TOKENS // TT
CH = 4
NCH = NTT // CH
CW = CH * TT
VH, VD = 16, 8
KT = 125
NKT = SK // KT
THIRD = 4
NTHIRD = NKT // THIRD
TK = THIRD * KT
NE = 8
FF = 256
EPS = 1e-5
LAMBDA_INIT = 0.8 - 0.6 * math.exp(-0.3 * 4)

QK_UP = 64.0
EXP_SCALE = 1.0 / (QK_UP * QK_UP)
BIG = 32768.0
SLOTS = 3


class Layer:

    def __init__(self, name, heads, hd, group_dims, masked):
        self.name = name
        self.heads, self.hd = heads, hd
        self.group_dims = group_dims
        self.groups = D // group_dims
        self.group_heads = group_dims // hd
        self.group_cols = self.group_heads * SQ
        self.masked = masked
        self.mask_rows = SQ if masked else 0
        self.score_rows = 3 * group_dims + self.mask_rows
        self.rows = self.score_rows + 2
        self.cols = heads * SQ
        self.halves = self.cols // 896
        self.half_groups = self.groups // self.halves
        self.pair_tiles = self.cols // TT
        self.pieces = self.pair_tiles * NTHIRD
        self.o_cols = self.cols // 4
        self.uses_f = 2


L0 = Layer("L0", 32, 4, 32, False)
L1 = Layer("L1", 16, 8, 16, True)


def at_least(eng, sem, value):
    if isinstance(value, int) and value <= 0:
        return
    eng.wait_ge(sem, value)


def build(nc, a, out):
    ctx = ExitStack()
    with ctx:
        def sb(name, shape, dt=F32):
            return ctx.enter_context(nc.sbuf_tensor(name, shape, dt))

        def sem(name):
            return ctx.enter_context(nc.semaphore(name))

        score_ps = [ctx.enter_context(nc.psum_tensor(f"score_ps{i}", [128, 2, 512], F32)) for i in range(2)]
        max_ps = [ctx.enter_context(nc.psum_tensor(f"max_ps{i}", [128, 512], F32)) for i in range(2)]
        acc_ps = ctx.enter_context(nc.psum_tensor("acc_ps", [128, 512], F32))
        spare_ps = ctx.enter_context(nc.psum_tensor("spare_ps", [128, 512], F32))
        bank = [score_ps[0][:, 0, :], score_ps[0][:, 1, :], score_ps[1][:, 0, :], score_ps[1][:, 1, :],
                max_ps[0][:, :], max_ps[1][:, :], acc_ps[:, :], spare_ps[:, :]]

        X = sb("X", [TT, NTT, D])
        XnT = sb("XnT", [128, TOKENS])
        attnT = sb("attnT", [128, TOKENS])
        ident = sb("ident", [128, 128])
        neg_half = sb("neg_half", [128, 64])
        tg = sb("tg", [128, 4])
        lam = sb("lam", [SQ, 16])
        keep = sb("keep", [TT, NTT])
        small = {n: sb(n, s) for n, s in (
            ("WqT0", [128, D]), ("WkT0", [128, D]), ("WvT0", [128, D]), ("WpT0", [128, D]),
            ("WqT1", [128, D]), ("WkT1", [128, D]), ("WvT1", [128, D]), ("WpT1", [128, D]),
            ("bp0", [TT, D]), ("bp1", [TT, D]), ("bq1", [TT, D]), ("bv1", [SQ, D]), ("bk1", [128, 1]),
            ("subln", [128, 1]), ("headsel0", [128, L0.group_heads]), ("headsel1", [128, L1.group_heads]),
            ("routerT0", [128, NE]), ("routerT1", [128, NE]), ("router_b", [TT, NE]), ("desc", [TT, NE]))}

        ks_words = L1.groups * SK
        kstack = [sb(f"kstack{i}", [128, ks_words], F16) for i in range(SLOTS)]
        qstack = [sb(f"qstack{i}", [128, L0.cols], F16) for i in range(SLOTS)]
        vext = [sb(f"vext{i}", [KT, NKT, VH // 2, 32]) for i in range(SLOTS)]
        probs = [sb(f"probs{i}", [KT, 2 * 896]) for i in range(2)]
        ctx_in = sb("ctx_in", [KT, NKT, D])
        ctxT = sb("ctxT", [128, SK])
        khl = sb("khl", [128, 2, SK], F16)
        qh = sb("qh", [128, TOKENS], F16)
        ql = sb("ql", [128, TOKENS], F16)
        qblock = [sb(f"qblock{i}", [128, L0.group_cols], F16) for i in range(2)]
        mask_in = sb("mask_in", [SQ, SK], U8)
        mask_big = sb("mask_big", [SQ, SK], F16)
        out_sb = sb("out_sb", [128, L0.o_cols])
        max_part = sb("max_part", [TT, 16, NTHIRD])
        neg_max = sb("neg_max", [TT, 16])
        max_rows = sb("max_rows", [16, 2, TT], F16)
        rden = sb("rden", [SQ, 2, 2, 4])
        heads_out = sb("heads_out", [SQ, 2, VH, VD])
        attn = sb("attn", [SQ, VH, VD])
        attn_sq = sb("attn_sq", [SQ, VH, VD])
        rms = sb("rms", [SQ, 2, VH])
        attn_n = sb("attn_n", [SQ, VH, VD])

        s_in = sem("inputs_loaded")
        s_set = sem("vector_setup")
        s_tanh = sem("tanh_done")
        loads = [(ident[:, :], a["ident"]), (X[:, :, :], a["x"].rearrange("(t p) d -> p t d", p=TT)),
                 (tg[:, 0:2], a["g_xattn"].partition_broadcast(128)),
                 (tg[:, 2:4], a["g_ffn"].partition_broadcast(128)),
                 (small["bp0"][:, :], a["bp0"].partition_broadcast(TT)),
                 (small["bp1"][:, :], a["bp1"].partition_broadcast(TT)),
                 (small["bq1"][:, :], a["bq1"].partition_broadcast(TT)),
                 (small["bv1"][:, :], a["bv1"].partition_broadcast(SQ)),
                 (small["bk1"][:, :], a["bk1"].rearrange("(p o) -> p o", o=1)),
                 (small["router_b"][:, :], a["router_b"].partition_broadcast(TT)),
                 (small["desc"][:, :], a["desc"].partition_broadcast(TT)),
                 (small["headsel0"][:, :], a["headsel0"]), (small["headsel1"][:, :], a["headsel1"]),
                 (small["routerT0"][:, :], a["routerT0"]), (small["routerT1"][:, :], a["routerT1"])]
        loads += [(lam[:, 4 * i:4 * i + 4], a[n].partition_broadcast(SQ)) for i, n in enumerate(("lq1", "lk1", "lq2", "lk2"))]
        loads += [(small[f"W{w}T{i}"][:, :], a[f"W{w}T{i}"]) for i in range(2) for w in "qkvp"]
        loads += [(small["subln"][VD * h:VD * h + VD, :], a["subln"].rearrange("(p o) -> p o", o=1)) for h in range(VH)]

        lam_s = sb("lam_s", [SQ, 8])
        lam_t = sb("lam_t", [SQ, 8])

        with nc.Block() as block:
            @block.sync
            def _(sp):
                for dst, src in loads:
                    sp.dma_start(dst, src).then_inc(s_in, 16)

            @block.gpsimd
            def _(pool):
                for i in range(SLOTS):
                    nc.gpsimd.memset(vext[i][:, :, :, :], 0.0).then_inc(s_set, 1)
                pool.wait_ge(s_set, SLOTS)
                for i in range(SLOTS):
                    for h in range(2):
                        nc.gpsimd.memset(vext[i][:, :, :, 16 * h + VD:16 * h + VD + 1], 1.0)
                nc.gpsimd.memset(neg_half[:, :], -0.5)

            @block.vector
            def _(dve):
                link = chain(dve, sem("setup_chain"))
                dve.wait_ge(s_in, 16 * len(loads))
                link(nc.vector.tensor_tensor(lam_t[:, 0:4], lam[:, 0:4], lam[:, 4:8], ALU.mult))
                link(nc.vector.tensor_tensor(lam_t[:, 4:8], lam[:, 8:12], lam[:, 12:16], ALU.mult))
                nc.vector.reduce_sum(lam_s[:, 0:2], lam_t[:, :].rearrange("p (a b) -> p a b", a=2), AX.X).then_inc(s_tanh, 1)
                dve.wait_ge(s_tanh, 3)
                link(nc.vector.tensor_tensor(lam_s[:, 4:5], lam_s[:, 3:4], lam_s[:, 2:3], ALU.subtract))
                link(nc.vector.tensor_scalar(lam_s[:, 5:6], lam_s[:, 4:5], -LAMBDA_INIT, None, ALU.add))
                link(nc.vector.tensor_scalar(small["WpT0"][:, :], small["WpT0"][:, :], small["subln"][:, :],
                                             1.0 - LAMBDA_INIT, ALU.mult, ALU.mult))
                for i in range(2):
                    link(nc.vector.tensor_scalar(small[f"WpT{i}"][:, :], small[f"WpT{i}"][:, :], tg[:, i:i + 1], None, ALU.mult))
                    link(nc.vector.tensor_scalar(small[f"bp{i}"][:, :], small[f"bp{i}"][:, :], tg[0:TT, i:i + 1], None, ALU.mult))
                    link(nc.vector.tensor_scalar(small[f"WkT{i}"][:, :], small[f"WkT{i}"][:, :], QK_UP, None, ALU.mult))
                link(nc.vector.tensor_scalar(small["bk1"][:, :], small["bk1"][:, :], QK_UP, None, ALU.mult))

            @block.scalar
            def _(act):
                act.wait_ge(s_tanh, 1)
                nc.scalar.activation(lam_s[:, 2:4], lam_s[:, 0:2], ACT.Exp).then_inc(s_tanh, 1)
                nc.scalar.activation(tg[:, :], tg[:, :], ACT.Tanh).then_inc(s_tanh, 1)

        T = dict(nc=nc, a=a, sem=sem, bank=bank, score_ps=score_ps, max_ps=max_ps, acc_ps=acc_ps, spare_ps=spare_ps,
                 X=X, XnT=XnT, attnT=attnT, ident=ident, neg_half=neg_half, tg=tg, small=small, kstack=kstack,
                 qstack=qstack, vext=vext, probs=probs, ctx_in=ctx_in, ctxT=ctxT, khl=khl, qh=qh, ql=ql,
                 qblock=qblock, mask_in=mask_in, mask_big=mask_big, out_sb=out_sb, max_part=max_part,
                 neg_max=neg_max, max_rows=max_rows, rden=rden, heads_out=heads_out, attn=attn, attn_sq=attn_sq,
                 rms=rms, attn_n=attn_n, neg_lam=lam_s[:, 5:6], keep=keep, sb=sb, ctx=ctx)
        normalise(T, "norm0", 0)
        attend(T, L0)
        project(T, 0)
        normalise(T, "norm0f", None)
        feed_forward(T, 0)
        normalise(T, "norm1", 1)
        attend(T, L1)
        project(T, 1)
        normalise(T, "norm1f", None)
        feed_forward(T, 1)

        s_out = sem("result_stored")
        with nc.Block() as block:
            @block.sync
            def _(sp):
                sp.dma_start(out.rearrange("(t p) d -> p t d", p=TT), X[:, :, :]).then_inc(s_out, 16)
                sp.wait_ge(s_out, 16)


def apart(eng):
    eng.nop(nofuse=True)


def chain(eng, s):
    count = [0]

    def link(instruction):
        count[0] += 1
        instruction.then_inc(s, 1)
        eng.wait_ge(s, count[0])
    return link


def carve(words, start, shape):
    n = int(np.prod(shape))
    flat = words[:, 2 * start:2 * (start + n)].bitcast(F32)
    if len(shape) == 1:
        return flat
    if len(shape) == 2:
        return flat.rearrange("p (a b) -> p a b", a=shape[0])
    return flat.rearrange("p (a b c) -> p a b c", a=shape[0], b=shape[1])


def normalise(T, tag, layer):
    nc, a, sem, bank = T["nc"], T["a"], T["sem"], T["bank"]
    X, XnT, ident, small = T["X"], T["XnT"], T["ident"], T["small"]
    xn = carve(T["kstack"][1][0:TT, :], 0, [NTT, D])
    xsq = carve(T["kstack"][2][0:TT, :], 0, [CH, D])
    st = carve(T["kstack"][2][0:TT, :], CH * D, [6, NTT])
    keep = T["keep"]
    s_var = sem(tag + "_variance_ready")
    s_rstd = sem(tag + "_rstd_ready")
    s_xn = sem(tag + "_normalised")
    s_xt = sem(tag + "_transposed")
    s_xnt = sem(tag + "_xnt_ready")
    s_qn = sem(tag + "_queries_projected")
    s_qs = sem(tag + "_queries_scaled")
    s_qt = sem(tag + "_queries_transposed")
    s_qh = sem(tag + "_query_high_ready")
    s_mask = sem(tag + "_mask_loaded")
    head_scale = QK_UP * (L0.hd, L1.hd)[layer or 0] ** -0.5
    mask_row = T["kstack"][0][0:TT, :].bitcast(U8)
    MT = 4

    with nc.Block() as block:
        if layer == 1:
            @block.sync
            def _(sp):
                src = a["mask"].rearrange("(t p) k -> p t k", p=TT)
                for c in range(NTT // MT):
                    sp.dma_start(mask_row[:, c * MT * SK:(c + 1) * MT * SK].rearrange("p (t k) -> p t k", t=MT)
                                 if c < 4 else None, src[:, MT * c:MT * c + MT, :]).then_inc(s_mask, 16)

        @block.vector
        def _(dve):
            link = chain(dve, sem(tag + "_chain"))

            def wide(v):
                return v.unsqueeze(2).to_broadcast([TT, CH, D])

            def first(c):
                x = X[:, CH * c:CH * c + CH, :]
                s = [st[:, k, CH * c:CH * c + CH] for k in range(6)]
                link(nc.vector.reduce_sum(s[0], x, AX.X))
                link(nc.vector.tensor_scalar(s[1], s[0], 1.0 / D, None, ALU.mult))
                link(nc.vector.tensor_tensor(xn[:, CH * c:CH * c + CH, :], x, wide(s[1]), ALU.subtract))
                xm = xn[:, CH * c:CH * c + CH, :]
                link(nc.vector.tensor_tensor(xsq[:, :, :], xm, xm, ALU.mult))
                link(nc.vector.reduce_sum(s[2], xsq[:, :, :], AX.X))
                nc.vector.tensor_scalar(s[3], s[2], 1.0 / D, EPS, ALU.mult, ALU.add).then_inc(s_var, 1)

            def second(c):
                dve.wait_ge(s_rstd, c + 1)
                xm = xn[:, CH * c:CH * c + CH, :]
                nc.vector.tensor_tensor(xm, xm, wide(st[:, 4, CH * c:CH * c + CH]), ALU.mult).then_inc(s_xn, 1)

            for c in range(NCH):
                first(c)
                if c:
                    second(c - 1)
            second(NCH - 1)
            if layer is None:
                return
            if layer == 1:
                dve.wait_ge(s_mask, 16 * (NTT // MT))
                link(nc.vector.tensor_reduce(keep[:, :], mask_row[:, 0:NTT * SK].rearrange("p (t k) -> p t k", t=NTT),
                                             AX.X, ALU.min))
                link(nc.vector.tensor_scalar(keep[:, :], keep[:, :], -head_scale, head_scale, ALU.mult, ALU.add))
                for c in range(NCH):
                    dve.wait_ge(s_qn, c + 1)
                    dst = xn[:, CH * c:CH * c + CH, :]
                    ps = bank[4 + c][0:TT, :].rearrange("p (t d) -> p t d", t=CH)
                    bq = small["bq1"][:, :].unsqueeze(1).to_broadcast([TT, CH, D])
                    link(nc.vector.tensor_tensor(dst, ps, bq, ALU.add))
                    nc.vector.tensor_tensor(dst, dst, wide(keep[:, CH * c:CH * c + CH]), ALU.mult).then_inc(s_qs, 1)
            for c in range(NCH):
                dve.wait_ge(s_qh, c + 1)
                nc.vector.tensor_tensor(T["ql"][:, CW * c:CW * c + CW], bank[c][:, 0:CW],
                                        T["qh"][:, CW * c:CW * c + CW], ALU.subtract)

        @block.gpsimd
        def _(pool):
            for c in range(NCH):
                pool.wait_ge(s_var, c + 1)
                nc.gpsimd.tensor_tensor(st[:, 4, CH * c:CH * c + CH], st[:, 3, CH * c:CH * c + CH],
                                        T["neg_half"][0:TT, 0:CH], ALU.pow).then_inc(s_rstd, 1)

        @block.tensor
        def _(pe):
            for c in range(NCH):
                pe.wait_ge(s_xn, c + 1)
                for t in range(CH):
                    last = nc.tensor.transpose(bank[c][:, TT * t:TT * t + TT], xn[:, CH * c + t, :], ident[0:TT, 0:TT])
                last.then_inc(s_xt, 1)
            if layer is None:
                return
            for c in range(NCH):
                pe.wait_ge(s_xnt, c + 1)
                for t in range(CH):
                    last = nc.tensor.matmul(bank[4 + c][0:TT, D * t:D * t + D],
                                            XnT[:, CW * c + TT * t:CW * c + TT * t + TT],
                                            small[f"WqT{layer}"][:, :], start=True, stop=True)
                last.then_inc(s_qn, 1)
            for c in range(NCH):
                pe.wait_ge(s_qs, c + 1)
                for t in range(CH):
                    last = nc.tensor.transpose(bank[c][:, TT * t:TT * t + TT], xn[:, CH * c + t, :], ident[0:TT, 0:TT])
                last.then_inc(s_qt, 1)

        @block.scalar
        def _(act):
            for c in range(NCH):
                act.wait_ge(s_xt, c + 1)
                nc.scalar.activation(XnT[:, CW * c:CW * c + CW], bank[c][:, 0:CW], ACT.Copy).then_inc(s_xnt, 1)
            if layer is None:
                return
            if layer == 0:
                for c in range(NCH):
                    act.wait_ge(s_qn, c + 1)
                    nc.scalar.activation(xn[:, CH * c:CH * c + CH, :].rearrange("p t d -> p (t d)"), bank[4 + c][0:TT, :],
                                         ACT.Copy, scale=head_scale).then_inc(s_qs, 1)
            for c in range(NCH):
                act.wait_ge(s_qt, c + 1)
                nc.scalar.activation(T["qh"][:, CW * c:CW * c + CW], bank[c][:, 0:CW], ACT.Copy).then_inc(s_qh, 1)


def attend(T, L):
    nc, a, sem, ident, small = T["nc"], T["a"], T["sem"], T["ident"], T["small"]
    score_ps, max_ps, acc_ps, spare_ps = T["score_ps"], T["max_ps"], T["acc_ps"], T["spare_ps"]
    probs, ctx_in, ctxT, khl, vext = T["probs"], T["ctx_in"], T["ctxT"], T["khl"], T["vext"]
    qblock, mask_in, mask_big, out_sb = T["qblock"], T["mask_in"], T["mask_big"], T["out_sb"]
    max_part, neg_max, max_rows = T["max_part"], T["neg_max"], T["max_rows"]
    rden, heads_out, attn, attn_sq, rms, attn_n = (T[k] for k in ("rden", "heads_out", "attn", "attn_sq", "rms", "attn_n"))
    layer = 0 if L is L0 else 1
    GD, NG, GC, H = L.group_dims, L.groups, L.group_cols, L.halves
    kstack = [T["kstack"][i][:, 0:NG * SK].rearrange("p (g k) -> p g k", g=NG) for i in range(SLOTS)]
    qstack = [T["qstack"][i][:, 0:L.cols].rearrange("p (g c) -> p g c", g=NG) for i in range(SLOTS)]
    Wk, Wv = small[f"WkT{layer}"], small[f"WvT{layer}"]
    R = L.rows
    S = heads_sets = L.heads // VH

    s_const = sem(L.name + "_constant_rows")
    s_ctx = sem(L.name + "_context_loaded")
    s_mask = sem(L.name + "_mask_loaded")
    s_big = sem(L.name + "_mask_scaled")
    s_ks = [sem(f"{L.name}_kstack_filled{i}") for i in range(SLOTS)]
    s_qs = [sem(f"{L.name}_qstack_filled{i}") for i in range(SLOTS)]
    s_mrow = [sem(f"{L.name}_maximum_rows_filled{i}") for i in range(SLOTS)]
    s_ctxT = sem(L.name + "_ctxT_ready")
    s_kh = sem(L.name + "_key_high_ready")
    s_kl = sem(L.name + "_key_low_ready")
    s_v = sem(L.name + "_values_ready")
    s_qb = sem(L.name + "_qblock_ready")
    s_ready = sem(L.name + "_spare_filled")
    s_turned = sem(L.name + "_heads_normalised")
    s_at = sem(L.name + "_attnT_ready")
    s_scores = sem(L.name + "_scores_ready")
    s_exp = sem(L.name + "_probs_ready")
    s_av = sem(L.name + "_weighted_values_done")
    s_piece = sem(L.name + "_max_scores_ready")
    s_red = sem(L.name + "_max_reduced")
    s_neg = sem(L.name + "_negative_max_ready")
    s_mr = sem(L.name + "_max_split")
    s_os = sem(L.name + "_output_copied")
    s_attn = sem(L.name + "_attention_normalised")
    s_ms = sem(L.name + "_mean_square_ready")
    s_rs = sem(L.name + "_rms_ready")

    CONST = 16 * SLOTS * NG * (2 if L.masked else 1)

    K_INC = 16 * (3 * NG + (NG if L.masked else 0))
    Q_INC = 16 * 3 * NG
    M_INC = 32
    LAST = NKT - 1

    prep = [("T", 0), ("K", 0), ("T", 1), ("K", 1), ("T", 2), ("K", 2), ("V", 0), ("V", 1), ("V", 2)]
    where = {("T", 0): (0, 0), ("K", 0): (0, 1), ("T", 1): (1, 0), ("K", 1): (1, 1), ("T", 2): (2, 0), ("K", 2): (2, 1),
             ("F", 0): (3, 0), ("F", 1): (3, 1), ("V", 0): (4, 0), ("V", 1): (4, 1), ("V", 2): (5, 0), ("A", 0): (5, 1),
             ("M", 0): (10 if H == 2 else 9, 0)}
    per_step = 5 if H == 2 else 3
    turnaround = [("F", i) for i in range(L.uses_f)] + [("A", 0)]

    def spare_uses(has_f, has_m, has_p):
        uses = (prep if has_p else []) + (turnaround if has_f else []) + ([("M", 0)] if has_m else [])
        return sorted(uses, key=lambda u: where[u])

    FULL = len(spare_uses(True, True, True))
    PROLOGUE = 2 * len(prep) + 1
    FIRST = PROLOGUE + len(prep) + 1

    LOOPS = (B - 5) // SLOTS

    class At:

        def __init__(self, j, c):
            self.j, self.c = j, c
            self.n = j * SLOTS + c
            self.slot = c % SLOTS
            self.turn = j + c // SLOTS

        def plus(self, d):
            return At(self.j, self.c + d)

    def iterations(eng, body, prologue=None, epilogue=None):
        if prologue:
            prologue()
        body(At(0, 0), PROLOGUE, spare_uses(False, True, True), False, True, True)
        with eng.Fori(0, LOOPS) as j:
            for c in range(1, 1 + SLOTS):
                at = At(j, c)
                body(at, (at.n - 1) * FULL + FIRST, spare_uses(True, True, True), True, True, True)
        before = FIRST + SLOTS * LOOPS * FULL
        for n in range(SLOTS * LOOPS + 1, B):
            has_m, has_p = n + 1 < B, n + 2 < B
            uses = spare_uses(True, has_m, has_p)
            body(At(0, n), before, uses, True, has_m, has_p)
            before += len(uses)
        if epilogue:
            epilogue(before)

    def copied_out(at, kind, i):
        p = at.plus(2)
        return {"T": (s_ctxT, NTHIRD * p.n + i + 1), "K": (s_kl, NTHIRD * p.n + i + 1),
                "V": (s_v, NTHIRD * p.n + i + 1), "M": (s_mr, at.n + 2),
                "F": (s_turned, (at.n - 1) * L.uses_f + i + 1), "A": (s_at, at.n)}[kind]

    def at_step(uses, base, t, side):
        return [(kind, i, base + k) for k, (kind, i) in enumerate(uses) if where[kind, i] == (t, side)]

    def pieces_of(t, part):
        first = min(t * per_step, L.pieces)
        last = min((t + 1) * per_step, L.pieces)
        cut = min(first + (2 if H == 2 else 1), last)
        return range(first, cut) if part == 0 else range(cut, last)

    with nc.Block() as block:
        @block.sync
        def _(sp):
            for i in range(SLOTS):
                for g in range(NG):
                    sp.dma_start(kstack[i][R - 2:R, g, :], a["ones_rows"]).then_inc(s_const, 16)
                if L.masked:
                    for g in range(NG):
                        sp.dma_start(qstack[i][3 * GD:3 * GD + SQ, g, :], a["big_ident"]).then_inc(s_const, 16)
            sp.wait_ge(s_const, CONST)

            def load(at):
                sp.dma_start(ctx_in[:, :, :],
                             a["ctx"][bass.ds(at.n, 1), :, :].rearrange("b (p t) d -> (b p) t d", t=NKT)).then_inc(s_ctx, 16)
                if L.masked:
                    at_least(sp, s_big, at.n)
                    sp.dma_start(mask_in[:, :], a["mask"][bass.ds(at.n * SQ, SQ), :]).then_inc(s_mask, 16)

            def fill_q(at):
                sp.wait_ge(s_qb, at.n + 1)
                apart(sp)
                at_least(sp, s_scores, (at.n - 2) * NKT * H)
                for g in range(NG):
                    for row, part in ((0, 0), (GD, 1), (2 * GD, 0)):
                        sp.dma_start(qstack[at.slot][row:row + GD, g, :],
                                     qblock[part][GD * g:GD * g + GD, 0:GC]).then_inc(s_qs[at.slot], 16)

            def fill_k(at):
                sp.wait_ge(s_kl, NTHIRD * (at.n + 1))
                for g in range(NG):
                    for row, part in ((0, 0), (GD, 0), (2 * GD, 1)):
                        sp.dma_start(kstack[at.slot][row:row + GD, g, :],
                                     khl[GD * g:GD * g + GD, part, :]).then_inc(s_ks[at.slot], 16)
                if L.masked:
                    sp.wait_ge(s_big, at.n + 1)
                    for g in range(NG):
                        sp.dma_start(kstack[at.slot][3 * GD:3 * GD + SQ, g, :], mask_big[:, :]).then_inc(s_ks[at.slot], 16)

            def fill_m(at):
                sp.wait_ge(s_mr, at.n + 1)
                for part in range(2):
                    row = L.score_rows + part
                    sp.dma_start(T["qstack"][at.slot][row:row + 1, 0:L.cols],
                                 max_rows[0:L.pair_tiles, part, :]).then_inc(s_mrow[at.slot], 16)

            def prologue():
                load(At(0, 0))
                for n in range(2):
                    sp.wait_ge(s_ctxT, NTHIRD * (n + 1))
                    load(At(0, n + 1))
                    fill_q(At(0, n))
                    fill_k(At(0, n))
                fill_m(At(0, 0))

            def body(at, base, uses, has_f, has_m, has_p):
                if has_p:
                    sp.wait_ge(s_ctxT, NTHIRD * (at.n + 3))
                    if not (isinstance(at.n, int) and at.n + 3 >= B):
                        load(at.plus(3))
                    fill_q(at.plus(2))
                    fill_k(at.plus(2))
                if has_m:
                    fill_m(at.plus(1))

            iterations(sp, body, prologue)

        @block.gpsimd
        def _(pool):
            sel = small[f"headsel{layer}"]

            def prepare(at):
                prev = at.plus(-1)
                if not (isinstance(at.n, int) and at.n == 0):
                    pool.wait_ge(s_qs[prev.slot], Q_INC * (prev.turn + 1))
                apart(pool)
                for part, src in enumerate((T["qh"], T["ql"])):
                    q = src[:, bass.ds(at.n * SQ, SQ)]
                    last = nc.gpsimd.tensor_tensor(
                        qblock[part][:, 0:GC].rearrange("p (h q) -> p h q", q=SQ),
                        q.unsqueeze(1).to_broadcast([128, L.group_heads, SQ]),
                        sel[:, :].unsqueeze(2).to_broadcast([128, L.group_heads, SQ]), ALU.mult)
                last.then_inc(s_qb, 1)
                if L.masked:
                    pool.wait_ge(s_mask, 16 * (at.n + 1))
                    if not (isinstance(at.n, int) and at.n == 0):
                        pool.wait_ge(s_ks[prev.slot], K_INC * (prev.turn + 1))
                    apart(pool)
                    nc.gpsimd.tensor_scalar(mask_big[:, :].rearrange("q (t p) -> q t p", t=NKT),
                                            mask_in[:, :].rearrange("q (p t) -> q t p", t=NKT),
                                            -BIG, None, ALU.mult).then_inc(s_big, 1)

            def rms_power(n):
                if L is L0:
                    pool.wait_ge(s_ms, n)
                    nc.gpsimd.tensor_tensor(rms[:, 1, :], rms[:, 0, :], T["neg_half"][0:SQ, 0:VH], ALU.pow).then_inc(s_rs, 1)

            def body(at, base, uses, has_f, has_m, has_p):
                if has_p:
                    prepare(at.plus(2))
                if has_f:
                    rms_power(at.n)

            iterations(pool, body, lambda: (prepare(At(0, 0)), prepare(At(0, 1))), lambda before: rms_power(B))

        @block.tensor
        def _(pe):
            pe.wait_ge(s_const, CONST)

            def use(at, kind, i, before):
                if before:
                    pe.wait_ge(*copied_out(*before))
                p = at.plus(2)
                if kind == "T":
                    if i == 0:
                        pe.wait_ge(s_ctx, 16 * (p.n + 1))
                    for t in range(THIRD):
                        last = nc.tensor.transpose(spare_ps[:, KT * t:KT * t + KT], ctx_in[:, THIRD * i + t, :], ident[0:KT, 0:KT])
                    last.then_inc(s_ready, 1)
                if kind == "K":
                    pe.wait_ge(s_ctxT, NTHIRD * p.n + i + 1)
                    nc.tensor.matmul(spare_ps[:, 0:TK], Wk[:, :], ctxT[:, TK * i:TK * i + TK], start=True, stop=True).then_inc(s_ready, 1)
                if kind == "V":
                    for t in range(THIRD):
                        k = TK * i + KT * t
                        last = nc.tensor.matmul(spare_ps[0:KT, D * t:D * t + D], ctxT[:, k:k + KT], Wv[:, :], start=True, stop=True)
                    last.then_inc(s_ready, 1)
                if kind == "M":
                    pe.wait_ge(s_neg, at.n + 2)
                    nc.tensor.transpose(spare_ps[0:L.pair_tiles, 0:TT], neg_max[:, 0:L.pair_tiles], ident[0:TT, 0:TT]).then_inc(s_ready, 1)
                if kind == "F":
                    pe.wait_ge(s_os, at.n)
                    apart(pe)
                    for b in range(2 * S):
                        k = (i * 2 * S + b) * SQ
                        last = nc.tensor.transpose(spare_ps[0:SQ, 128 * b:128 * b + 128], out_sb[:, k:k + SQ], ident[:, :])
                    last.then_inc(s_ready, 1)
                if kind == "A":
                    pe.wait_ge(s_attn, at.n)
                    apart(pe)
                    nc.tensor.transpose(spare_ps[:, 0:SQ], attn_n[:, :, :].rearrange("q h d -> q (h d)"), ident[0:SQ, 0:SQ]).then_inc(s_ready, 1)

            def search(at, p):
                u, third = p // NTHIRD, p % NTHIRD
                g = u * TT // GC
                if p == 0:
                    pe.wait_ge(s_ks[at.slot], K_INC * (at.turn + 1))
                    pe.wait_ge(s_qs[at.slot], Q_INC * (at.turn + 1))
                at_least(pe, s_red, at.n * L.pieces + p - 1)
                nc.tensor.matmul(max_ps[p % 2][0:TT, 0:TK], T["qstack"][at.slot][0:L.score_rows, TT * u:TT * u + TT],
                                 kstack[at.slot][0:L.score_rows, g, TK * third:TK * third + TK],
                                 start=True, stop=True).then_inc(s_piece, 1)

            def scores(at, t, h):
                number = (at.n * NKT + t) * H + h
                at_least(pe, s_exp, number - 1)
                if t == 0 and h == 0:
                    pe.wait_ge(s_mrow[at.slot], M_INC * (at.turn + 1))
                buf = score_ps[number_parity(t, h)]
                for k in range(L.half_groups):
                    g = h * L.half_groups + k
                    per_bank = L.half_groups // 2
                    o = (k % per_bank) * GC
                    last = nc.tensor.matmul(buf[0:KT, k // per_bank, o:o + GC], kstack[at.slot][0:R, g, KT * t:KT * t + KT],
                                            qstack[at.slot][0:R, g, :], start=True, stop=True)
                last.then_inc(s_scores, 1)

            def number_parity(t, h):
                return (t * H + h) % 2

            def weigh(at, t):
                pe.wait_ge(s_exp, (at.n * NKT + t + 1) * H)
                if t == 0:
                    at_least(pe, s_os, at.n)
                    pe.wait_ge(s_v, NTHIRD * (at.n + 1))
                for i in range(2):
                    for j in range(4):
                        u = 4 * i + j
                        moving = probs[t % 2][:, 0:S * 896].rearrange("k (s c) -> k s c", s=S)[:, :, TT * u:TT * u + TT]
                        last = nc.tensor.matmul(
                            acc_ps[32 * j:32 * j + 32, TT * S * i:TT * S * (i + 1)].rearrange("p (s c) -> p s c", s=S),
                            vext[at.slot][:, t, u, :], moving, start=(t == 0 and i == 0), stop=(t == LAST),
                            skip_group_check=True)
                last.then_inc(s_av, 1)

            def prologue():
                before = None
                for n in range(2):
                    for kind, i in prep:
                        use(At(0, n - 2), kind, i, before)
                        before = (At(0, n - 2), kind, i)
                for p in range(L.pieces):
                    search(At(0, 0), p)
                use(At(0, -1), "M", 0, before)

            def body(at, base, uses, has_f, has_m, has_p):
                before = (at.plus(-1), "M", 0)

                def step_uses(t, side):
                    nonlocal before
                    for kind, i, _ in at_step(uses, base, t, side):
                        use(at, kind, i, before)
                        before = (at, kind, i)

                for t in range(NKT):
                    step_uses(t, 0)
                    for h in range(H):
                        scores(at, t, h)
                        if h == 0 and has_m:
                            for p in pieces_of(t, 0):
                                search(at.plus(1), p)
                    if t:
                        weigh(at, t - 1)
                    elif has_f:
                        weigh(at.plus(-1), LAST)
                    if has_m:
                        for p in pieces_of(t, 1):
                            search(at.plus(1), p)
                    step_uses(t, 1)

            def epilogue(base):
                weigh(At(0, B - 1), LAST)
                before = (At(0, B - 1), "A", 0)
                for kind, i in turnaround:
                    use(At(0, B), kind, i, before)
                    before = (At(0, B), kind, i)

            iterations(pe, body, prologue, epilogue)

        @block.scalar
        def _(act):
            def drain(at, kind, i, number):
                p = at.plus(2)
                if kind in "MF":
                    return
                act.wait_ge(s_ready, number + 1)
                if kind == "T":
                    nc.scalar.activation(ctxT[:, TK * i:TK * i + TK], spare_ps[:, 0:TK], ACT.Copy).then_inc(s_ctxT, 1)
                if kind == "K":
                    if i == 0 and not (isinstance(p.n, int) and p.n == 0):
                        prev = p.plus(-1)
                        act.wait_ge(s_ks[prev.slot], K_INC * (prev.turn + 1))
                    if L is L0:
                        nc.scalar.activation(khl[:, 0, TK * i:TK * i + TK], spare_ps[:, 0:TK], ACT.Copy).then_inc(s_kh, 1)
                    else:
                        nc.scalar.activation(khl[:, 0, TK * i:TK * i + TK], spare_ps[:, 0:TK], ACT.Identity,
                                             bias=small["bk1"][:, :]).then_inc(s_kh, 1)
                if kind == "V":
                    nc.scalar.activation(
                        vext[p.slot][:, THIRD * i:THIRD * i + THIRD, :, :].rearrange("k t u (a e) -> k t (u a) e", a=2)[:, :, :, 0:VD],
                        spare_ps[0:KT, :].rearrange("k (t h d) -> k t h d", t=THIRD, d=VD), ACT.Copy).then_inc(s_v, 1)
                if kind == "A":
                    nc.scalar.activation(T["attnT"][:, bass.ds((at.n - 1) * SQ, SQ)], spare_ps[:, 0:SQ], ACT.Copy).then_inc(s_at, 1)

            def exps(at, t, h):
                number = (at.n * NKT + t) * H + h
                act.wait_ge(s_scores, number + 1)
                if h == 0:
                    at_least(act, s_av, at.n * NKT + t - 1)
                nc.scalar.activation(probs[t % 2][:, 896 * h:896 * h + 896].rearrange("k (b c) -> k b c", b=2),
                                     score_ps[(t * H + h) % 2][0:KT, :, 0:448], ACT.Exp, scale=EXP_SCALE).then_inc(s_exp, 1)

            def copy_output(n):
                act.wait_ge(s_av, n * NKT)
                nc.scalar.activation(out_sb[:, 0:L.o_cols], acc_ps[:, 0:L.o_cols], ACT.Copy).then_inc(s_os, 1)

            def prologue():
                number = 0
                for n in range(2):
                    for kind, i in prep:
                        drain(At(0, n - 2), kind, i, number)
                        number += 1

            def body(at, base, uses, has_f, has_m, has_p):
                for t in range(NKT):
                    for kind, i, number in at_step(uses, base, t, 0):
                        drain(at, kind, i, number)
                    for h in range(H):
                        exps(at, t, h)
                    if t == 0 and has_f:
                        copy_output(at.n)
                    for kind, i, number in at_step(uses, base, t, 1):
                        drain(at, kind, i, number)

            def epilogue(before):
                copy_output(B)
                for k, (kind, i) in enumerate(turnaround):
                    drain(At(0, B), kind, i, before + k)

            iterations(act, body, prologue, epilogue)

        s_chain = sem(L.name + "_normalisation_chain")
        s_high = sem(L.name + "_max_high_ready")
        LINKS = L.uses_f * 3 + (3 if L is L0 else 0)

        @block.vector
        def _(dve):
            def drain(at, kind, i, number):
                if kind in "TVA":
                    return
                dve.wait_ge(s_ready, number + 1)
                if kind == "K":
                    p = at.plus(2)
                    dve.wait_ge(s_kh, NTHIRD * p.n + i + 1)
                    if L is L0:
                        nc.vector.tensor_tensor(khl[:, 1, TK * i:TK * i + TK], spare_ps[:, 0:TK],
                                                khl[:, 0, TK * i:TK * i + TK], ALU.subtract).then_inc(s_kl, 1)
                    else:
                        nc.vector.scalar_tensor_tensor(khl[:, 1, TK * i:TK * i + TK], spare_ps[:, 0:TK], small["bk1"][:, :],
                                                       khl[:, 0, TK * i:TK * i + TK], ALU.add, ALU.subtract).then_inc(s_kl, 1)
                if kind == "M":
                    m = at.plus(1)
                    high, low = max_rows[0:L.pair_tiles, 0, :], max_rows[0:L.pair_tiles, 1, :]
                    nc.vector.tensor_scalar(high, spare_ps[0:L.pair_tiles, 0:TT], 1.0 / BIG, None, ALU.mult).then_inc(s_high, 1)
                    dve.wait_ge(s_high, m.n + 1)
                    nc.vector.scalar_tensor_tensor(low, high, -BIG, spare_ps[0:L.pair_tiles, 0:TT],
                                                   ALU.mult, ALU.add).then_inc(s_mr, 1)
                if kind == "F":
                    link = linked(at)
                    turned = spare_ps[0:SQ, 0:256 * S].rearrange("q (s a j e) -> q s a j e", s=S, a=2, j=4)
                    for h in range(2):
                        link(nc.vector.reciprocal(rden[:, h, 0:S, :], turned[:, :, h, :, 16 * h + VD]))
                    for h in range(2):
                        last = nc.vector.tensor_tensor(
                            heads_out[:, 0:S, :, :].rearrange("q s (i j a) d -> q s i j a d", i=2, a=2)[:, :, i, :, h, :],
                            turned[:, :, h, :, 16 * h:16 * h + VD],
                            rden[:, h, 0:S, :].unsqueeze(3).to_broadcast([SQ, S, 4, VD]), ALU.mult)
                        if h == 0:
                            link(last)
                    last.then_inc(s_turned, 1)
                    if i == L.uses_f - 1:
                        dve.wait_ge(s_turned, at.n * L.uses_f)
                        if L is L0:
                            link(nc.vector.scalar_tensor_tensor(attn[:, :, :], heads_out[:, 1, :, :], T["neg_lam"],
                                                                heads_out[:, 0, :, :], ALU.mult, ALU.add))
                            link(nc.vector.tensor_tensor(attn_sq[:, :, :], attn[:, :, :], attn[:, :, :], ALU.mult))
                            link(nc.vector.reduce_sum(rms[:, 0, :], attn_sq[:, :, :], AX.X))
                            nc.vector.tensor_scalar(rms[:, 0, :], rms[:, 0, :], 1.0 / VD, EPS, ALU.mult, ALU.add).then_inc(s_ms, 1)

            links = {}

            def linked(at):
                if links.get("at") is not at:
                    links.update(at=at, count=0)

                def link(instruction):
                    links["count"] += 1
                    instruction.then_inc(s_chain, 1)
                    dve.wait_ge(s_chain, (at.n - 1) * LINKS + links["count"])
                return link

            def finish(at):
                if L is L0:
                    dve.wait_ge(s_rs, at.n)
                    nc.vector.tensor_tensor(attn_n[:, :, :], attn[:, :, :], rms[:, 1, :].unsqueeze(2).to_broadcast([SQ, VH, VD]),
                                            ALU.mult).then_inc(s_attn, 1)
                else:
                    nc.vector.tensor_tensor(attn_n[:, :, :].rearrange("q h d -> q (h d)"),
                                            heads_out[:, 0, :, :].rearrange("q h d -> q (h d)"),
                                            small["bv1"][:, :], ALU.add).then_inc(s_attn, 1)

            def reduce_piece(at, p):
                dve.wait_ge(s_piece, at.n * L.pieces + p + 1)
                nc.vector.reduce_max(max_part[:, p // NTHIRD, p % NTHIRD:p % NTHIRD + 1], max_ps[p % 2][0:TT, 0:TK],
                                     AX.X).then_inc(s_red, 1)
                if p == L.pieces - 1:
                    dve.wait_ge(s_red, (at.n + 1) * L.pieces)
                    nc.vector.tensor_reduce(neg_max[:, 0:L.pair_tiles], max_part[:, 0:L.pair_tiles, :], AX.X, ALU.max,
                                            negate=True).then_inc(s_neg, 1)

            def prologue():
                number = 0
                for n in range(2):
                    for kind, i in prep:
                        drain(At(0, n - 2), kind, i, number)
                        number += 1
                for p in range(L.pieces):
                    reduce_piece(At(0, 0), p)
                drain(At(0, -1), "M", 0, number)

            def body(at, base, uses, has_f, has_m, has_p):
                for t in range(NKT):
                    for kind, i, number in at_step(uses, base, t, 0):
                        drain(at, kind, i, number)
                    if has_m:
                        for p in (*pieces_of(t, 0), *pieces_of(t, 1)):
                            reduce_piece(at.plus(1), p)
                    if t == where["A", 0][0] and has_f:
                        finish(at)
                    for kind, i, number in at_step(uses, base, t, 1):
                        drain(at, kind, i, number)

            def epilogue(before):
                for k, (kind, i) in enumerate(turnaround):
                    if kind == "A":
                        finish(At(0, B))
                    drain(last_at, kind, i, before + k)

            last_at = At(0, B)
            iterations(dve, body, prologue, epilogue)


def project(T, layer):
    nc, sem, bank, X, small = T["nc"], T["sem"], T["bank"], T["X"], T["small"]
    s_ps = sem(f"p{layer}_projected")
    s_x = sem(f"p{layer}_bias_added")
    with nc.Block() as block:
        @block.tensor
        def _(pe):
            for c in range(NCH):
                for t in range(CH):
                    k = CW * c + TT * t
                    last = nc.tensor.matmul(bank[c][0:TT, D * t:D * t + D], T["attnT"][:, k:k + TT], small[f"WpT{layer}"][:, :],
                                            start=True, stop=True)
                last.then_inc(s_ps, 1)

        @block.vector
        def _(dve):
            for c in range(NCH):
                x = X[:, CH * c:CH * c + CH, :]
                nc.vector.tensor_tensor(x, x, small[f"bp{layer}"][:, :].unsqueeze(1).to_broadcast([TT, CH, D]), ALU.add).then_inc(s_x, 1)
            for c in range(NCH):
                x = X[:, CH * c:CH * c + CH, :]
                dve.wait_ge(s_x, c + 1)
                dve.wait_ge(s_ps, c + 1)
                nc.vector.tensor_tensor(x, bank[c][0:TT, :].rearrange("p (t d) -> p t d", t=CH), x, ALU.add)


def feed_forward(T, layer):
    nc, a, sem, bank, X, XnT, small = T["nc"], T["a"], T["sem"], T["bank"], T["X"], T["XnT"], T["small"]
    NX = NE + 1 if layer == 0 else NE
    UP = FF * (1 if layer == 0 else 2)
    NF = FF // 128
    gated = layer == 1
    UB = 2 if gated else 3
    DB = 2 if gated else 3
    HS = 4 if gated else 6
    assert NX * NF % UB == NX * NF % HS == NX % DB == 0
    n = f"f{layer}_"
    s_w = sem(n + "weights_loaded")
    s_lg = sem(n + "logits_ready")
    s_d = sem(n + "logit_difference_ready")
    s_e = sem(n + "second_weight_ready")
    s_up = sem(n + "hidden_projected")
    s_si = sem(n + "silu_done")
    s_hid = sem(n + "hidden_ready") if gated else s_si
    s_dn = sem(n + "expert_projected")
    s_tmp = sem(n + "weighted")
    s_acc = sem(n + "accumulated")
    s_zero = sem(n + "total_zeroed")
    k0, k1, k2 = (T["kstack"][i][:, :] for i in range(3))
    wup = carve(k0, 0, [NX, UP])
    wdn = carve(k1, 0, [NX, NF, D])
    total = carve(k2[0:TT, :], 0, [NTT, D])
    hidden = [carve(k2, NTT * D + CW * i, [CW]) for i in range(HS)]
    gate = [T["ctxT"][:, CW * i:CW * i + CW] for i in range(2)]
    tmp = [T["probs"][0][0:TT, CH * D * i:CH * D * i + CH * D].rearrange("p (t d) -> p t d", t=CH) for i in range(DB)]
    row = T["probs"][1][0:TT, :]
    lg, *r = [row[:, NTT * NE * i:NTT * NE * (i + 1)].rearrange("p (t e) -> p t e", e=NE) for i in range(5)]
    comb = row[:, 640:640 + NTT * (NE + 1)].rearrange("p (t e) -> p t e", e=NE + 1)
    m = row[:, 800:800 + 8 * NTT].rearrange("p (k t) -> p k t", k=8)

    with nc.Block() as block:
        @block.sync
        def _(sp):
            sp.dma_start(wup[:, :, :], a[f"wup{layer}"]).then_inc(s_w, 16)
            sp.dma_start(wdn[:, :, :, :], a[f"wdn{layer}"]).then_inc(s_w, 16)

        def before_hidden(c, u):
            return c * NX + (u - HS) // NF + 1

        def steps(eng, body):
            body(0)
            with eng.Fori(1, NCH) as c:
                body(c)

        @block.tensor
        def _(pe):
            for t in range(NTT):
                last = nc.tensor.matmul(bank[7][0:TT, NE * t:NE * t + NE], XnT[:, TT * t:TT * t + TT],
                                        small[f"routerT{layer}"][:, :], start=True, stop=True)
            last.then_inc(s_lg, 1)
            pe.wait_ge(s_w, 32)

            def up(c, e):
                x = XnT[:, bass.ds(c * CW, CW)]
                for f in range(NF):
                    u = e * NF + f
                    number = c * (NX * NF) + u
                    at_least(pe, s_hid, number - UB + 1)
                    if gated:
                        nc.tensor.matmul(bank[2 * (u % UB)][:, 0:CW], wup[:, e, 128 * f:128 * f + 128], x, start=True, stop=True)
                        last = nc.tensor.matmul(bank[2 * (u % UB) + 1][:, 0:CW], wup[:, e, FF + 128 * f:FF + 128 * f + 128], x,
                                                start=True, stop=True)
                    else:
                        last = nc.tensor.matmul(bank[u % UB][:, 0:CW], wup[:, e, 128 * f:128 * f + 128], x, start=True, stop=True)
                    last.then_inc(s_up, 1)

            def down(c, e):
                number = c * NX + e
                pe.wait_ge(s_hid, (number + 1) * NF)
                at_least(pe, s_tmp, number - DB + 1)
                for t in range(CH):
                    for f in range(NF):
                        last = nc.tensor.matmul(bank[4 + e % DB - (0 if gated else 1)][0:TT, D * t:D * t + D],
                                                hidden[(e * NF + f) % HS][:, TT * t:TT * t + TT], wdn[:, e, f, :],
                                                start=f == 0, stop=f == NF - 1)
                last.then_inc(s_dn, 1)

            def chunk(c):
                for e in range(NX):
                    up(c, e)
                    if e:
                        down(c, e - 1)
                down(c, NX - 1)
            steps(pe, chunk)

        @block.scalar
        def _(act):
            act.wait_ge(s_d, 1)
            nc.scalar.activation(m[:, 3, :], m[:, 2, :], ACT.Exp).then_inc(s_e, 1)

            def chunk(c):
                for u in range(NX * NF):
                    number = c * (NX * NF) + u
                    act.wait_ge(s_up, number + 1)
                    if gated:
                        at_least(act, s_hid, number - 1)
                        nc.scalar.activation(gate[u % 2][:, :], bank[2 * (u % UB)][:, 0:CW], ACT.Silu).then_inc(s_si, 1)
                    else:
                        if not (isinstance(c, int) and number < HS):
                            act.wait_ge(s_dn, before_hidden(c, u))
                        nc.scalar.activation(hidden[u % HS][:, :], bank[u % UB][:, 0:CW], ACT.Silu).then_inc(s_si, 1)
            steps(act, chunk)

        @block.vector
        def _(dve):
            link = chain(dve, sem(n + "chain"))

            def over(v):
                return v.unsqueeze(2).to_broadcast([TT, NTT, NE])

            dve.wait_ge(s_lg, 1)
            logits = bank[7][0:TT, 0:NTT * NE].rearrange("p (t e) -> p t e", e=NE)
            desc = small["desc"][:, :].unsqueeze(1).to_broadcast([TT, NTT, NE])
            if layer == 0:
                link(nc.vector.tensor_tensor(lg[:, :, :], logits, small["router_b"][:, :].unsqueeze(1).to_broadcast([TT, NTT, NE]), ALU.add))
            else:
                link(nc.vector.tensor_copy(lg[:, :, :], logits))
            cur = lg
            for k in range(2):
                link(nc.vector.reduce_max(m[:, k, :], cur[:, :, :], AX.X))
                link(nc.vector.tensor_tensor(r[2][:, :, :], cur[:, :, :], over(m[:, k, :]), ALU.is_equal))
                link(nc.vector.tensor_tensor(r[2][:, :, :], r[2][:, :, :], desc, ALU.mult))
                link(nc.vector.reduce_max(m[:, 4, :], r[2][:, :, :], AX.X))
                link(nc.vector.tensor_tensor(r[k][:, :, :], r[2][:, :, :], over(m[:, 4, :]), ALU.is_equal))
                if k == 0:
                    link(nc.vector.scalar_tensor_tensor(r[3][:, :, :], r[0][:, :, :], -1e30, lg[:, :, :], ALU.mult, ALU.add))
                    cur = r[3]
            nc.vector.tensor_tensor(m[:, 2, :], m[:, 1, :], m[:, 0, :], ALU.subtract).then_inc(s_d, 1)
            dve.wait_ge(s_e, 1)
            link(nc.vector.tensor_scalar(m[:, 5, :], m[:, 3, :], 1.0, None, ALU.add))
            link(nc.vector.reciprocal(m[:, 6, :], m[:, 5, :]))
            link(nc.vector.tensor_tensor(m[:, 7, :], m[:, 6, :], m[:, 3, :], ALU.mult))
            link(nc.vector.tensor_tensor(r[2][:, :, :], r[0][:, :, :], over(m[:, 6, :]), ALU.mult))
            link(nc.vector.tensor_tensor(r[3][:, :, :], r[1][:, :, :], over(m[:, 7, :]), ALU.mult))
            link(nc.vector.memset(comb[:, :, NE:NE + 1], 1.0))
            link(nc.vector.tensor_tensor(comb[:, :, 0:NE], r[2][:, :, :], r[3][:, :, :], ALU.add))

            def take(c, e):
                number = c * NX + e
                dve.wait_ge(s_dn, number + 1)
                w = comb[:, bass.ds(c * CH, CH), e:e + 1].to_broadcast([TT, CH, D])
                at_least(dve, s_acc, number - DB + 1)
                nc.vector.tensor_tensor(tmp[e % DB][:, :, :],
                                        bank[4 + e % DB - (0 if gated else 1)][0:TT, :].rearrange("p (t d) -> p t d", t=CH),
                                        w, ALU.mult).then_inc(s_tmp, 1)

            def chunk(c):
                for e in range(NX):
                    if gated:
                        for f in range(NF):
                            u = e * NF + f
                            number = c * (NX * NF) + u
                            dve.wait_ge(s_si, number + 1)
                            if not (isinstance(c, int) and number < HS):
                                dve.wait_ge(s_dn, before_hidden(c, u))
                            nc.vector.tensor_tensor(hidden[u % HS][:, :], bank[2 * (u % UB) + 1][:, 0:CW], gate[u % 2][:, :],
                                                    ALU.mult).then_inc(s_hid, 1)
                    if e:
                        take(c, e - 1)
                take(c, NX - 1)
            steps(dve, chunk)
            g = T["tg"][0:TT, 2 + layer:3 + layer]
            for c in range(NCH):
                dve.wait_ge(s_acc, (c + 1) * NX)
                k = slice(CH * c, CH * c + CH)
                nc.vector.scalar_tensor_tensor(X[:, k, :], total[:, k, :], g, X[:, k, :], ALU.mult, ALU.add)

        @block.gpsimd
        def _(pool):
            nc.gpsimd.memset(total[:, :, :], 0.0).then_inc(s_zero, 1)
            pool.wait_ge(s_zero, 1)

            def chunk(c):
                for e in range(NX):
                    number = c * NX + e
                    pool.wait_ge(s_tmp, number + 1)
                    at_least(pool, s_acc, number)
                    apart(pool)
                    k = total[:, bass.ds(c * CH, CH), :]
                    nc.gpsimd.tensor_tensor(k, k, tmp[e % DB][:, :, :], ALU.add).then_inc(s_acc, 1)
            steps(pool, chunk)


def kernel(**inputs):
    import concourse.bacc as bacc
    from concourse.bass_utils import run_bass_kernel_spmd

    x = {k: np.ascontiguousarray(v) for k, v in inputs.items()}
    arrays = {
        "x": x["x"].reshape(TOKENS, D), "ctx": x["ctx_1024"], "mask": x["mask_BxSxS2_bk1"].reshape(TOKENS, SK),
        "g_xattn": x["g_xattn"], "g_ffn": x["g_ffn"],
        "WqT0": x["L0_xattn_Wq"].T, "WkT0": x["L0_xattn_Wk"].T, "WvT0": x["L0_xattn_Wv"].T, "WpT0": x["L0_xattn_Wp"].T,
        "WqT1": x["L1_xattn_Wq"].T, "WkT1": x["L1_xattn_Wk"].T, "WvT1": x["L1_xattn_Wv"].T, "WpT1": x["L1_xattn_Wo"].T,
        "bp0": x["L0_xattn_bp"], "bp1": x["L1_xattn_bo"], "bq1": x["L1_xattn_bq"], "bk1": x["L1_xattn_bk"], "bv1": x["L1_xattn_bv"],
        "subln": x["L0_xattn_subln_w"], "lq1": x["L0_xattn_lq1"], "lk1": x["L0_xattn_lk1"], "lq2": x["L0_xattn_lq2"],
        "lk2": x["L0_xattn_lk2"], "routerT0": x["L0_ffn_router_w"].T, "router_b": x["L0_ffn_router_b"],
        "routerT1": x["L1_ffn_gate_w"].T,
        "wup0": np.concatenate([x["L0_ffn_w_up"], x["L0_ffn_shared_w_up"]]).transpose(2, 0, 1),
        "wdn0": np.concatenate([x["L0_ffn_w_down"], x["L0_ffn_shared_w_down"]]).reshape(NE + 1, D, FF // 128, 128).transpose(3, 0, 2, 1),
        "wup1": x["L1_ffn_w12"].transpose(2, 0, 1),
        "wdn1": x["L1_ffn_w3"].reshape(NE, D, FF // 128, 128).transpose(3, 0, 2, 1),
        "ident": np.eye(128, dtype=np.float32),
        "headsel0": (np.arange(D)[:, None] // L0.hd % L0.group_heads == np.arange(L0.group_heads)).astype(np.float32),
        "headsel1": (np.arange(D)[:, None] // L1.hd % L1.group_heads == np.arange(L1.group_heads)).astype(np.float32),
        "ones_rows": np.repeat(np.array([[BIG], [1.0]], np.float16), SK, axis=1),
        "big_ident": np.tile(np.eye(SQ) * BIG, L1.group_heads).astype(np.float16),
        "desc": np.arange(NE, 0, -1).astype(np.float32),
    }
    nc = bacc.Bacc("TRN2", target_bir_lowering=False, num_devices=1)
    feeds, aps = {}, {}
    for name, array in arrays.items():
        array = np.ascontiguousarray(array)
        feeds[f"in_{name}"] = array
        aps[name] = nc.dram_tensor(f"in_{name}", array.shape, mybir.dt.from_np(array.dtype), kind="ExternalInput").ap()
    out = nc.dram_tensor("result", (TOKENS, D), F32, kind="ExternalOutput").ap()
    build(nc, aps, out)
    got = run_bass_kernel_spmd(nc, [feeds], core_ids=[0])
    return got.results[0]["result"].reshape(B, SQ, D)
```

```python
import math
from contextlib import ExitStack

import numpy as np
import concourse.bass as bass
from concourse import mybir

F32 = mybir.dt.float32
F16 = mybir.dt.float16
U8 = mybir.dt.uint8
ALU = mybir.AluOpType
ACT = mybir.ActivationFunctionType
AX = mybir.AxisListType

B, SQ, D, SK = 32, 56, 128, 1500
TOKENS = B * SQ
TT = 2 * SQ
NTT = TOKENS // TT
CH = 4
NCH = NTT // CH
CW = CH * TT
VH, VD = 16, 8
KT = 125
NKT = SK // KT
THIRD = 4
NTHIRD = NKT // THIRD
TK = THIRD * KT
NE = 8
FF = 256
EPS = 1e-5
LAMBDA_INIT = 0.8 - 0.6 * math.exp(-0.3 * 4)

QK_UP = 64.0
EXP_SCALE = 1.0 / (QK_UP * QK_UP)
BIG = 32768.0
SLOTS = 3


class Layer:

    def __init__(self, name, heads, hd, group_dims, masked):
        self.name = name
        self.heads, self.hd = heads, hd
        self.group_dims = group_dims
        self.groups = D // group_dims
        self.group_heads = group_dims // hd
        self.group_cols = self.group_heads * SQ
        self.masked = masked
        self.mask_rows = SQ if masked else 0
        self.score_rows = 3 * group_dims + self.mask_rows
        self.rows = self.score_rows + 2
        self.cols = heads * SQ
        self.halves = self.cols // 896
        self.half_groups = self.groups // self.halves
        self.pair_tiles = self.cols // TT
        self.pieces = self.pair_tiles * NTHIRD
        self.o_cols = self.cols // 4
        self.uses_f = 2


L0 = Layer("L0", 32, 4, 32, False)
L1 = Layer("L1", 16, 8, 16, True)


def at_least(eng, sem, value):
    if isinstance(value, int) and value <= 0:
        return
    eng.wait_ge(sem, value)


def build(nc, a, out):
    ctx = ExitStack()
    with ctx:
        def sb(name, shape, dt=F32):
            return ctx.enter_context(nc.sbuf_tensor(name, shape, dt))

        def sem(name):
            return ctx.enter_context(nc.semaphore(name))

        score_ps = [ctx.enter_context(nc.psum_tensor(f"score_ps{i}", [128, 2, 512], F32)) for i in range(2)]
        max_ps = [ctx.enter_context(nc.psum_tensor(f"max_ps{i}", [128, 512], F32)) for i in range(2)]
        acc_ps = ctx.enter_context(nc.psum_tensor("acc_ps", [128, 512], F32))
        spare_ps = ctx.enter_context(nc.psum_tensor("spare_ps", [128, 512], F32))
        bank = [score_ps[0][:, 0, :], score_ps[0][:, 1, :], score_ps[1][:, 0, :], score_ps[1][:, 1, :],
                max_ps[0][:, :], max_ps[1][:, :], acc_ps[:, :], spare_ps[:, :]]

        X = sb("X", [TT, NTT, D])
        XnT = sb("XnT", [128, TOKENS])
        attnT = sb("attnT", [128, TOKENS])
        ident = sb("ident", [128, 128])
        neg_half = sb("neg_half", [128, 64])
        tg = sb("tg", [128, 4])
        lam = sb("lam", [SQ, 16])
        keep = sb("keep", [TT, NTT])
        small = {n: sb(n, s) for n, s in (
            ("WqT0", [128, D]), ("WkT0", [128, D]), ("WvT0", [128, D]), ("WpT0", [128, D]),
            ("WqT1", [128, D]), ("WkT1", [128, D]), ("WvT1", [128, D]), ("WpT1", [128, D]),
            ("bp0", [TT, D]), ("bp1", [TT, D]), ("bq1", [TT, D]), ("bv1", [SQ, D]), ("bk1", [128, 1]),
            ("subln", [128, 1]), ("headsel0", [3 * L0.group_dims, L0.group_heads]), ("headsel1", [3 * L1.group_dims, L1.group_heads]),
            ("routerT0", [128, NE]), ("routerT1", [128, NE]), ("router_b", [TT, NE]), ("desc", [TT, NE]))}

        ks_words = L1.groups * SK
        kstack = [sb(f"kstack{i}", [128, ks_words], F16) for i in range(SLOTS)]
        qstack = [sb(f"qstack{i}", [128, L0.cols], F16) for i in range(SLOTS)]
        vext = [sb(f"vext{i}", [KT, NKT, VH // 2, 32]) for i in range(SLOTS)]
        probs = [sb(f"probs{i}", [KT, 2 * 896]) for i in range(2)]
        ctx_in = sb("ctx_in", [KT, NKT, D])
        ctxT = sb("ctxT", [128, SK])
        khl = sb("khl", [128, 2, SK], F16)
        qh = sb("qh", [128, TOKENS], F16)
        ql = sb("ql", [128, TOKENS], F16)
        qrows = sb("qrows", [128, L1.groups, SQ], F16)
        mask_in = sb("mask_in", [SQ, SK], U8)
        mask_big = sb("mask_big", [SQ, SK], F16)
        out_sb = sb("out_sb", [128, L0.o_cols])
        max_part = sb("max_part", [TT, 16, NTHIRD])
        neg_max = sb("neg_max", [TT, 16])
        max_rows = sb("max_rows", [16, 2, TT], F16)
        turned = sb("turned", [SQ, 2, 512])
        rden = sb("rden", [SQ, 2, 4, 4])
        heads_out = sb("heads_out", [SQ, 2, VH, VD])
        attn = sb("attn", [SQ, VH, VD])
        attn_sq = sb("attn_sq", [SQ, VH, VD])
        rms = sb("rms", [SQ, 2, VH])
        attn_n = sb("attn_n", [SQ, VH, VD])

        s_in = sem("inputs_loaded")
        s_set = sem("vector_setup")
        s_tanh = sem("tanh_done")
        loads = [(ident[:, :], a["ident"]), (X[:, :, :], a["x"].rearrange("(t p) d -> p t d", p=TT)),
                 (tg[:, 0:2], a["g_xattn"].partition_broadcast(128)),
                 (tg[:, 2:4], a["g_ffn"].partition_broadcast(128)),
                 (small["bp0"][:, :], a["bp0"].partition_broadcast(TT)),
                 (small["bp1"][:, :], a["bp1"].partition_broadcast(TT)),
                 (small["bq1"][:, :], a["bq1"].partition_broadcast(TT)),
                 (small["bv1"][:, :], a["bv1"].partition_broadcast(SQ)),
                 (small["bk1"][:, :], a["bk1"].rearrange("(p o) -> p o", o=1)),
                 (small["router_b"][:, :], a["router_b"].partition_broadcast(TT)),
                 (small["desc"][:, :], a["desc"].partition_broadcast(TT)),
                 (small["headsel0"][:, :], a["headsel0"]), (small["headsel1"][:, :], a["headsel1"]),
                 (small["routerT0"][:, :], a["routerT0"]), (small["routerT1"][:, :], a["routerT1"])]
        loads += [(lam[:, 4 * i:4 * i + 4], a[n].partition_broadcast(SQ)) for i, n in enumerate(("lq1", "lk1", "lq2", "lk2"))]
        loads += [(small[f"W{w}T{i}"][:, :], a[f"W{w}T{i}"]) for i in range(2) for w in "qkvp"]
        loads += [(small["subln"][VD * h:VD * h + VD, :], a["subln"].rearrange("(p o) -> p o", o=1)) for h in range(VH)]

        lam_s = sb("lam_s", [SQ, 8])
        lam_t = sb("lam_t", [SQ, 8])

        with nc.Block() as block:
            @block.sync
            def _(sp):
                for dst, src in loads:
                    sp.dma_start(dst, src).then_inc(s_in, 16)

            @block.gpsimd
            def _(pool):
                for i in range(SLOTS):
                    nc.gpsimd.memset(vext[i][:, :, :, :], 0.0).then_inc(s_set, 1)
                pool.wait_ge(s_set, SLOTS)
                for i in range(SLOTS):
                    for h in range(2):
                        nc.gpsimd.memset(vext[i][:, :, :, 16 * h + VD:16 * h + VD + 1], 1.0)
                nc.gpsimd.memset(neg_half[:, :], -0.5)

            @block.vector
            def _(dve):
                link = chain(dve, sem("setup_chain"))
                dve.wait_ge(s_in, 16 * len(loads))
                link(nc.vector.tensor_tensor(lam_t[:, 0:4], lam[:, 0:4], lam[:, 4:8], ALU.mult))
                link(nc.vector.tensor_tensor(lam_t[:, 4:8], lam[:, 8:12], lam[:, 12:16], ALU.mult))
                nc.vector.reduce_sum(lam_s[:, 0:2], lam_t[:, :].rearrange("p (a b) -> p a b", a=2), AX.X).then_inc(s_tanh, 1)
                dve.wait_ge(s_tanh, 3)
                link(nc.vector.tensor_tensor(lam_s[:, 4:5], lam_s[:, 3:4], lam_s[:, 2:3], ALU.subtract))
                link(nc.vector.tensor_scalar(lam_s[:, 5:6], lam_s[:, 4:5], -LAMBDA_INIT, None, ALU.add))
                link(nc.vector.tensor_scalar(small["WpT0"][:, :], small["WpT0"][:, :], small["subln"][:, :],
                                             1.0 - LAMBDA_INIT, ALU.mult, ALU.mult))
                for i in range(2):
                    link(nc.vector.tensor_scalar(small[f"WpT{i}"][:, :], small[f"WpT{i}"][:, :], tg[:, i:i + 1], None, ALU.mult))
                    link(nc.vector.tensor_scalar(small[f"bp{i}"][:, :], small[f"bp{i}"][:, :], tg[0:TT, i:i + 1], None, ALU.mult))
                    link(nc.vector.tensor_scalar(small[f"WkT{i}"][:, :], small[f"WkT{i}"][:, :], QK_UP, None, ALU.mult))
                link(nc.vector.tensor_scalar(small["bk1"][:, :], small["bk1"][:, :], QK_UP, None, ALU.mult))

            @block.scalar
            def _(act):
                act.wait_ge(s_tanh, 1)
                nc.scalar.activation(lam_s[:, 2:4], lam_s[:, 0:2], ACT.Exp).then_inc(s_tanh, 1)
                nc.scalar.activation(tg[:, :], tg[:, :], ACT.Tanh).then_inc(s_tanh, 1)

        q_dram = nc.dram_tensor("q_parts", (2, D, TOKENS), F16).ap()
        k_dram = nc.dram_tensor("k_parts", (2, D, SK), F16).ap()
        T = dict(nc=nc, a=a, q_dram=q_dram, k_dram=k_dram, sem=sem, bank=bank, score_ps=score_ps, max_ps=max_ps, acc_ps=acc_ps, spare_ps=spare_ps,
                 X=X, XnT=XnT, attnT=attnT, ident=ident, neg_half=neg_half, tg=tg, small=small, kstack=kstack,
                 qstack=qstack, vext=vext, probs=probs, ctx_in=ctx_in, ctxT=ctxT, khl=khl, qh=qh, ql=ql,
                 qrows=qrows, mask_in=mask_in, mask_big=mask_big, out_sb=out_sb, max_part=max_part,
                 neg_max=neg_max, max_rows=max_rows, turned=turned, rden=rden, heads_out=heads_out, attn=attn, attn_sq=attn_sq,
                 rms=rms, attn_n=attn_n, neg_lam=lam_s[:, 5:6], keep=keep, sb=sb, ctx=ctx)
        normalise(T, "norm0", 0)
        attend(T, L0)
        project(T, 0)
        normalise(T, "norm0f", None)
        feed_forward(T, 0)
        normalise(T, "norm1", 1)
        attend(T, L1)
        project(T, 1)
        normalise(T, "norm1f", None)
        feed_forward(T, 1)

        s_out = sem("result_stored")
        with nc.Block() as block:
            @block.sync
            def _(sp):
                sp.dma_start(out.rearrange("(t p) d -> p t d", p=TT), X[:, :, :]).then_inc(s_out, 16)
                sp.wait_ge(s_out, 16)


def apart(eng):
    eng.nop(nofuse=True)


def chain(eng, s):
    count = [0]

    def link(instruction):
        count[0] += 1
        instruction.then_inc(s, 1)
        eng.wait_ge(s, count[0])
    return link


def carve(words, start, shape):
    n = int(np.prod(shape))
    flat = words[:, 2 * start:2 * (start + n)].bitcast(F32)
    if len(shape) == 1:
        return flat
    if len(shape) == 2:
        return flat.rearrange("p (a b) -> p a b", a=shape[0])
    return flat.rearrange("p (a b c) -> p a b c", a=shape[0], b=shape[1])


def normalise(T, tag, layer):
    nc, a, sem, bank = T["nc"], T["a"], T["sem"], T["bank"]
    X, XnT, ident, small = T["X"], T["XnT"], T["ident"], T["small"]
    xn = carve(T["kstack"][1][0:TT, :], 0, [NTT, D])
    xsq = carve(T["kstack"][2][0:TT, :], 0, [CH, D])
    st = carve(T["kstack"][2][0:TT, :], CH * D, [6, NTT])
    keep = T["keep"]
    s_var = sem(tag + "_variance_ready")
    s_rstd = sem(tag + "_rstd_ready")
    s_xn = sem(tag + "_normalised")
    s_xt = sem(tag + "_transposed")
    s_xnt = sem(tag + "_xnt_ready")
    s_qn = sem(tag + "_queries_projected")
    s_qs = sem(tag + "_queries_scaled")
    s_qt = sem(tag + "_queries_transposed")
    s_qh = sem(tag + "_query_high_ready")
    s_mask = sem(tag + "_mask_loaded")
    s_ql = sem(tag + "_query_low_ready")
    s_qd = sem(tag + "_queries_stored")
    head_scale = QK_UP * (L0.hd, L1.hd)[layer or 0] ** -0.5
    mask_row = T["kstack"][0][0:TT, :].bitcast(U8)
    MT = 4

    with nc.Block() as block:
        if layer is not None:
            @block.sync
            def _(sp):
                if layer == 1:
                    src = a["mask"].rearrange("(t p) k -> p t k", p=TT)
                    for c in range(NTT // MT):
                        sp.dma_start(mask_row[:, c * MT * SK:(c + 1) * MT * SK].rearrange("p (t k) -> p t k", t=MT),
                                     src[:, MT * c:MT * c + MT, :]).then_inc(s_mask, 16)
                sp.wait_ge(s_qh, NCH)
                sp.dma_start(T["q_dram"][0, :, :], T["qh"][:, :]).then_inc(s_qd, 16)
                sp.wait_ge(s_ql, NCH)
                sp.dma_start(T["q_dram"][1, :, :], T["ql"][:, :]).then_inc(s_qd, 16)
                sp.wait_ge(s_qd, 32)

        @block.vector
        def _(dve):
            link = chain(dve, sem(tag + "_chain"))

            def wide(v):
                return v.unsqueeze(2).to_broadcast([TT, CH, D])

            def first(c):
                x = X[:, CH * c:CH * c + CH, :]
                s = [st[:, k, CH * c:CH * c + CH] for k in range(6)]
                link(nc.vector.reduce_sum(s[0], x, AX.X))
                link(nc.vector.tensor_scalar(s[1], s[0], 1.0 / D, None, ALU.mult))
                link(nc.vector.tensor_tensor(xn[:, CH * c:CH * c + CH, :], x, wide(s[1]), ALU.subtract))
                xm = xn[:, CH * c:CH * c + CH, :]
                link(nc.vector.tensor_tensor(xsq[:, :, :], xm, xm, ALU.mult))
                link(nc.vector.reduce_sum(s[2], xsq[:, :, :], AX.X))
                nc.vector.tensor_scalar(s[3], s[2], 1.0 / D, EPS, ALU.mult, ALU.add).then_inc(s_var, 1)

            def second(c):
                dve.wait_ge(s_rstd, c + 1)
                xm = xn[:, CH * c:CH * c + CH, :]
                nc.vector.tensor_tensor(xm, xm, wide(st[:, 4, CH * c:CH * c + CH]), ALU.mult).then_inc(s_xn, 1)

            for c in range(NCH):
                first(c)
                if c:
                    second(c - 1)
            second(NCH - 1)
            if layer is None:
                return
            if layer == 1:
                dve.wait_ge(s_mask, 16 * (NTT // MT))
                link(nc.vector.tensor_reduce(keep[:, :], mask_row[:, 0:NTT * SK].rearrange("p (t k) -> p t k", t=NTT),
                                             AX.X, ALU.min))
                link(nc.vector.tensor_scalar(keep[:, :], keep[:, :], -head_scale, head_scale, ALU.mult, ALU.add))
                for c in range(NCH):
                    dve.wait_ge(s_qn, c + 1)
                    dst = xn[:, CH * c:CH * c + CH, :]
                    ps = bank[4 + c][0:TT, :].rearrange("p (t d) -> p t d", t=CH)
                    bq = small["bq1"][:, :].unsqueeze(1).to_broadcast([TT, CH, D])
                    link(nc.vector.tensor_tensor(dst, ps, bq, ALU.add))
                    nc.vector.tensor_tensor(dst, dst, wide(keep[:, CH * c:CH * c + CH]), ALU.mult).then_inc(s_qs, 1)
            for c in range(NCH):
                dve.wait_ge(s_qh, c + 1)
                nc.vector.tensor_tensor(T["ql"][:, CW * c:CW * c + CW], bank[c][:, 0:CW],
                                        T["qh"][:, CW * c:CW * c + CW], ALU.subtract).then_inc(s_ql, 1)

        @block.gpsimd
        def _(pool):
            for c in range(NCH):
                pool.wait_ge(s_var, c + 1)
                nc.gpsimd.tensor_tensor(st[:, 4, CH * c:CH * c + CH], st[:, 3, CH * c:CH * c + CH],
                                        T["neg_half"][0:TT, 0:CH], ALU.pow).then_inc(s_rstd, 1)

        @block.tensor
        def _(pe):
            for c in range(NCH):
                pe.wait_ge(s_xn, c + 1)
                for t in range(CH):
                    last = nc.tensor.transpose(bank[c][:, TT * t:TT * t + TT], xn[:, CH * c + t, :], ident[0:TT, 0:TT])
                last.then_inc(s_xt, 1)
            if layer is None:
                return
            for c in range(NCH):
                pe.wait_ge(s_xnt, c + 1)
                for t in range(CH):
                    last = nc.tensor.matmul(bank[4 + c][0:TT, D * t:D * t + D],
                                            XnT[:, CW * c + TT * t:CW * c + TT * t + TT],
                                            small[f"WqT{layer}"][:, :], start=True, stop=True)
                last.then_inc(s_qn, 1)
            for c in range(NCH):
                pe.wait_ge(s_qs, c + 1)
                for t in range(CH):
                    last = nc.tensor.transpose(bank[c][:, TT * t:TT * t + TT], xn[:, CH * c + t, :], ident[0:TT, 0:TT])
                last.then_inc(s_qt, 1)

        @block.scalar
        def _(act):
            for c in range(NCH):
                act.wait_ge(s_xt, c + 1)
                nc.scalar.activation(XnT[:, CW * c:CW * c + CW], bank[c][:, 0:CW], ACT.Copy).then_inc(s_xnt, 1)
            if layer is None:
                return
            if layer == 0:
                for c in range(NCH):
                    act.wait_ge(s_qn, c + 1)
                    nc.scalar.activation(xn[:, CH * c:CH * c + CH, :].rearrange("p t d -> p (t d)"), bank[4 + c][0:TT, :],
                                         ACT.Copy, scale=head_scale).then_inc(s_qs, 1)
            for c in range(NCH):
                act.wait_ge(s_qt, c + 1)
                nc.scalar.activation(T["qh"][:, CW * c:CW * c + CW], bank[c][:, 0:CW], ACT.Copy).then_inc(s_qh, 1)


def attend(T, L):
    nc, a, sem, ident, small = T["nc"], T["a"], T["sem"], T["ident"], T["small"]
    score_ps, max_ps, acc_ps, spare_ps = T["score_ps"], T["max_ps"], T["acc_ps"], T["spare_ps"]
    probs, ctx_in, ctxT, khl, vext = T["probs"], T["ctx_in"], T["ctxT"], T["khl"], T["vext"]
    qrows, mask_in, mask_big, out_sb = T["qrows"], T["mask_in"], T["mask_big"], T["out_sb"]
    max_part, neg_max, max_rows = T["max_part"], T["neg_max"], T["max_rows"]
    turned, rden, heads_out, attn, attn_sq, rms, attn_n = (T[k] for k in ("turned", "rden", "heads_out", "attn", "attn_sq", "rms", "attn_n"))
    layer = 0 if L is L0 else 1
    GD, NG, GC, H = L.group_dims, L.groups, L.group_cols, L.halves
    kstack = [T["kstack"][i][:, 0:NG * SK].rearrange("p (g k) -> p g k", g=NG) for i in range(SLOTS)]
    qstack = [T["qstack"][i][:, 0:L.cols].rearrange("p (g c) -> p g c", g=NG) for i in range(SLOTS)]
    Wk, Wv = small[f"WkT{layer}"], small[f"WvT{layer}"]
    R = L.rows
    S = L.heads // VH

    s_const = sem(L.name + "_constant_rows")
    s_ctx = sem(L.name + "_context_loaded")
    s_mask = sem(L.name + "_mask_loaded")
    s_big = sem(L.name + "_mask_scaled")
    s_ks = [sem(f"{L.name}_kstack_filled{i}") for i in range(SLOTS)]
    s_qr = sem(L.name + "_query_rows_loaded")
    s_kd = sem(L.name + "_keys_stored")
    s_mrow = [sem(f"{L.name}_maximum_rows_filled{i}") for i in range(SLOTS)]
    s_ctxT = sem(L.name + "_ctxT_ready")
    s_kh = sem(L.name + "_key_high_ready")
    s_kl = sem(L.name + "_key_low_ready")
    s_v = sem(L.name + "_values_ready")
    s_qs = sem(L.name + "_qstack_ready")
    s_ready = sem(L.name + "_spare_filled")
    s_turned = sem(L.name + "_turned_output_ready")
    s_rden = sem(L.name + "_reciprocals_ready")
    s_at = sem(L.name + "_attnT_ready")
    s_scores = sem(L.name + "_scores_ready")
    s_exp = sem(L.name + "_probs_ready")
    s_av = sem(L.name + "_weighted_values_done")
    s_piece = sem(L.name + "_max_scores_ready")
    s_red = sem(L.name + "_max_reduced")
    s_neg = sem(L.name + "_negative_max_ready")
    s_mr = sem(L.name + "_max_split")
    s_os = sem(L.name + "_output_copied")
    s_attn = sem(L.name + "_attention_normalised")
    CONST = 16 * SLOTS * NG * (2 if L.masked else 1)

    K_INC = 16 * (3 * NTHIRD + 1 if L.masked else 3 * NG)
    Q_INC = 16 * 3
    M_INC = 32
    LAST = NKT - 1

    prep = [("T", 0), ("K", 0), ("T", 1), ("K", 1), ("T", 2), ("K", 2), ("V", 0), ("V", 1), ("V", 2)]
    if L is L0:
        where = {("T", 0): (0, 0), ("K", 0): (1, 0), ("F", 0): (1, 1), ("T", 1): (2, 0), ("F", 1): (2, 1), ("K", 1): (3, 0),
                 ("T", 2): (4, 0), ("K", 2): (5, 0), ("V", 0): (6, 0), ("V", 1): (7, 0), ("V", 2): (8, 0), ("A", 0): (9, 0),
                 ("M", 0): (9, 1)}
    else:
        where = {("T", 0): (0, 0), ("K", 0): (0, 1), ("T", 1): (1, 1), ("K", 1): (2, 0), ("T", 2): (3, 0), ("K", 2): (3, 1),
                 ("F", 0): (4, 1), ("F", 1): (5, 0), ("V", 0): (6, 0), ("V", 1): (6, 1), ("V", 2): (7, 1), ("A", 0): (8, 1),
                 ("M", 0): (9, 1)}
    per_step = L.pieces // NKT
    AHEAD = 3
    early = AHEAD * per_step
    turnaround = [("F", i) for i in range(L.uses_f)] + [("A", 0)]

    def spare_uses(has_f, has_m, has_p):
        uses = (prep if has_p else []) + (turnaround if has_f else []) + ([("M", 0)] if has_m else [])
        return sorted(uses, key=lambda u: where[u])

    FULL = len(spare_uses(True, True, True))
    PROLOGUE = 2 * len(prep) + 1
    FIRST = PROLOGUE + len(prep) + 1

    LOOPS = (B - 5) // SLOTS

    class At:

        def __init__(self, j, c):
            self.j, self.c = j, c
            self.n = j * SLOTS + c
            self.slot = c % SLOTS
            self.turn = j + c // SLOTS

        def plus(self, d):
            return At(self.j, self.c + d)

    def iterations(eng, body, prologue=None, epilogue=None):
        if prologue:
            prologue()
        body(At(0, 0), PROLOGUE, spare_uses(False, True, True), False, True, True)
        with eng.Fori(0, LOOPS) as j:
            for c in range(1, 1 + SLOTS):
                at = At(j, c)
                body(at, (at.n - 1) * FULL + FIRST, spare_uses(True, True, True), True, True, True)
        before = FIRST + SLOTS * LOOPS * FULL
        for n in range(SLOTS * LOOPS + 1, B):
            has_m, has_p = n + 1 < B, n + 2 < B
            uses = spare_uses(True, has_m, has_p)
            body(At(0, n), before, uses, True, has_m, has_p)
            before += len(uses)
        if epilogue:
            epilogue(before)

    def copied_out(at, kind, i):
        p = at.plus(2)
        return {"T": (s_ctxT, NTHIRD * p.n + i + 1), "K": (s_kl, NTHIRD * p.n + i + 1),
                "V": (s_v, NTHIRD * p.n + i + 1), "M": (s_mr, at.n + 2),
                "F": (s_turned, (at.n - 1) * L.uses_f + i + 1), "A": (s_at, at.n)}[kind]

    def at_step(uses, base, t, side):
        return [(kind, i, base + k) for k, (kind, i) in enumerate(uses) if where[kind, i] == (t, side)]

    def searched(at, t, k):
        if k >= per_step:
            return []
        d, p = (1, early + t * per_step + k) if t < NKT - AHEAD else (2, (t - NKT + AHEAD) * per_step + k)
        return [] if isinstance(at.n, int) and at.n + d >= B else [(at.plus(d), p)]

    with nc.Block() as block:
        @block.sync
        def _(sp):
            for i in range(SLOTS):
                for g in range(NG):
                    sp.dma_start(kstack[i][R - 2:R, g, :], a["ones_rows"]).then_inc(s_const, 16)
                if L.masked:
                    for g in range(NG):
                        sp.dma_start(qstack[i][3 * GD:3 * GD + SQ, g, :], a["big_ident"]).then_inc(s_const, 16)
            sp.wait_ge(s_const, CONST)

            def load(at):
                sp.dma_start(ctx_in[:, :, :],
                             a["ctx"][bass.ds(at.n, 1), :, :].rearrange("b (p t) d -> (b p) t d", t=NKT)).then_inc(s_ctx, 16)
                if L.masked:
                    at_least(sp, s_big, at.n)
                    sp.dma_start(mask_in[:, :], a["mask"][bass.ds(at.n * SQ, SQ), :]).then_inc(s_mask, 16)

            def load_q(at):
                at_least(sp, s_qs, at.n)
                apart(sp)
                for row, part in ((0, 0), (GD, 1), (2 * GD, 0)):
                    sp.dma_start(qrows[row:row + GD, 0:NG, :],
                                 T["q_dram"][part, :, bass.ds(at.n * SQ, SQ)].rearrange("(g r) q -> r g q", g=NG)).then_inc(s_qr, 16)

            def fill_k(at):
                sp.wait_ge(s_kl, NTHIRD * (at.n + 1))
                for g in range(NG):
                    for row, part in ((0, 0), (GD, 0), (2 * GD, 1)):
                        sp.dma_start(kstack[at.slot][row:row + GD, g, :],
                                     khl[GD * g:GD * g + GD, part, :]).then_inc(s_ks[at.slot], 16)

            def fill_mask(at):
                at_least(sp, s_scores, (at.n - 2) * NKT * H)
                apart(sp)
                sp.wait_ge(s_big, at.n + 1)
                sp.dma_start(kstack[at.slot][3 * GD:3 * GD + SQ, :, :],
                             mask_big[:, :].unsqueeze(1).to_broadcast([SQ, NG, SK])).then_inc(s_ks[at.slot], 16)

            def fill_k_third(at, i):
                sp.wait_ge(s_kl, NTHIRD * at.n + i + 1)
                apart(sp)
                k = slice(TK * i, TK * i + TK)
                sp.dma_start(T["k_dram"][:, :, k].rearrange("a p k -> p a k"), khl[:, :, k]).then_inc(s_kd, 16)
                sp.wait_ge(s_kd, 16 * (NTHIRD * at.n + i + 1))
                for row, part in ((0, 0), (GD, 0), (2 * GD, 1)):
                    sp.dma_start(kstack[at.slot][row:row + GD, :, k],
                                 T["k_dram"][part, :, k].rearrange("(g r) k -> r g k", g=NG)).then_inc(s_ks[at.slot], 16)

            def fill_m(at):
                sp.wait_ge(s_mr, at.n + 1)
                for part in range(2):
                    row = L.score_rows + part
                    sp.dma_start(T["qstack"][at.slot][row:row + 1, 0:L.cols],
                                 max_rows[0:L.pair_tiles, part, :]).then_inc(s_mrow[at.slot], 16)

            def fill(at, after):
                if L.masked:
                    fill_mask(at)
                    for i in range(NTHIRD - 1):
                        fill_k_third(at, i)
                sp.wait_ge(s_ctxT, NTHIRD * (at.n + 1))
                if after:
                    load(at.plus(1))
                if L.masked:
                    fill_k_third(at, NTHIRD - 1)
                else:
                    fill_k(at)
                if after:
                    load_q(at.plus(1))

            def prologue():
                load(At(0, 0))
                load_q(At(0, 0))
                for n in range(2):
                    fill(At(0, n), True)
                fill_m(At(0, 0))

            def body(at, base, uses, has_f, has_m, has_p):
                if has_p:
                    fill(at.plus(2), not (isinstance(at.n, int) and at.n + 3 >= B))
                if has_m:
                    fill_m(at.plus(1))

            iterations(sp, body, prologue)

        s_chain = sem(L.name + "_normalisation_chain")
        s_high = sem(L.name + "_max_high_ready")
        LINKS = 2 * S + (8 if L is L0 else 0)

        def turned_view(x, h):
            return turned[:, :, 0:256 * S].rearrange("q i (s a j e) -> q i s a j e", s=S, a=2, j=4)[:, :, x, h, :, :]

        @block.gpsimd
        def _(pool):
            sel = small[f"headsel{layer}"]

            def prepare(at):
                prev = at.plus(-1)
                if L.masked:
                    pool.wait_ge(s_mask, 16 * (at.n + 1))
                    if not (isinstance(at.n, int) and at.n == 0):
                        pool.wait_ge(s_ks[prev.slot], K_INC * (prev.turn + 1))
                    apart(pool)
                    nc.gpsimd.tensor_scalar(mask_big[:, :].rearrange("q (t p) -> q t p", t=NKT),
                                            mask_in[:, :].rearrange("q (p t) -> q t p", t=NKT),
                                            -BIG, None, ALU.mult).then_inc(s_big, 1)
                pool.wait_ge(s_qr, Q_INC * (at.n + 1))
                at_least(pool, s_scores, (at.n - 2) * NKT * H)
                nc.gpsimd.tensor_tensor(
                    qstack[at.slot][0:3 * GD, :, :].rearrange("r g (h q) -> r g h q", q=SQ),
                    qrows[0:3 * GD, 0:NG, :].unsqueeze(2).to_broadcast([3 * GD, NG, L.group_heads, SQ]),
                    sel[:, :].unsqueeze(1).unsqueeze(3).to_broadcast([3 * GD, NG, L.group_heads, SQ]), ALU.mult).then_inc(s_qs, 1)

            def finish(n):
                count = [0]

                def link(instruction):
                    count[0] += 1
                    instruction.then_inc(s_chain, 1)
                    pool.wait_ge(s_chain, (n - 1) * LINKS + count[0])

                pool.wait_ge(s_rden, n * 2)
                for h in range(2):
                    for x in range(S):
                        ins = nc.gpsimd.tensor_tensor(
                            heads_out[:, x, :, :].rearrange("q (i j a) d -> q i j a d", i=2, a=2)[:, :, :, h, :],
                            turned_view(x, h)[:, :, :, 16 * h:16 * h + VD],
                            rden[:, h, 0:2 * S, :].rearrange("q (i s) j -> q i s j", i=2)[:, :, x, :].unsqueeze(3).to_broadcast([SQ, 2, 4, VD]),
                            ALU.mult)
                        link(ins)
                if L is L0:
                    apart(pool)
                    link(nc.gpsimd.tensor_scalar(attn[:, :, :], heads_out[:, 1, :, :], T["neg_lam"], None, ALU.mult))
                    link(nc.gpsimd.tensor_tensor(attn[:, :, :], attn[:, :, :], heads_out[:, 0, :, :], ALU.add))
                    link(nc.gpsimd.tensor_tensor(attn_sq[:, :, :], attn[:, :, :], attn[:, :, :], ALU.mult))
                    for w in (4, 2, 1):
                        link(nc.gpsimd.tensor_tensor(attn_sq[:, :, 0:w], attn_sq[:, :, 0:w], attn_sq[:, :, w:2 * w], ALU.add))
                    apart(pool)
                    link(nc.gpsimd.tensor_scalar(rms[:, 0, :], attn_sq[:, :, 0], 1.0 / VD, EPS, ALU.mult, ALU.add))
                    link(nc.gpsimd.tensor_tensor(rms[:, 1, :], rms[:, 0, :], T["neg_half"][0:SQ, 0:VH], ALU.pow))
                    nc.gpsimd.tensor_tensor(attn_n[:, :, :], attn[:, :, :], rms[:, 1, :].unsqueeze(2).to_broadcast([SQ, VH, VD]),
                                            ALU.mult).then_inc(s_attn, 1)
                else:
                    nc.gpsimd.tensor_tensor(attn_n[:, :, :].rearrange("q h d -> q (h d)"),
                                            heads_out[:, 0, :, :].rearrange("q h d -> q (h d)"),
                                            small["bv1"][:, :], ALU.add).then_inc(s_attn, 1)

            def body(at, base, uses, has_f, has_m, has_p):
                if has_p:
                    prepare(at.plus(2))
                if has_f:
                    finish(at.n)

            iterations(pool, body, lambda: (prepare(At(0, 0)), prepare(At(0, 1))), lambda before: finish(B))

        @block.tensor
        def _(pe):
            pe.wait_ge(s_const, CONST)

            def use(at, kind, i, before):
                if before:
                    pe.wait_ge(*copied_out(*before))
                p = at.plus(2)
                if kind == "T":
                    if i == 0:
                        pe.wait_ge(s_ctx, 16 * (p.n + 1))
                    for t in range(THIRD):
                        last = nc.tensor.transpose(spare_ps[:, KT * t:KT * t + KT], ctx_in[:, THIRD * i + t, :], ident[0:KT, 0:KT])
                    last.then_inc(s_ready, 1)
                if kind == "K":
                    pe.wait_ge(s_ctxT, NTHIRD * p.n + i + 1)
                    nc.tensor.matmul(spare_ps[:, 0:TK], Wk[:, :], ctxT[:, TK * i:TK * i + TK], start=True, stop=True).then_inc(s_ready, 1)
                if kind == "V":
                    for t in range(THIRD):
                        k = TK * i + KT * t
                        last = nc.tensor.matmul(spare_ps[0:KT, D * t:D * t + D], ctxT[:, k:k + KT], Wv[:, :], start=True, stop=True)
                    last.then_inc(s_ready, 1)
                if kind == "M":
                    pe.wait_ge(s_neg, at.n + 2)
                    nc.tensor.transpose(spare_ps[0:L.pair_tiles, 0:TT], neg_max[:, 0:L.pair_tiles], ident[0:TT, 0:TT]).then_inc(s_ready, 1)
                if kind == "F":
                    pe.wait_ge(s_os, at.n)
                    apart(pe)
                    for b in range(2 * S):
                        k = (i * 2 * S + b) * SQ
                        last = nc.tensor.transpose(spare_ps[0:SQ, 128 * b:128 * b + 128], out_sb[:, k:k + SQ], ident[:, :])
                    last.then_inc(s_ready, 1)
                if kind == "A":
                    pe.wait_ge(s_attn, at.n)
                    apart(pe)
                    nc.tensor.transpose(spare_ps[:, 0:SQ], attn_n[:, :, :].rearrange("q h d -> q (h d)"), ident[0:SQ, 0:SQ]).then_inc(s_ready, 1)

            def search(at, p):
                u, third = p // NTHIRD, p % NTHIRD
                g = u * TT // GC
                if p == 0:
                    pe.wait_ge(s_ks[at.slot], K_INC * (at.turn + 1))
                    pe.wait_ge(s_qs, at.n + 1)
                at_least(pe, s_red, at.n * L.pieces + p - 1)
                nc.tensor.matmul(max_ps[p % 2][0:TT, 0:TK], T["qstack"][at.slot][0:L.score_rows, TT * u:TT * u + TT],
                                 kstack[at.slot][0:L.score_rows, g, TK * third:TK * third + TK],
                                 start=True, stop=True).then_inc(s_piece, 1)

            def scores(at, t, h):
                number = (at.n * NKT + t) * H + h
                at_least(pe, s_exp, number - 1)
                if t == 0 and h == 0:
                    pe.wait_ge(s_mrow[at.slot], M_INC * (at.turn + 1))
                buf = score_ps[number_parity(t, h)]
                for k in range(L.half_groups):
                    g = h * L.half_groups + k
                    per_bank = L.half_groups // 2
                    o = (k % per_bank) * GC
                    last = nc.tensor.matmul(buf[0:KT, k // per_bank, o:o + GC], kstack[at.slot][0:R, g, KT * t:KT * t + KT],
                                            qstack[at.slot][0:R, g, :], start=True, stop=True)
                last.then_inc(s_scores, 1)

            def number_parity(t, h):
                return (t * H + h) % 2

            def weigh(at, t, i):
                if i == 0:
                    pe.wait_ge(s_exp, (at.n * NKT + t + 1) * H)
                    if t == 0:
                        at_least(pe, s_os, at.n)
                        pe.wait_ge(s_v, NTHIRD * (at.n + 1))
                for j in range(4):
                    u = 4 * i + j
                    moving = probs[t % 2][:, 0:S * 896].rearrange("k (s c) -> k s c", s=S)[:, :, TT * u:TT * u + TT]
                    last = nc.tensor.matmul(
                        acc_ps[32 * j:32 * j + 32, TT * S * i:TT * S * (i + 1)].rearrange("p (s c) -> p s c", s=S),
                        vext[at.slot][:, t, u, :], moving, start=(t == 0 and i == 0), stop=(t == LAST),
                        skip_group_check=True)
                if i == 1:
                    last.then_inc(s_av, 1)

            def prologue():
                before = None
                for n in range(2):
                    for kind, i in prep:
                        use(At(0, n - 2), kind, i, before)
                        before = (At(0, n - 2), kind, i)
                for p in range(L.pieces):
                    search(At(0, 0), p)
                use(At(0, -1), "M", 0, before)
                for p in range(early):
                    search(At(0, 1), p)

            def body(at, base, uses, has_f, has_m, has_p):
                before = (at.plus(-1), "M", 0)

                def step_uses(t, side):
                    nonlocal before
                    for kind, i, _ in at_step(uses, base, t, side):
                        use(at, kind, i, before)
                        before = (at, kind, i)

                def step_search(t, k):
                    for ahead, p in searched(at, t, k):
                        search(ahead, p)

                for t in range(NKT):
                    step_uses(t, 0)
                    for h in range(H):
                        scores(at, t, h)
                        step_search(t, h)
                    for i in range(2):
                        if t:
                            weigh(at, t - 1, i)
                        elif has_f:
                            weigh(at.plus(-1), LAST, i)
                        if i == 0:
                            step_uses(t, 1)
                        step_search(t, H + i)

            def epilogue(base):
                for i in range(2):
                    weigh(At(0, B - 1), LAST, i)
                before = (At(0, B - 1), "A", 0)
                for kind, i in turnaround:
                    use(At(0, B), kind, i, before)
                    before = (At(0, B), kind, i)

            iterations(pe, body, prologue, epilogue)

        @block.scalar
        def _(act):
            def drain(at, kind, i, number):
                p = at.plus(2)
                if kind == "M":
                    return
                act.wait_ge(s_ready, number + 1)
                if kind == "T":
                    nc.scalar.activation(ctxT[:, TK * i:TK * i + TK], spare_ps[:, 0:TK], ACT.Copy).then_inc(s_ctxT, 1)
                if kind == "K":
                    if i == 0 and not (isinstance(p.n, int) and p.n == 0):
                        prev = p.plus(-1)
                        act.wait_ge(s_ks[prev.slot], K_INC * (prev.turn + 1))
                    if L is L0:
                        nc.scalar.activation(khl[:, 0, TK * i:TK * i + TK], spare_ps[:, 0:TK], ACT.Copy).then_inc(s_kh, 1)
                    else:
                        nc.scalar.activation(khl[:, 0, TK * i:TK * i + TK], spare_ps[:, 0:TK], ACT.Identity,
                                             bias=small["bk1"][:, :]).then_inc(s_kh, 1)
                if kind == "V":
                    nc.scalar.activation(
                        vext[p.slot][:, THIRD * i:THIRD * i + THIRD, :, :].rearrange("k t u (a e) -> k t (u a) e", a=2)[:, :, :, 0:VD],
                        spare_ps[0:KT, :].rearrange("k (t h d) -> k t h d", t=THIRD, d=VD), ACT.Copy).then_inc(s_v, 1)
                if kind == "F":
                    if i == 0 and not (isinstance(at.n, int) and at.n == 1):
                        act.wait_ge(s_attn, at.n - 1)
                    nc.scalar.activation(turned[:, i, 0:256 * S], spare_ps[0:SQ, 0:256 * S], ACT.Copy).then_inc(s_turned, 1)
                if kind == "A":
                    nc.scalar.activation(T["attnT"][:, bass.ds((at.n - 1) * SQ, SQ)], spare_ps[:, 0:SQ], ACT.Copy).then_inc(s_at, 1)

            def exps(at, t, h):
                number = (at.n * NKT + t) * H + h
                act.wait_ge(s_scores, number + 1)
                if h == 0:
                    at_least(act, s_av, at.n * NKT + t - 1)
                nc.scalar.activation(probs[t % 2][:, 896 * h:896 * h + 896].rearrange("k (b c) -> k b c", b=2),
                                     score_ps[(t * H + h) % 2][0:KT, :, 0:448], ACT.Exp, scale=EXP_SCALE).then_inc(s_exp, 1)

            def copy_output(n):
                act.wait_ge(s_av, n * NKT)
                nc.scalar.activation(out_sb[:, 0:L.o_cols], acc_ps[:, 0:L.o_cols], ACT.Copy).then_inc(s_os, 1)

            def prologue():
                number = 0
                for n in range(2):
                    for kind, i in prep:
                        drain(At(0, n - 2), kind, i, number)
                        number += 1

            def body(at, base, uses, has_f, has_m, has_p):
                for t in range(NKT):
                    for kind, i, number in at_step(uses, base, t, 0):
                        drain(at, kind, i, number)
                    for h in range(H):
                        exps(at, t, h)
                    if t == 0 and has_f:
                        copy_output(at.n)
                    for kind, i, number in at_step(uses, base, t, 1):
                        drain(at, kind, i, number)

            def epilogue(before):
                copy_output(B)
                for k, (kind, i) in enumerate(turnaround):
                    drain(At(0, B), kind, i, before + k)

            iterations(act, body, prologue, epilogue)


        @block.vector
        def _(dve):
            def drain(at, kind, i, number):
                if kind in "TVAF":
                    return
                dve.wait_ge(s_ready, number + 1)
                if kind == "K":
                    p = at.plus(2)
                    dve.wait_ge(s_kh, NTHIRD * p.n + i + 1)
                    if L is L0:
                        nc.vector.tensor_tensor(khl[:, 1, TK * i:TK * i + TK], spare_ps[:, 0:TK],
                                                khl[:, 0, TK * i:TK * i + TK], ALU.subtract).then_inc(s_kl, 1)
                    else:
                        nc.vector.scalar_tensor_tensor(khl[:, 1, TK * i:TK * i + TK], spare_ps[:, 0:TK], small["bk1"][:, :],
                                                       khl[:, 0, TK * i:TK * i + TK], ALU.add, ALU.subtract).then_inc(s_kl, 1)
                if kind == "M":
                    m = at.plus(1)
                    high, low = max_rows[0:L.pair_tiles, 0, :], max_rows[0:L.pair_tiles, 1, :]
                    nc.vector.tensor_scalar(high, spare_ps[0:L.pair_tiles, 0:TT], 1.0 / BIG, None, ALU.mult).then_inc(s_high, 1)
                    dve.wait_ge(s_high, m.n + 1)
                    nc.vector.scalar_tensor_tensor(low, high, -BIG, spare_ps[0:L.pair_tiles, 0:TT],
                                                   ALU.mult, ALU.add).then_inc(s_mr, 1)

            def reciprocals(n):
                dve.wait_ge(s_turned, n * L.uses_f)
                for h in range(2):
                    t5 = turned[:, :, 0:256 * S].rearrange("q i (s a j e) -> q i s a j e", s=S, a=2, j=4)
                    nc.vector.reciprocal(rden[:, h, 0:2 * S, :].rearrange("q (i s) j -> q i s j", i=2),
                                         t5[:, :, :, h, :, 16 * h + VD]).then_inc(s_rden, 1)

            def reduce_piece(at, p):
                if p == 0:
                    at_least(dve, s_neg, at.n)
                dve.wait_ge(s_piece, at.n * L.pieces + p + 1)
                nc.vector.reduce_max(max_part[:, p // NTHIRD, p % NTHIRD:p % NTHIRD + 1], max_ps[p % 2][0:TT, 0:TK],
                                     AX.X).then_inc(s_red, 1)
                if p == L.pieces - 1:
                    dve.wait_ge(s_red, (at.n + 1) * L.pieces)
                    nc.vector.tensor_reduce(neg_max[:, 0:L.pair_tiles], max_part[:, 0:L.pair_tiles, :], AX.X, ALU.max,
                                            negate=True).then_inc(s_neg, 1)

            def prologue():
                number = 0
                for n in range(2):
                    for kind, i in prep:
                        drain(At(0, n - 2), kind, i, number)
                        number += 1
                for p in range(L.pieces):
                    reduce_piece(At(0, 0), p)
                drain(At(0, -1), "M", 0, number)
                for p in range(early):
                    reduce_piece(At(0, 1), p)

            def body(at, base, uses, has_f, has_m, has_p):
                for t in range(NKT):
                    for kind, i, number in at_step(uses, base, t, 0):
                        drain(at, kind, i, number)
                    for k in range(H + 2):
                        if k == H:
                            for kind, i, number in at_step(uses, base, t, 1):
                                drain(at, kind, i, number)
                            if t == where["F", 1][0] + 1 and has_f:
                                reciprocals(at.n)
                        for ahead, p in searched(at, t, k):
                            reduce_piece(ahead, p)

            iterations(dve, body, prologue, lambda before: reciprocals(B))


def project(T, layer):
    nc, sem, bank, X, small = T["nc"], T["sem"], T["bank"], T["X"], T["small"]
    s_ps = sem(f"p{layer}_projected")
    s_x = sem(f"p{layer}_bias_added")
    with nc.Block() as block:
        @block.tensor
        def _(pe):
            for c in range(NCH):
                for t in range(CH):
                    k = CW * c + TT * t
                    last = nc.tensor.matmul(bank[c][0:TT, D * t:D * t + D], T["attnT"][:, k:k + TT], small[f"WpT{layer}"][:, :],
                                            start=True, stop=True)
                last.then_inc(s_ps, 1)

        @block.vector
        def _(dve):
            for c in range(NCH):
                x = X[:, CH * c:CH * c + CH, :]
                nc.vector.tensor_tensor(x, x, small[f"bp{layer}"][:, :].unsqueeze(1).to_broadcast([TT, CH, D]), ALU.add).then_inc(s_x, 1)
            for c in range(NCH):
                x = X[:, CH * c:CH * c + CH, :]
                dve.wait_ge(s_x, c + 1)
                dve.wait_ge(s_ps, c + 1)
                nc.vector.tensor_tensor(x, bank[c][0:TT, :].rearrange("p (t d) -> p t d", t=CH), x, ALU.add)


def feed_forward(T, layer):
    nc, a, sem, bank, X, XnT, small = T["nc"], T["a"], T["sem"], T["bank"], T["X"], T["XnT"], T["small"]
    NX = NE + 1 if layer == 0 else NE
    UP = FF * (1 if layer == 0 else 2)
    NF = FF // 128
    gated = layer == 1
    UB = 2 if gated else 3
    DB = 2 if gated else 3
    HS = 4 if gated else 6
    assert NX * NF % UB == NX * NF % HS == NX % DB == 0
    n = f"f{layer}_"
    s_w = sem(n + "weights_loaded")
    s_lg = sem(n + "logits_ready")
    s_d = sem(n + "logit_difference_ready")
    s_e = sem(n + "second_weight_ready")
    s_up = sem(n + "hidden_projected")
    s_si = sem(n + "silu_done")
    s_hid = sem(n + "hidden_ready") if gated else s_si
    s_dn = sem(n + "expert_projected")
    s_tmp = sem(n + "weighted")
    s_acc = sem(n + "accumulated")
    s_zero = sem(n + "total_zeroed")
    k0, k1, k2 = (T["kstack"][i][:, :] for i in range(3))
    wup = carve(k0, 0, [NX, UP])
    wdn = carve(k1, 0, [NX, NF, D])
    total = carve(k2[0:TT, :], 0, [NTT, D])
    hidden = [carve(k2, NTT * D + CW * i, [CW]) for i in range(HS)]
    gate = [T["ctxT"][:, CW * i:CW * i + CW] for i in range(2)]
    tmp = [T["probs"][0][0:TT, CH * D * i:CH * D * i + CH * D].rearrange("p (t d) -> p t d", t=CH) for i in range(DB)]
    row = T["probs"][1][0:TT, :]
    lg, *r = [row[:, NTT * NE * i:NTT * NE * (i + 1)].rearrange("p (t e) -> p t e", e=NE) for i in range(5)]
    comb = row[:, 640:640 + NTT * (NE + 1)].rearrange("p (t e) -> p t e", e=NE + 1)
    m = row[:, 800:800 + 8 * NTT].rearrange("p (k t) -> p k t", k=8)

    with nc.Block() as block:
        @block.sync
        def _(sp):
            sp.dma_start(wup[:, :, :], a[f"wup{layer}"]).then_inc(s_w, 16)
            sp.dma_start(wdn[:, :, :, :], a[f"wdn{layer}"]).then_inc(s_w, 16)

        def before_hidden(c, u):
            return c * NX + (u - HS) // NF + 1

        def steps(eng, body):
            body(0)
            with eng.Fori(1, NCH) as c:
                body(c)

        @block.tensor
        def _(pe):
            for t in range(NTT):
                last = nc.tensor.matmul(bank[7][0:TT, NE * t:NE * t + NE], XnT[:, TT * t:TT * t + TT],
                                        small[f"routerT{layer}"][:, :], start=True, stop=True)
            last.then_inc(s_lg, 1)
            pe.wait_ge(s_w, 32)

            def up(c, e):
                x = XnT[:, bass.ds(c * CW, CW)]
                for f in range(NF):
                    u = e * NF + f
                    number = c * (NX * NF) + u
                    at_least(pe, s_hid, number - UB + 1)
                    if gated:
                        nc.tensor.matmul(bank[2 * (u % UB)][:, 0:CW], wup[:, e, 128 * f:128 * f + 128], x, start=True, stop=True)
                        last = nc.tensor.matmul(bank[2 * (u % UB) + 1][:, 0:CW], wup[:, e, FF + 128 * f:FF + 128 * f + 128], x,
                                                start=True, stop=True)
                    else:
                        last = nc.tensor.matmul(bank[u % UB][:, 0:CW], wup[:, e, 128 * f:128 * f + 128], x, start=True, stop=True)
                    last.then_inc(s_up, 1)

            def down(c, e):
                number = c * NX + e
                pe.wait_ge(s_hid, (number + 1) * NF)
                at_least(pe, s_tmp, number - DB + 1)
                for t in range(CH):
                    for f in range(NF):
                        last = nc.tensor.matmul(bank[4 + e % DB - (0 if gated else 1)][0:TT, D * t:D * t + D],
                                                hidden[(e * NF + f) % HS][:, TT * t:TT * t + TT], wdn[:, e, f, :],
                                                start=f == 0, stop=f == NF - 1)
                last.then_inc(s_dn, 1)

            def chunk(c):
                for e in range(NX):
                    up(c, e)
                    if e:
                        down(c, e - 1)
                down(c, NX - 1)
            steps(pe, chunk)

        @block.scalar
        def _(act):
            act.wait_ge(s_d, 1)
            nc.scalar.activation(m[:, 3, :], m[:, 2, :], ACT.Exp).then_inc(s_e, 1)

            def chunk(c):
                for u in range(NX * NF):
                    number = c * (NX * NF) + u
                    act.wait_ge(s_up, number + 1)
                    if gated:
                        at_least(act, s_hid, number - 1)
                        nc.scalar.activation(gate[u % 2][:, :], bank[2 * (u % UB)][:, 0:CW], ACT.Silu).then_inc(s_si, 1)
                    else:
                        if not (isinstance(c, int) and number < HS):
                            act.wait_ge(s_dn, before_hidden(c, u))
                        nc.scalar.activation(hidden[u % HS][:, :], bank[u % UB][:, 0:CW], ACT.Silu).then_inc(s_si, 1)
            steps(act, chunk)

        @block.vector
        def _(dve):
            link = chain(dve, sem(n + "chain"))

            def over(v):
                return v.unsqueeze(2).to_broadcast([TT, NTT, NE])

            dve.wait_ge(s_lg, 1)
            logits = bank[7][0:TT, 0:NTT * NE].rearrange("p (t e) -> p t e", e=NE)
            desc = small["desc"][:, :].unsqueeze(1).to_broadcast([TT, NTT, NE])
            if layer == 0:
                link(nc.vector.tensor_tensor(lg[:, :, :], logits, small["router_b"][:, :].unsqueeze(1).to_broadcast([TT, NTT, NE]), ALU.add))
            else:
                link(nc.vector.tensor_copy(lg[:, :, :], logits))
            cur = lg
            for k in range(2):
                link(nc.vector.reduce_max(m[:, k, :], cur[:, :, :], AX.X))
                link(nc.vector.tensor_tensor(r[2][:, :, :], cur[:, :, :], over(m[:, k, :]), ALU.is_equal))
                link(nc.vector.tensor_tensor(r[2][:, :, :], r[2][:, :, :], desc, ALU.mult))
                link(nc.vector.reduce_max(m[:, 4, :], r[2][:, :, :], AX.X))
                link(nc.vector.tensor_tensor(r[k][:, :, :], r[2][:, :, :], over(m[:, 4, :]), ALU.is_equal))
                if k == 0:
                    link(nc.vector.scalar_tensor_tensor(r[3][:, :, :], r[0][:, :, :], -1e30, lg[:, :, :], ALU.mult, ALU.add))
                    cur = r[3]
            nc.vector.tensor_tensor(m[:, 2, :], m[:, 1, :], m[:, 0, :], ALU.subtract).then_inc(s_d, 1)
            dve.wait_ge(s_e, 1)
            link(nc.vector.tensor_scalar(m[:, 5, :], m[:, 3, :], 1.0, None, ALU.add))
            link(nc.vector.reciprocal(m[:, 6, :], m[:, 5, :]))
            link(nc.vector.tensor_tensor(m[:, 7, :], m[:, 6, :], m[:, 3, :], ALU.mult))
            link(nc.vector.tensor_tensor(r[2][:, :, :], r[0][:, :, :], over(m[:, 6, :]), ALU.mult))
            link(nc.vector.tensor_tensor(r[3][:, :, :], r[1][:, :, :], over(m[:, 7, :]), ALU.mult))
            link(nc.vector.memset(comb[:, :, NE:NE + 1], 1.0))
            link(nc.vector.tensor_tensor(comb[:, :, 0:NE], r[2][:, :, :], r[3][:, :, :], ALU.add))

            def take(c, e):
                number = c * NX + e
                dve.wait_ge(s_dn, number + 1)
                w = comb[:, bass.ds(c * CH, CH), e:e + 1].to_broadcast([TT, CH, D])
                at_least(dve, s_acc, number - DB + 1)
                nc.vector.tensor_tensor(tmp[e % DB][:, :, :],
                                        bank[4 + e % DB - (0 if gated else 1)][0:TT, :].rearrange("p (t d) -> p t d", t=CH),
                                        w, ALU.mult).then_inc(s_tmp, 1)

            def chunk(c):
                for e in range(NX):
                    if gated:
                        for f in range(NF):
                            u = e * NF + f
                            number = c * (NX * NF) + u
                            dve.wait_ge(s_si, number + 1)
                            if not (isinstance(c, int) and number < HS):
                                dve.wait_ge(s_dn, before_hidden(c, u))
                            nc.vector.tensor_tensor(hidden[u % HS][:, :], bank[2 * (u % UB) + 1][:, 0:CW], gate[u % 2][:, :],
                                                    ALU.mult).then_inc(s_hid, 1)
                    if e:
                        take(c, e - 1)
                take(c, NX - 1)
            steps(dve, chunk)
            g = T["tg"][0:TT, 2 + layer:3 + layer]
            for c in range(NCH):
                dve.wait_ge(s_acc, (c + 1) * NX)
                k = slice(CH * c, CH * c + CH)
                nc.vector.scalar_tensor_tensor(X[:, k, :], total[:, k, :], g, X[:, k, :], ALU.mult, ALU.add)

        @block.gpsimd
        def _(pool):
            nc.gpsimd.memset(total[:, :, :], 0.0).then_inc(s_zero, 1)
            pool.wait_ge(s_zero, 1)

            def chunk(c):
                for e in range(NX):
                    number = c * NX + e
                    pool.wait_ge(s_tmp, number + 1)
                    at_least(pool, s_acc, number)
                    apart(pool)
                    k = total[:, bass.ds(c * CH, CH), :]
                    nc.gpsimd.tensor_tensor(k, k, tmp[e % DB][:, :, :], ALU.add).then_inc(s_acc, 1)
            steps(pool, chunk)


def kernel(**inputs):
    import concourse.bacc as bacc
    from concourse.bass_utils import run_bass_kernel_spmd

    x = {k: np.ascontiguousarray(v) for k, v in inputs.items()}
    arrays = {
        "x": x["x"].reshape(TOKENS, D), "ctx": x["ctx_1024"], "mask": x["mask_BxSxS2_bk1"].reshape(TOKENS, SK),
        "g_xattn": x["g_xattn"], "g_ffn": x["g_ffn"],
        "WqT0": x["L0_xattn_Wq"].T, "WkT0": x["L0_xattn_Wk"].T, "WvT0": x["L0_xattn_Wv"].T, "WpT0": x["L0_xattn_Wp"].T,
        "WqT1": x["L1_xattn_Wq"].T, "WkT1": x["L1_xattn_Wk"].T, "WvT1": x["L1_xattn_Wv"].T, "WpT1": x["L1_xattn_Wo"].T,
        "bp0": x["L0_xattn_bp"], "bp1": x["L1_xattn_bo"], "bq1": x["L1_xattn_bq"], "bk1": x["L1_xattn_bk"], "bv1": x["L1_xattn_bv"],
        "subln": x["L0_xattn_subln_w"], "lq1": x["L0_xattn_lq1"], "lk1": x["L0_xattn_lk1"], "lq2": x["L0_xattn_lq2"],
        "lk2": x["L0_xattn_lk2"], "routerT0": x["L0_ffn_router_w"].T, "router_b": x["L0_ffn_router_b"],
        "routerT1": x["L1_ffn_gate_w"].T,
        "wup0": np.concatenate([x["L0_ffn_w_up"], x["L0_ffn_shared_w_up"]]).transpose(2, 0, 1),
        "wdn0": np.concatenate([x["L0_ffn_w_down"], x["L0_ffn_shared_w_down"]]).reshape(NE + 1, D, FF // 128, 128).transpose(3, 0, 2, 1),
        "wup1": x["L1_ffn_w12"].transpose(2, 0, 1),
        "wdn1": x["L1_ffn_w3"].reshape(NE, D, FF // 128, 128).transpose(3, 0, 2, 1),
        "ident": np.eye(128, dtype=np.float32),
        **{f"headsel{i}": np.tile(np.arange(L.group_dims)[:, None] // L.hd == np.arange(L.group_heads), (3, 1)).astype(np.float32)
           for i, L in enumerate((L0, L1))},
        "ones_rows": np.repeat(np.array([[BIG], [1.0]], np.float16), SK, axis=1),
        "big_ident": np.tile(np.eye(SQ) * BIG, L1.group_heads).astype(np.float16),
        "desc": np.arange(NE, 0, -1).astype(np.float32),
    }
    nc = bacc.Bacc("TRN2", target_bir_lowering=False, num_devices=1)
    feeds, aps = {}, {}
    for name, array in arrays.items():
        array = np.ascontiguousarray(array)
        feeds[f"in_{name}"] = array
        aps[name] = nc.dram_tensor(f"in_{name}", array.shape, mybir.dt.from_np(array.dtype), kind="ExternalInput").ap()
    out = nc.dram_tensor("result", (TOKENS, D), F32, kind="ExternalOutput").ap()
    build(nc, aps, out)
    got = run_bass_kernel_spmd(nc, [feeds], core_ids=[0])
    return got.results[0]["result"].reshape(B, SQ, D)
```

```python
import math
from contextlib import ExitStack

import numpy as np
import concourse.bass as bass
from concourse import mybir

F32 = mybir.dt.float32
F16 = mybir.dt.float16
U8 = mybir.dt.uint8
ALU = mybir.AluOpType
ACT = mybir.ActivationFunctionType
AX = mybir.AxisListType

B, SQ, D, SK = 32, 56, 128, 1500
TOKENS = B * SQ
TT = 2 * SQ
NTT = TOKENS // TT
CH = 4
NCH = NTT // CH
CW = CH * TT
VH, VD = 16, 8
KT = 125
NKT = SK // KT
THIRD = 4
NTHIRD = NKT // THIRD
TK = THIRD * KT
NE = 8
FF = 256
EPS = 1e-5
LAMBDA_INIT = 0.8 - 0.6 * math.exp(-0.3 * 4)

QK_UP = 64.0
EXP_SCALE = 1.0 / (QK_UP * QK_UP)
BIG = 32768.0
SLOTS = 3


class Layer:

    def __init__(self, name, heads, hd, group_dims, masked):
        self.name = name
        self.heads, self.hd = heads, hd
        self.group_dims = group_dims
        self.groups = D // group_dims
        self.group_heads = group_dims // hd
        self.group_cols = self.group_heads * SQ
        self.masked = masked
        self.mask_rows = SQ if masked else 0
        self.score_rows = 3 * group_dims + self.mask_rows
        self.rows = self.score_rows + 2
        self.cols = heads * SQ
        self.halves = self.cols // 896
        self.half_groups = self.groups // self.halves
        self.tile = min(128, self.group_cols)
        self.whole_tiles = self.group_cols // self.tile * self.groups
        self.rest = self.group_cols % self.tile
        self.tiles = self.whole_tiles + self.rest * self.groups // self.tile
        assert self.rest in (0, 64)
        self.pieces = self.tiles * NTHIRD
        self.o_cols = self.cols // 4
        self.uses_f = 2


L0 = Layer("L0", 32, 4, 32, False)
L1 = Layer("L1", 16, 8, 16, True)


WIDE = {"ident": 128, **{f"W{w}T{i}": D for i in range(2) for w in "qkvp"}, "routerT0": NE, "routerT1": NE,
        "headsel0": L0.group_heads, "headsel1": L1.group_heads}
ROWS = {"gates": 4, "lambdas": 16, "bp0": D, "bp1": D, "bq1": D, "bv1": D, "router_b": NE, "desc": NE}


def unpacked(buffer, widths):
    parts, start = {}, 0
    for name, width in widths.items():
        parts[name] = buffer[:, start:start + width]
        start += width
    return parts


def at_least(eng, sem, value):
    if isinstance(value, int) and value <= 0:
        return
    eng.wait_ge(sem, value)


def build(nc, a, out):
    ctx = ExitStack()
    with ctx:
        def sb(name, shape, dt=F32):
            return ctx.enter_context(nc.sbuf_tensor(name, shape, dt))

        def sem(name):
            return ctx.enter_context(nc.semaphore(name))

        score_ps = [ctx.enter_context(nc.psum_tensor(f"score_ps{i}", [128, 2, 512], F32)) for i in range(2)]
        max_ps = [ctx.enter_context(nc.psum_tensor(f"max_ps{i}", [128, 512], F32)) for i in range(2)]
        acc_ps = ctx.enter_context(nc.psum_tensor("acc_ps", [128, 512], F32))
        spare_ps = ctx.enter_context(nc.psum_tensor("spare_ps", [128, 512], F32))
        bank = [score_ps[0][:, 0, :], score_ps[0][:, 1, :], score_ps[1][:, 0, :], score_ps[1][:, 1, :],
                max_ps[0][:, :], max_ps[1][:, :], acc_ps[:, :], spare_ps[:, :]]

        X = sb("X", [TT, NTT, D])
        XnT = sb("XnT", [128, TOKENS])
        attnT = sb("attnT", [128, TOKENS])
        neg_half = sb("neg_half", [128, 64])
        keep = sb("keep", [TT, NTT])
        wide = sb("wide", [128, sum(WIDE.values())])
        rows = sb("rows", [128, sum(ROWS.values())])
        columns = sb("columns", [128, 2])
        small = {**unpacked(wide, WIDE), **unpacked(rows, ROWS), "subln": columns[:, 0:1], "bk1": columns[:, 1:2]}
        tg = small["gates"]
        lam = small["lambdas"]
        ident = small["ident"]

        ks_words = L1.groups * SK
        kstack = [sb(f"kstack{i}", [128, ks_words], F16) for i in range(SLOTS)]
        qstack = [sb(f"qstack{i}", [128, L0.cols], F16) for i in range(SLOTS)]
        vext = [sb(f"vext{i}", [KT, NKT, VH // 2, 32]) for i in range(SLOTS)]
        probs = [sb(f"probs{i}", [KT, 2 * 896]) for i in range(2)]
        ctx_in = sb("ctx_in", [KT, NKT, D])
        ctxT = sb("ctxT", [128, 2, SK], F16)
        w_parts = sb("w_parts", [128, 2, 2, 2, D], F16)
        khl = sb("khl", [128, 2, SK], F16)
        qh = sb("qh", [128, TOKENS], F16)
        ql = sb("ql", [128, TOKENS], F16)
        qrows = sb("qrows", [128, L1.groups, SQ], F16)
        mask_in = sb("mask_in", [SQ, SK], U8)
        mask_big = sb("mask_big", [SQ, SK], F16)
        out_sb = sb("out_sb", [128, L0.o_cols])
        max_part = sb("max_part", [128, 16, NTHIRD])
        neg_max = sb("neg_max", [128, 16])
        max_rows = sb("max_rows", [16, 2, 128], F16)
        turned = sb("turned", [SQ, 2, 512])
        rden = sb("rden", [SQ, 2, 4, 4])
        heads_out = sb("heads_out", [SQ, 2, VH, VD])
        attn = sb("attn", [SQ, VH, VD])
        attn_sq = sb("attn_sq", [SQ, VH, VD])
        rms = sb("rms", [SQ, 2, VH])
        attn_n = sb("attn_n", [SQ, VH, VD])

        s_in = sem("inputs_loaded")
        s_set = sem("vector_setup")
        s_tanh = sem("tanh_done")
        loads = [(X[:, :, :], a["x"].rearrange("(t p) d -> p t d", p=TT)), (rows[:, :], a["rows"].partition_broadcast(128)),
                 (columns[:, :], a["columns"]), (wide[:, :], a["wide"])]

        lam_s = sb("lam_s", [128, 8])
        lam_t = sb("lam_t", [128, 8])

        with nc.Block() as block:
            @block.sync
            def _(sp):
                for dst, src in loads:
                    sp.dma_start(dst, src).then_inc(s_in, 16)

            @block.gpsimd
            def _(pool):
                for i in range(SLOTS):
                    nc.gpsimd.memset(vext[i][:, :, :, :], 0.0).then_inc(s_set, 1)
                pool.wait_ge(s_set, SLOTS)
                for i in range(SLOTS):
                    for h in range(2):
                        nc.gpsimd.memset(vext[i][:, :, :, 16 * h + VD:16 * h + VD + 1], 1.0)
                nc.gpsimd.memset(neg_half[:, :], -0.5)

            @block.vector
            def _(dve):
                link = chain(dve, sem("setup_chain"))
                dve.wait_ge(s_in, 16 * len(loads))
                link(nc.vector.tensor_tensor(lam_t[:, 0:4], lam[:, 0:4], lam[:, 4:8], ALU.mult))
                link(nc.vector.tensor_tensor(lam_t[:, 4:8], lam[:, 8:12], lam[:, 12:16], ALU.mult))
                nc.vector.reduce_sum(lam_s[:, 0:2], lam_t[:, :].rearrange("p (a b) -> p a b", a=2), AX.X).then_inc(s_tanh, 1)
                dve.wait_ge(s_tanh, 3)
                link(nc.vector.tensor_tensor(lam_s[:, 4:5], lam_s[:, 3:4], lam_s[:, 2:3], ALU.subtract))
                link(nc.vector.tensor_scalar(lam_s[:, 5:6], lam_s[:, 4:5], -LAMBDA_INIT, None, ALU.add))
                link(nc.vector.tensor_scalar(small["WpT0"][:, :], small["WpT0"][:, :], small["subln"][:, :],
                                             1.0 - LAMBDA_INIT, ALU.mult, ALU.mult))
                for i in range(2):
                    link(nc.vector.tensor_scalar(small[f"WpT{i}"][:, :], small[f"WpT{i}"][:, :], tg[:, i:i + 1], None, ALU.mult))
                    link(nc.vector.tensor_scalar(small[f"bp{i}"][:, :], small[f"bp{i}"][:, :], tg[:, i:i + 1], None, ALU.mult))
                    for w in range(2):
                        weight = small[f"W{'kv'[w]}T{i}"][:, :]
                        high, low = w_parts[:, i, w, 0, :], w_parts[:, i, w, 1, :]
                        link(nc.vector.tensor_scalar(weight, weight, QK_UP, None, ALU.mult))
                        link(nc.vector.tensor_copy(high, weight))
                        link(nc.vector.tensor_tensor(low, weight, high, ALU.subtract))
                link(nc.vector.tensor_scalar(small["bk1"][:, :], small["bk1"][:, :], QK_UP, None, ALU.mult))

            @block.scalar
            def _(act):
                act.wait_ge(s_tanh, 1)
                nc.scalar.activation(lam_s[:, 2:4], lam_s[:, 0:2], ACT.Exp).then_inc(s_tanh, 1)
                nc.scalar.activation(tg[:, :], tg[:, :], ACT.Tanh).then_inc(s_tanh, 1)

        q_dram = nc.dram_tensor("q_parts", (2, D, TOKENS), F16).ap()
        k_dram = nc.dram_tensor("k_parts", (2, D, SK), F16).ap()
        T = dict(nc=nc, a=a, q_dram=q_dram, k_dram=k_dram, sem=sem, bank=bank, score_ps=score_ps, max_ps=max_ps, acc_ps=acc_ps, spare_ps=spare_ps,
                 X=X, XnT=XnT, attnT=attnT, ident=ident, neg_half=neg_half, tg=tg, small=small, kstack=kstack,
                 qstack=qstack, vext=vext, probs=probs, ctx_in=ctx_in, ctxT=ctxT, w_parts=w_parts, khl=khl, qh=qh, ql=ql,
                 qrows=qrows, mask_in=mask_in, mask_big=mask_big, out_sb=out_sb, max_part=max_part,
                 neg_max=neg_max, max_rows=max_rows, turned=turned, rden=rden, heads_out=heads_out, attn=attn, attn_sq=attn_sq,
                 rms=rms, attn_n=attn_n, neg_lam=lam_s[0:SQ, 5:6], keep=keep, sb=sb, ctx=ctx)
        for L in (L0, L1):
            for kind in ("context", "mask"):
                T[f"{L.name}_{kind}_loaded"] = sem(f"{L.name}_{kind}_loaded")
        normalise(T, "norm0", 0)
        attend(T, L0)
        normalise(T, "norm0f", None, projected=0)
        feed_forward(T, 0)
        normalise(T, "norm1", 1)
        attend(T, L1)
        normalise(T, "norm1f", None, projected=1)
        feed_forward(T, 1)

        s_out = sem("result_stored")
        with nc.Block() as block:
            @block.sync
            def _(sp):
                sp.dma_start(out.rearrange("(t p) d -> p t d", p=TT), X[:, :, :]).then_inc(s_out, 16)
                sp.wait_ge(s_out, 16)


def apart(eng):
    eng.nop(nofuse=True)


def chain(eng, s):
    count = [0]

    def link(instruction):
        count[0] += 1
        instruction.then_inc(s, 1)
        eng.wait_ge(s, count[0])
    return link


def carve(words, start, shape):
    n = int(np.prod(shape))
    flat = words[:, 2 * start:2 * (start + n)].bitcast(F32)
    if len(shape) == 1:
        return flat
    if len(shape) == 2:
        return flat.rearrange("p (a b) -> p a b", a=shape[0])
    return flat.rearrange("p (a b c) -> p a b c", a=shape[0], b=shape[1])


def load_context(sp, T, L, n):
    sp.dma_start(T["ctx_in"][:, :, :],
                 T["a"]["ctx"][bass.ds(n, 1), :, :].rearrange("b (p t) d -> (b p) t d", t=NKT)).then_inc(T[L.name + "_context_loaded"], 16)
    if L.masked:
        sp.dma_start(T["mask_in"][:, :], T["a"]["mask"][bass.ds(n * SQ, SQ), :]).then_inc(T[L.name + "_mask_loaded"], 16)


def normalise(T, tag, layer, projected=None):
    nc, a, sem, bank = T["nc"], T["a"], T["sem"], T["bank"]
    X, XnT, ident, small = T["X"], T["XnT"], T["ident"], T["small"]
    xn = carve(T["kstack"][1][0:TT, :], 0, [NTT, D])
    xsq = [carve(T["kstack"][2][0:TT, :], CH * D * i, [CH, D]) for i in range(2)]
    st = carve(T["kstack"][2][0:TT, :], 2 * CH * D, [6, NTT])
    keep = T["keep"]
    if projected is not None:
        s_po = sem(tag + "_output_projected")
    s_cent = sem(tag + "_centred")
    s_sq = sem(tag + "_squared")
    s_sum2 = sem(tag + "_squares_summed")
    s_var = sem(tag + "_variance_ready")
    s_rstd = sem(tag + "_rstd_ready")
    s_xn = sem(tag + "_normalised")
    s_xt = sem(tag + "_transposed")
    s_xnt = sem(tag + "_xnt_ready")
    if layer is not None:
        s_qn = sem(tag + "_queries_projected")
        s_qs = sem(tag + "_queries_scaled")
        s_qt = sem(tag + "_queries_transposed")
        s_qh = sem(tag + "_query_high_ready")
        s_ql = sem(tag + "_query_low_ready")
        T[f"queries_stored{layer}"] = s_qd = sem(tag + "_queries_stored")
    head_scale = QK_UP * (L0.hd, L1.hd)[layer or 0] ** -0.5
    with nc.Block() as block:
        if projected is not None:
            T[f"weights_loaded{projected}"] = s_w = sem(tag + "_expert_weights_loaded")

            @block.sync
            def _(sp):
                up, down = expert_weights(T, projected)
                sp.dma_start(up, a[f"wup{projected}"]).then_inc(s_w, 16)
                sp.dma_start(down, a[f"wdn{projected}"]).then_inc(s_w, 16)

        if layer is not None:
            @block.sync
            def _(sp):
                load_context(sp, T, (L0, L1)[layer], 0)
                sp.wait_ge(s_qh, NCH)
                sp.dma_start(T["q_dram"][0, :, :], T["qh"][:, :]).then_inc(s_qd, 16)
                sp.wait_ge(s_ql, NCH)
                sp.dma_start(T["q_dram"][1, :, :], T["ql"][:, :]).then_inc(s_qd, 16)

        @block.vector
        def _(dve):
            link = chain(dve, sem(tag + "_chain"))

            def wide(v):
                return v.unsqueeze(2).to_broadcast([TT, CH, D])

            def centre(c):
                x = X[:, CH * c:CH * c + CH, :]
                s = [st[:, k, CH * c:CH * c + CH] for k in range(2)]
                if projected is not None:
                    dve.wait_ge(s_po, c + 1)
                    link(nc.vector.tensor_tensor(x, bank[4 + c][0:TT, :].rearrange("p (t d) -> p t d", t=CH), x, ALU.add))
                link(nc.vector.reduce_sum(s[0], x, AX.X))
                link(nc.vector.tensor_scalar(s[1], s[0], 1.0 / D, None, ALU.mult))
                nc.vector.tensor_tensor(xn[:, CH * c:CH * c + CH, :], x, wide(s[1]), ALU.subtract).then_inc(s_cent, 1)

            def variance(c):
                s = [st[:, k, CH * c:CH * c + CH] for k in range(6)]
                dve.wait_ge(s_sq, c + 1)
                nc.vector.reduce_sum(s[2], xsq[c % 2][:, :, :], AX.X).then_inc(s_sum2, 1)
                dve.wait_ge(s_sum2, c + 1)
                nc.vector.tensor_scalar(s[3], s[2], 1.0 / D, EPS, ALU.mult, ALU.add).then_inc(s_var, 1)

            centre(0)
            for c in range(1, NCH):
                centre(c)
                variance(c - 1)
            variance(NCH - 1)
            if layer is None:
                return
            if layer == 1:
                for c in range(NCH):
                    dve.wait_ge(s_qn, c + 1)
                    dst = xn[:, CH * c:CH * c + CH, :]
                    ps = bank[4 + c][0:TT, :].rearrange("p (t d) -> p t d", t=CH)
                    bq = small["bq1"][0:TT, :].unsqueeze(1).to_broadcast([TT, CH, D])
                    link(nc.vector.tensor_tensor(dst, ps, bq, ALU.add))
                    nc.vector.tensor_tensor(dst, dst, wide(keep[:, CH * c:CH * c + CH]), ALU.mult).then_inc(s_qs, 1)
            for c in range(NCH):
                dve.wait_ge(s_qh, c + 1)
                nc.vector.tensor_tensor(T["ql"][:, CW * c:CW * c + CW], bank[c][:, 0:CW],
                                        T["qh"][:, CW * c:CW * c + CW], ALU.subtract).then_inc(s_ql, 1)

        @block.gpsimd
        def _(pool):
            for c in range(NCH):
                pool.wait_ge(s_var, c + 1)
                nc.gpsimd.tensor_tensor(st[:, 4, CH * c:CH * c + CH], st[:, 3, CH * c:CH * c + CH],
                                        T["neg_half"][0:TT, 0:CH], ALU.pow).then_inc(s_rstd, 1)
                pool.wait_ge(s_rstd, c + 1)
                xm = xn[:, CH * c:CH * c + CH, :]
                nc.gpsimd.tensor_tensor(xm, xm, st[:, 4, CH * c:CH * c + CH].unsqueeze(2).to_broadcast([TT, CH, D]),
                                        ALU.mult).then_inc(s_xn, 1)
            if layer is not None:
                bias = small[f"bp{layer}"][0:TT, :].unsqueeze(1).to_broadcast([TT, CH, D])
                for c in range(NCH):
                    x = X[:, CH * c:CH * c + CH, :]
                    pool.wait_ge(s_cent, c + 1)
                    nc.gpsimd.tensor_tensor(x, x, bias, ALU.add)

        @block.tensor
        def _(pe):
            for c in range(NCH if projected is not None else 0):
                for t in range(CH):
                    k = CW * c + TT * t
                    last = nc.tensor.matmul(bank[4 + c][0:TT, D * t:D * t + D], T["attnT"][:, k:k + TT],
                                            small[f"WpT{projected}"][:, :], start=True, stop=True)
                last.then_inc(s_po, 1)
            for c in range(NCH):
                pe.wait_ge(s_xn, c + 1)
                for t in range(CH):
                    last = nc.tensor.transpose(bank[c][:, TT * t:TT * t + TT], xn[:, CH * c + t, :], ident[0:TT, 0:TT])
                last.then_inc(s_xt, 1)
            if layer is None:
                return
            for c in range(NCH):
                pe.wait_ge(s_xnt, c + 1)
                for t in range(CH):
                    last = nc.tensor.matmul(bank[4 + c][0:TT, D * t:D * t + D],
                                            XnT[:, CW * c + TT * t:CW * c + TT * t + TT],
                                            small[f"WqT{layer}"][:, :], start=True, stop=True)
                last.then_inc(s_qn, 1)
            for c in range(NCH):
                pe.wait_ge(s_qs, c + 1)
                for t in range(CH):
                    last = nc.tensor.transpose(bank[c][:, TT * t:TT * t + TT], xn[:, CH * c + t, :], ident[0:TT, 0:TT])
                last.then_inc(s_qt, 1)

        @block.scalar
        def _(act):
            for c in range(NCH):
                act.wait_ge(s_cent, c + 1)
                if c >= 2:
                    act.wait_ge(s_sum2, c - 1)
                nc.scalar.activation(xsq[c % 2][:, :, :], xn[:, CH * c:CH * c + CH, :], ACT.Square).then_inc(s_sq, 1)
            for c in range(NCH):
                act.wait_ge(s_xt, c + 1)
                nc.scalar.activation(XnT[:, CW * c:CW * c + CW], bank[c][:, 0:CW], ACT.Copy).then_inc(s_xnt, 1)
            if layer is None:
                return
            if layer == 0:
                for c in range(NCH):
                    act.wait_ge(s_qn, c + 1)
                    nc.scalar.activation(xn[:, CH * c:CH * c + CH, :].rearrange("p t d -> p (t d)"), bank[4 + c][0:TT, :],
                                         ACT.Copy, scale=head_scale).then_inc(s_qs, 1)
            for c in range(NCH):
                act.wait_ge(s_qt, c + 1)
                nc.scalar.activation(T["qh"][:, CW * c:CW * c + CW], bank[c][:, 0:CW], ACT.Copy).then_inc(s_qh, 1)


def attend(T, L):
    nc, a, sem, ident, small = T["nc"], T["a"], T["sem"], T["ident"], T["small"]
    score_ps, max_ps, acc_ps, spare_ps = T["score_ps"], T["max_ps"], T["acc_ps"], T["spare_ps"]
    probs, ctx_in, ctxT, khl, vext = T["probs"], T["ctx_in"], T["ctxT"], T["khl"], T["vext"]
    qrows, mask_in, mask_big, out_sb = T["qrows"], T["mask_in"], T["mask_big"], T["out_sb"]
    max_part, neg_max, max_rows = T["max_part"], T["neg_max"], T["max_rows"]
    turned, rden, heads_out, attn, attn_sq, rms, attn_n = (T[k] for k in ("turned", "rden", "heads_out", "attn", "attn_sq", "rms", "attn_n"))
    layer = 0 if L is L0 else 1
    GD, NG, GC, H = L.group_dims, L.groups, L.group_cols, L.halves
    kstack = [T["kstack"][i][:, 0:NG * SK].rearrange("p (g k) -> p g k", g=NG) for i in range(SLOTS)]
    qstack = [T["qstack"][i][:, 0:L.cols].rearrange("p (g c) -> p g c", g=NG) for i in range(SLOTS)]
    Wk, Wv = ([T["w_parts"][:, layer, w, part, :] for part in range(2)] for w in range(2))
    R = L.rows
    S = L.heads // VH

    s_const = sem(L.name + "_constant_rows")
    s_ctx, s_mask = T[L.name + "_context_loaded"], T[L.name + "_mask_loaded"]
    s_big = sem(L.name + "_mask_scaled")
    s_ks = [sem(f"{L.name}_kstack_filled{i}") for i in range(SLOTS)]
    s_qr = sem(L.name + "_query_rows_loaded")
    if L.masked:
        s_kd = [sem(f"{L.name}_key_third_stored{i}") for i in range(NTHIRD)]
    s_mrow = [sem(f"{L.name}_maximum_rows_filled{i}") for i in range(SLOTS)]
    s_ctxT = sem(L.name + "_ctxT_high_ready")
    s_cl = sem(L.name + "_ctxT_low_ready")
    s_kh = sem(L.name + "_key_high_ready")
    s_kl = sem(L.name + "_key_low_ready")
    s_v = sem(L.name + "_values_ready")
    s_qs = sem(L.name + "_qstack_ready")
    s_ready = sem(L.name + "_spare_filled")
    s_turned = sem(L.name + "_turned_output_ready")
    s_rden = sem(L.name + "_reciprocals_ready")
    s_at = sem(L.name + "_attnT_ready")
    s_scores = sem(L.name + "_scores_ready")
    s_exp = sem(L.name + "_probs_ready")
    s_av = sem(L.name + "_weighted_values_done")
    s_piece = sem(L.name + "_max_scores_ready")
    s_red = sem(L.name + "_max_reduced")
    s_neg = sem(L.name + "_negative_max_ready")
    s_mr = sem(L.name + "_max_split")
    s_os = sem(L.name + "_output_copied")
    s_attn = sem(L.name + "_attention_normalised")
    CONST = 16 * SLOTS * (2 if L.masked else 1)

    K_INC = 16 * (3 * NTHIRD + 1 if L.masked else 3 * NG)
    Q_INC = 16 * 3
    M_INC = 32 * (L.whole_tiles // NG + (1 if L.rest else 0))
    LAST = NKT - 1

    prep = [("T", 0), ("K", 0), ("T", 1), ("K", 1), ("T", 2), ("K", 2), ("V", 0), ("V", 1), ("V", 2)]
    if L is L0:
        where = {("T", 0): (0, 0), ("K", 0): (1, 0), ("F", 0): (1, 1), ("T", 1): (2, 0), ("F", 1): (2, 1), ("K", 1): (3, 0),
                 ("T", 2): (4, 0), ("K", 2): (5, 0), ("V", 0): (6, 0), ("V", 1): (7, 0), ("V", 2): (8, 0), ("A", 0): (9, 0),
                 ("M", 0): (9, 1)}
    else:
        where = {("T", 0): (0, 0), ("K", 0): (1, 0), ("T", 1): (1, 1), ("K", 1): (2, 1), ("T", 2): (3, 1), ("K", 2): (4, 1),
                 ("F", 0): (5, 1), ("F", 1): (6, 0), ("V", 0): (6, 1), ("V", 1): (7, 0), ("V", 2): (8, 0), ("A", 0): (9, 0),
                 ("M", 0): (9, 1)}
    per_step = -(-L.pieces // NKT)
    unused = NKT * per_step - L.pieces
    spread = NKT * per_step // unused if unused else NKT * per_step + 1
    assert unused == NKT * per_step // spread
    AHEAD = 3
    early = AHEAD * per_step
    turnaround = [("F", i) for i in range(L.uses_f)] + [("A", 0)]

    def spare_uses(has_f, has_m, has_p):
        uses = (prep if has_p else []) + (turnaround if has_f else []) + ([("M", 0)] if has_m else [])
        return sorted(uses, key=lambda u: where[u])

    class At:

        def __init__(self, j, c):
            self.j, self.c = j, c
            self.n = j * SLOTS + c
            self.slot = c % SLOTS
            self.turn = j + c // SLOTS

        def plus(self, d):
            return At(self.j, self.c + d)

    first_preps = [(At(0, n - 2), kind, i) for n in range(2) for kind in "TKV" for i in range(NTHIRD)]
    first_banks = [spare_ps[:, :]] + [score_ps[b][:, k, :] for b in range(2) for k in range(2)]

    FULL = len(spare_uses(True, True, True))
    PROLOGUE = 2 * len(prep) + 1
    FIRST = PROLOGUE + len(prep) + 1

    LOOPS = (B - 5) // SLOTS

    def iterations(eng, body, prologue=None, epilogue=None):
        if prologue:
            prologue()
        body(At(0, 0), PROLOGUE, spare_uses(False, True, True), False, True, True)
        with eng.Fori(0, LOOPS) as j:
            for c in range(1, 1 + SLOTS):
                at = At(j, c)
                body(at, (at.n - 1) * FULL + FIRST, spare_uses(True, True, True), True, True, True)
        before = FIRST + SLOTS * LOOPS * FULL
        for n in range(SLOTS * LOOPS + 1, B):
            has_m, has_p = n + 1 < B, n + 2 < B
            uses = spare_uses(True, has_m, has_p)
            body(At(0, n), before, uses, True, has_m, has_p)
            before += len(uses)
        if epilogue:
            epilogue(before)

    def copied_out(at, kind, i):
        p = at.plus(2)
        return {"T": (s_cl, NTHIRD * p.n + i + 1), "K": (s_kl, NTHIRD * p.n + i + 1),
                "V": (s_v, NTHIRD * p.n + i + 1), "M": (s_mr, at.n + 2),
                "F": (s_turned, (at.n - 1) * L.uses_f + i + 1), "A": (s_at, at.n)}[kind]

    def at_step(uses, base, t, side):
        return [(kind, i, base + k) for k, (kind, i) in enumerate(uses) if where[kind, i] == (t, side)]

    def searched(at, t, k):
        if k >= per_step:
            return []
        d, place = (1, early + t * per_step + k) if t < NKT - AHEAD else (2, (t - NKT + AHEAD) * per_step + k)
        if place % spread == spread - 1 or isinstance(at.n, int) and at.n + d >= B:
            return []
        return [(at.plus(d), place - place // spread)]

    with nc.Block() as block:
        @block.sync
        def _(sp):
            def constant_rows():
                for i in range(SLOTS):
                    sp.dma_start(kstack[i][R - 2:R, :, :],
                                 a["ones_rows"].unsqueeze(1).to_broadcast([2, NG, SK])).then_inc(s_const, 16)
                    if L.masked:
                        sp.dma_start(qstack[i][3 * GD:3 * GD + SQ, :, :],
                                     a["big_ident"].unsqueeze(1).to_broadcast([SQ, NG, GC])).then_inc(s_const, 16)

            def load(at):
                if L.masked:
                    at_least(sp, s_big, at.n)
                load_context(sp, T, L, at.n)

            def load_q(at):
                if isinstance(at.n, int) and at.n == 0:
                    sp.wait_ge(T[f"queries_stored{layer}"], 32)
                at_least(sp, s_qs, at.n)
                apart(sp)
                for row, part in ((0, 0), (GD, 1), (2 * GD, 0)):
                    sp.dma_start(qrows[row:row + GD, 0:NG, :],
                                 T["q_dram"][part, :, bass.ds(at.n * SQ, SQ)].rearrange("(g r) q -> r g q", g=NG)).then_inc(s_qr, 16)

            def fill_k(at):
                sp.wait_ge(s_kl, NTHIRD * (at.n + 1))
                for g in range(NG):
                    for row, part in ((0, 0), (GD, 0), (2 * GD, 1)):
                        sp.dma_start(kstack[at.slot][row:row + GD, g, :],
                                     khl[GD * g:GD * g + GD, part, :]).then_inc(s_ks[at.slot], 16)

            def fill_mask(at):
                at_least(sp, s_scores, (at.n - 2) * NKT * H)
                apart(sp)
                sp.wait_ge(s_big, at.n + 1)
                sp.dma_start(kstack[at.slot][3 * GD:3 * GD + SQ, :, :],
                             mask_big[:, :].unsqueeze(1).to_broadcast([SQ, NG, SK])).then_inc(s_ks[at.slot], 16)

            def store_k_third(at, i):
                sp.wait_ge(s_kl, NTHIRD * at.n + i + 1)
                apart(sp)
                k = slice(TK * i, TK * i + TK)
                sp.dma_start(T["k_dram"][:, :, k].rearrange("a p k -> p a k"), khl[:, :, k]).then_inc(s_kd[i], 16)

            def fill_k_third(at, i):
                sp.wait_ge(s_kd[i], 16 * (at.n + 1))
                k = slice(TK * i, TK * i + TK)
                for row, part in ((0, 0), (GD, 0), (2 * GD, 1)):
                    sp.dma_start(kstack[at.slot][row:row + GD, :, k],
                                 T["k_dram"][part, :, k].rearrange("(g r) k -> r g k", g=NG)).then_inc(s_ks[at.slot], 16)

            def fill_m(at):
                sp.wait_ge(s_mr, at.n + 1)
                for part in range(2):
                    row = qstack[at.slot][L.score_rows + part:L.score_rows + part + 1, :, :]
                    for i in range(L.whole_tiles // NG):
                        sp.dma_start(row[:, :, L.tile * i:L.tile * (i + 1)],
                                     max_rows[NG * i:NG * (i + 1), part, 0:L.tile]).then_inc(s_mrow[at.slot], 16)
                    if L.rest:
                        sp.dma_start(row[:, :, GC - L.rest:GC],
                                     max_rows[L.whole_tiles:L.tiles, part, 0:L.tile]).then_inc(s_mrow[at.slot], 16)

            def fill(at, after):
                if L.masked:
                    fill_mask(at)
                    store_k_third(at, 0)
                    store_k_third(at, 1)
                    fill_k_third(at, 0)
                sp.wait_ge(s_cl, NTHIRD * (at.n + 1))
                if after:
                    load(at.plus(1))
                if L.masked:
                    store_k_third(at, 2)
                    fill_k_third(at, 1)
                    fill_k_third(at, 2)
                else:
                    fill_k(at)
                if after:
                    load_q(at.plus(1))

            def prologue():
                load_q(At(0, 0))
                constant_rows()
                for n in range(2):
                    fill(At(0, n), True)
                fill_m(At(0, 0))

            def body(at, base, uses, has_f, has_m, has_p):
                if has_p:
                    fill(at.plus(2), not (isinstance(at.n, int) and at.n + 3 >= B))
                if has_m:
                    fill_m(at.plus(1))

            iterations(sp, body, prologue)

        s_chain = sem(L.name + "_normalisation_chain")
        s_high = sem(L.name + "_max_high_ready")
        LINKS = 2 * S + (8 if L is L0 else 0)

        def turned_view(x, h):
            return turned[:, :, 0:256 * S].rearrange("q i (s a j e) -> q i s a j e", s=S, a=2, j=4)[:, :, x, h, :, :]

        @block.gpsimd
        def _(pool):
            sel = small[f"headsel{layer}"]

            def prepare(at):
                prev = at.plus(-1)
                if L.masked:
                    pool.wait_ge(s_mask, 16 * (at.n + 1))
                    if not (isinstance(at.n, int) and at.n == 0):
                        pool.wait_ge(s_ks[prev.slot], K_INC * (prev.turn + 1))
                    apart(pool)
                    nc.gpsimd.tensor_scalar(mask_big[:, :].rearrange("q (t p) -> q t p", t=NKT),
                                            mask_in[:, :].rearrange("q (p t) -> q t p", t=NKT),
                                            -BIG, None, ALU.mult).then_inc(s_big, 1)
                pool.wait_ge(s_qr, Q_INC * (at.n + 1))
                at_least(pool, s_scores, (at.n - 2) * NKT * H)
                nc.gpsimd.tensor_tensor(
                    qstack[at.slot][0:3 * GD, :, :].rearrange("r g (h q) -> r g h q", q=SQ),
                    qrows[0:3 * GD, 0:NG, :].unsqueeze(2).to_broadcast([3 * GD, NG, L.group_heads, SQ]),
                    sel[0:3 * GD, :].unsqueeze(1).unsqueeze(3).to_broadcast([3 * GD, NG, L.group_heads, SQ]), ALU.mult).then_inc(s_qs, 1)

            def finish(n):
                count = [0]

                def link(instruction):
                    count[0] += 1
                    instruction.then_inc(s_chain, 1)
                    pool.wait_ge(s_chain, (n - 1) * LINKS + count[0])

                pool.wait_ge(s_rden, n * 2)
                for h in range(2):
                    for x in range(S):
                        ins = nc.gpsimd.tensor_tensor(
                            heads_out[:, x, :, :].rearrange("q (i j a) d -> q i j a d", i=2, a=2)[:, :, :, h, :],
                            turned_view(x, h)[:, :, :, 16 * h:16 * h + VD],
                            rden[:, h, 0:2 * S, :].rearrange("q (i s) j -> q i s j", i=2)[:, :, x, :].unsqueeze(3).to_broadcast([SQ, 2, 4, VD]),
                            ALU.mult)
                        link(ins)
                if L is L0:
                    apart(pool)
                    link(nc.gpsimd.tensor_scalar(attn[:, :, :], heads_out[:, 1, :, :], T["neg_lam"], None, ALU.mult))
                    link(nc.gpsimd.tensor_tensor(attn[:, :, :], attn[:, :, :], heads_out[:, 0, :, :], ALU.add))
                    link(nc.gpsimd.tensor_tensor(attn_sq[:, :, :], attn[:, :, :], attn[:, :, :], ALU.mult))
                    for w in (4, 2, 1):
                        link(nc.gpsimd.tensor_tensor(attn_sq[:, :, 0:w], attn_sq[:, :, 0:w], attn_sq[:, :, w:2 * w], ALU.add))
                    apart(pool)
                    link(nc.gpsimd.tensor_scalar(rms[:, 0, :], attn_sq[:, :, 0], 1.0 / VD, EPS, ALU.mult, ALU.add))
                    link(nc.gpsimd.tensor_tensor(rms[:, 1, :], rms[:, 0, :], T["neg_half"][0:SQ, 0:VH], ALU.pow))
                    nc.gpsimd.tensor_tensor(attn_n[:, :, :], attn[:, :, :], rms[:, 1, :].unsqueeze(2).to_broadcast([SQ, VH, VD]),
                                            ALU.mult).then_inc(s_attn, 1)
                else:
                    nc.gpsimd.tensor_tensor(attn_n[:, :, :].rearrange("q h d -> q (h d)"),
                                            heads_out[:, 0, :, :].rearrange("q h d -> q (h d)"),
                                            small["bv1"][0:SQ, :], ALU.add).then_inc(s_attn, 1)

            def body(at, base, uses, has_f, has_m, has_p):
                if has_p:
                    prepare(at.plus(2))
                if has_f:
                    finish(at.n)

            iterations(pool, body, lambda: (prepare(At(0, 0)), prepare(At(0, 1))), lambda before: finish(B))

        @block.tensor
        def _(pe):
            def use(at, kind, i, before, spare_ps=spare_ps):
                if before:
                    pe.wait_ge(*copied_out(*before))
                p = at.plus(2)
                if kind == "T":
                    if i == 0:
                        pe.wait_ge(s_ctx, 16 * (p.n + 1))
                    for t in range(THIRD):
                        last = nc.tensor.transpose(spare_ps[:, KT * t:KT * t + KT], ctx_in[:, THIRD * i + t, :], ident[0:KT, 0:KT])
                    last.then_inc(s_ready, 1)
                if kind == "K":
                    pe.wait_ge(s_cl, NTHIRD * p.n + i + 1)
                    for k, (w, x) in enumerate(((0, 0), (1, 0), (0, 1))):
                        last = nc.tensor.matmul(spare_ps[:, 0:TK], Wk[w], ctxT[:, x, TK * i:TK * i + TK], start=k == 0, stop=k == 2)
                    last.then_inc(s_ready, 1)
                if kind == "V":
                    for t in range(THIRD):
                        c = TK * i + KT * t
                        for k, (x, w) in enumerate(((0, 0), (0, 1), (1, 0))):
                            last = nc.tensor.matmul(spare_ps[0:KT, D * t:D * t + D], ctxT[:, x, c:c + KT], Wv[w],
                                                    start=k == 0, stop=k == 2)
                    last.then_inc(s_ready, 1)
                if kind == "M":
                    pe.wait_ge(s_neg, at.n + 2)
                    nc.tensor.transpose(spare_ps[0:L.tiles, 0:L.tile], neg_max[0:L.tile, 0:L.tiles], ident[0:L.tile, 0:L.tile]).then_inc(s_ready, 1)
                if kind == "F":
                    pe.wait_ge(s_os, at.n)
                    apart(pe)
                    for b in range(2 * S):
                        k = (i * 2 * S + b) * SQ
                        last = nc.tensor.transpose(spare_ps[0:SQ, 128 * b:128 * b + 128], out_sb[:, k:k + SQ], ident[:, :])
                    last.then_inc(s_ready, 1)
                if kind == "A":
                    pe.wait_ge(s_attn, at.n)
                    apart(pe)
                    nc.tensor.transpose(spare_ps[:, 0:SQ], attn_n[:, :, :].rearrange("q h d -> q (h d)"), ident[0:SQ, 0:SQ]).then_inc(s_ready, 1)

            def search(at, p):
                u, third = p // NTHIRD, p % NTHIRD
                if p == 0:
                    pe.wait_ge(s_ks[at.slot], K_INC * (at.turn + 1))
                    pe.wait_ge(s_qs, at.n + 1)
                at_least(pe, s_red, at.n * L.pieces + p - 1)
                if u < L.whole_tiles:
                    parts = [(0, L.tile, u % NG, u // NG * L.tile)]
                else:
                    g = (u - L.whole_tiles) * 2
                    parts = [(L.rest * i, L.rest * (i + 1), g + i, GC - L.rest) for i in range(2)]
                for start, end, g, column in parts:
                    last = nc.tensor.matmul(max_ps[p % 2][start:end, 0:TK],
                                            qstack[at.slot][0:L.score_rows, g, column:column + end - start],
                                            kstack[at.slot][0:L.score_rows, g, TK * third:TK * third + TK],
                                            start=True, stop=True, skip_group_check=True)
                last.then_inc(s_piece, 1)

            def scores(at, t, h):
                number = (at.n * NKT + t) * H + h
                at_least(pe, s_exp, number - 1)
                if t == 0 and h == 0:
                    pe.wait_ge(s_mrow[at.slot], M_INC * (at.turn + 1))
                buf = score_ps[(t * H + h) % 2]
                for k in range(L.half_groups):
                    g = h * L.half_groups + k
                    per_bank = L.half_groups // 2
                    o = (k % per_bank) * GC
                    last = nc.tensor.matmul(buf[0:KT, k // per_bank, o:o + GC], kstack[at.slot][0:R, g, KT * t:KT * t + KT],
                                            qstack[at.slot][0:R, g, :], start=True, stop=True)
                last.then_inc(s_scores, 1)

            def weigh(at, t, i):
                if i == 0:
                    pe.wait_ge(s_exp, (at.n * NKT + t + 1) * H)
                    if t == 0:
                        at_least(pe, s_os, at.n)
                        pe.wait_ge(s_v, NTHIRD * (at.n + 1))
                for j in range(4):
                    u = 4 * i + j
                    moving = probs[t % 2][:, 0:S * 896].rearrange("k (s c) -> k s c", s=S)[:, :, TT * u:TT * u + TT]
                    last = nc.tensor.matmul(
                        acc_ps[32 * j:32 * j + 32, TT * S * i:TT * S * (i + 1)].rearrange("p (s c) -> p s c", s=S),
                        vext[at.slot][:, t, u, :], moving, start=(t == 0 and i == 0), stop=(t == LAST),
                        skip_group_check=True)
                if i == 1:
                    last.then_inc(s_av, 1)

            def prologue():
                turns = len(first_banks)
                for k, (at, kind, i) in enumerate(first_preps):
                    use(at, kind, i, first_preps[k - turns] if k >= turns else None, first_banks[k % turns])
                for k in range(len(first_preps) - turns, len(first_preps)):
                    pe.wait_ge(*copied_out(*first_preps[k]))
                pe.wait_ge(s_const, CONST)
                for p in range(L.pieces):
                    search(At(0, 0), p)
                use(At(0, -1), "M", 0, None)
                for p in range(early - early // spread):
                    search(At(0, 1), p)

            def body(at, base, uses, has_f, has_m, has_p):
                before = (at.plus(-1), "M", 0)

                def step_uses(t, side):
                    nonlocal before
                    for kind, i, _ in at_step(uses, base, t, side):
                        use(at, kind, i, before)
                        before = (at, kind, i)

                def step_search(t, k):
                    for ahead, p in searched(at, t, k):
                        search(ahead, p)

                for t in range(NKT):
                    step_uses(t, 0)
                    for h in range(H):
                        scores(at, t, h)
                        step_search(t, h)
                    for i in range(2):
                        if t:
                            weigh(at, t - 1, i)
                        elif has_f:
                            weigh(at.plus(-1), LAST, i)
                        if i == 0:
                            step_uses(t, 1)
                        step_search(t, H + i)

            def epilogue(base):
                for i in range(2):
                    weigh(At(0, B - 1), LAST, i)
                before = (At(0, B - 1), "A", 0)
                for kind, i in turnaround:
                    use(At(0, B), kind, i, before)
                    before = (At(0, B), kind, i)

            iterations(pe, body, prologue, epilogue)

        @block.scalar
        def _(act):
            def drain(at, kind, i, number, spare_ps=spare_ps):
                p = at.plus(2)
                if kind == "M":
                    return
                act.wait_ge(s_ready, number + 1)
                if kind == "T":
                    nc.scalar.activation(ctxT[:, 0, TK * i:TK * i + TK], spare_ps[:, 0:TK], ACT.Copy).then_inc(s_ctxT, 1)
                if kind == "K":
                    if i == 0 and not (isinstance(p.n, int) and p.n == 0):
                        prev = p.plus(-1)
                        act.wait_ge(s_ks[prev.slot], K_INC * (prev.turn + 1))
                    if L is L0:
                        nc.scalar.activation(khl[:, 0, TK * i:TK * i + TK], spare_ps[:, 0:TK], ACT.Copy).then_inc(s_kh, 1)
                    else:
                        nc.scalar.activation(khl[:, 0, TK * i:TK * i + TK], spare_ps[:, 0:TK], ACT.Identity,
                                             bias=small["bk1"][:, :]).then_inc(s_kh, 1)
                if kind == "V":
                    nc.scalar.activation(
                        vext[p.slot][:, THIRD * i:THIRD * i + THIRD, :, :].rearrange("k t u (a e) -> k t (u a) e", a=2)[:, :, :, 0:VD],
                        spare_ps[0:KT, :].rearrange("k (t h d) -> k t h d", t=THIRD, d=VD), ACT.Copy,
                        scale=1.0 / QK_UP).then_inc(s_v, 1)
                if kind == "F":
                    if i == 0 and not (isinstance(at.n, int) and at.n == 1):
                        act.wait_ge(s_attn, at.n - 1)
                    nc.scalar.activation(turned[:, i, 0:256 * S], spare_ps[0:SQ, 0:256 * S], ACT.Copy).then_inc(s_turned, 1)
                if kind == "A":
                    nc.scalar.activation(T["attnT"][:, bass.ds((at.n - 1) * SQ, SQ)], spare_ps[:, 0:SQ], ACT.Copy).then_inc(s_at, 1)

            def exps(at, t, h):
                number = (at.n * NKT + t) * H + h
                act.wait_ge(s_scores, number + 1)
                if h == 0:
                    at_least(act, s_av, at.n * NKT + t - 1)
                nc.scalar.activation(probs[t % 2][:, 896 * h:896 * h + 896].rearrange("k (b c) -> k b c", b=2),
                                     score_ps[(t * H + h) % 2][0:KT, :, 0:448], ACT.Exp, scale=EXP_SCALE).then_inc(s_exp, 1)

            def copy_output(n):
                act.wait_ge(s_av, n * NKT)
                nc.scalar.activation(out_sb[:, 0:L.o_cols], acc_ps[:, 0:L.o_cols], ACT.Copy).then_inc(s_os, 1)

            def prologue():
                for k, (at, kind, i) in enumerate(first_preps):
                    drain(at, kind, i, k, first_banks[k % len(first_banks)])

            def body(at, base, uses, has_f, has_m, has_p):
                for t in range(NKT):
                    for kind, i, number in at_step(uses, base, t, 0):
                        drain(at, kind, i, number)
                    for h in range(H):
                        exps(at, t, h)
                    if t == 0 and has_f:
                        copy_output(at.n)
                    for kind, i, number in at_step(uses, base, t, 1):
                        drain(at, kind, i, number)

            def epilogue(before):
                copy_output(B)
                for k, (kind, i) in enumerate(turnaround):
                    drain(At(0, B), kind, i, before + k)

            iterations(act, body, prologue, epilogue)


        @block.vector
        def _(dve):
            def drain(at, kind, i, number, spare_ps=spare_ps):
                if kind in "VAF":
                    return
                dve.wait_ge(s_ready, number + 1)
                if kind == "T":
                    k = slice(TK * i, TK * i + TK)
                    dve.wait_ge(s_ctxT, NTHIRD * at.plus(2).n + i + 1)
                    nc.vector.tensor_tensor(ctxT[:, 1, k], spare_ps[:, 0:TK], ctxT[:, 0, k], ALU.subtract).then_inc(s_cl, 1)
                if kind == "K":
                    p = at.plus(2)
                    dve.wait_ge(s_kh, NTHIRD * p.n + i + 1)
                    if L is L0:
                        nc.vector.tensor_tensor(khl[:, 1, TK * i:TK * i + TK], spare_ps[:, 0:TK],
                                                khl[:, 0, TK * i:TK * i + TK], ALU.subtract).then_inc(s_kl, 1)
                    else:
                        nc.vector.scalar_tensor_tensor(khl[:, 1, TK * i:TK * i + TK], spare_ps[:, 0:TK], small["bk1"][:, :],
                                                       khl[:, 0, TK * i:TK * i + TK], ALU.add, ALU.subtract).then_inc(s_kl, 1)
                if kind == "M":
                    m = at.plus(1)
                    high, low = max_rows[0:L.tiles, 0, 0:L.tile], max_rows[0:L.tiles, 1, 0:L.tile]
                    nc.vector.tensor_scalar(high, spare_ps[0:L.tiles, 0:L.tile], 1.0 / BIG, None, ALU.mult).then_inc(s_high, 1)
                    dve.wait_ge(s_high, m.n + 1)
                    nc.vector.scalar_tensor_tensor(low, high, -BIG, spare_ps[0:L.tiles, 0:L.tile],
                                                   ALU.mult, ALU.add).then_inc(s_mr, 1)

            def drain_uses(at, uses, base, t, side):
                for kind, i, number in at_step(uses, base, t, side):
                    drain(at, kind, i, number)

            def reciprocals(n):
                dve.wait_ge(s_turned, n * L.uses_f)
                for h in range(2):
                    t5 = turned[:, :, 0:256 * S].rearrange("q i (s a j e) -> q i s a j e", s=S, a=2, j=4)
                    nc.vector.reciprocal(rden[:, h, 0:2 * S, :].rearrange("q (i s) j -> q i s j", i=2),
                                         t5[:, :, :, h, :, 16 * h + VD]).then_inc(s_rden, 1)

            def reduce_piece(at, p):
                if p == 0:
                    at_least(dve, s_neg, at.n)
                dve.wait_ge(s_piece, at.n * L.pieces + p + 1)
                nc.vector.reduce_max(max_part[0:L.tile, p // NTHIRD, p % NTHIRD:p % NTHIRD + 1], max_ps[p % 2][0:L.tile, 0:TK],
                                     AX.X).then_inc(s_red, 1)
                if p == L.pieces - 1:
                    dve.wait_ge(s_red, (at.n + 1) * L.pieces)
                    nc.vector.tensor_reduce(neg_max[0:L.tile, 0:L.tiles], max_part[0:L.tile, 0:L.tiles, :], AX.X, ALU.max,
                                            negate=True).then_inc(s_neg, 1)

            def prologue():
                for k, (at, kind, i) in enumerate(first_preps):
                    drain(at, kind, i, k, first_banks[k % len(first_banks)])
                for p in range(L.pieces):
                    reduce_piece(At(0, 0), p)
                drain(At(0, -1), "M", 0, len(first_preps))
                for p in range(early - early // spread):
                    reduce_piece(At(0, 1), p)

            def body(at, base, uses, has_f, has_m, has_p):
                for t in range(NKT):
                    if L is L1:
                        drain_uses(at, uses, base, t, 0)
                    for k in range(H + 2):
                        if k == H:
                            drain_uses(at, uses, base, t, 1)
                            if t == where["F", 1][0] + 1 and has_f:
                                reciprocals(at.n)
                        for ahead, p in searched(at, t, k):
                            reduce_piece(ahead, p)
                        if k == 0 and L is L0:
                            drain_uses(at, uses, base, t, 0)

            iterations(dve, body, prologue, lambda before: reciprocals(B))


def expert_weights(T, layer):
    NX = NE + 1 if layer == 0 else NE
    up = carve(T["kstack"][0][:, :], 0, [NX, FF * (1 + layer)])
    down = carve(T["kstack"][1][:, :], NTT * D, [NX, FF // 128, D])
    return up, down


def feed_forward(T, layer):
    nc, a, sem, bank, X, XnT, small = T["nc"], T["a"], T["sem"], T["bank"], T["X"], T["XnT"], T["small"]
    NX = NE + 1 if layer == 0 else NE
    UP = FF * (1 if layer == 0 else 2)
    NF = FF // 128
    gated = layer == 1
    UB = 2 if gated else 3
    DB = 2 if gated else 3
    HS = 4 if gated else 6
    assert NX * NF % UB == NX * NF % HS == NX % DB == 0
    n = f"f{layer}_"
    s_w = T[f"weights_loaded{layer}"]
    s_xh = sem(n + "token_high_ready")
    s_xl = sem(n + "token_low_ready")
    s_wh = sem(n + "weight_high_ready")
    s_wl = sem(n + "weight_low_ready")
    s_lg = sem(n + "logits_ready")
    s_d = sem(n + "logit_difference_ready")
    s_e = sem(n + "second_weight_ready")
    s_up = sem(n + "hidden_projected")
    s_si = sem(n + "silu_done")
    s_hid = sem(n + "hidden_ready") if gated else s_si
    s_dn = sem(n + "expert_projected")
    s_tmp = sem(n + "weighted")
    s_acc = sem(n + "accumulated")
    s_zero = sem(n + "total_zeroed")
    k0, k1, k2 = (T["kstack"][i][:, :] for i in range(3))
    wup, wdn = expert_weights(T, layer)
    x_parts = T["qh"], T["ql"]
    rooms = k0[:, 2 * NX * UP:], T["attnT"][:, :].bitcast(F16), T["khl"][:, :, :].rearrange("p a k -> p (a k)")
    wup_parts = [[rooms[e // 3][:, (e % 3 * 2 + part) * UP:(e % 3 * 2 + part + 1) * UP] for part in range(2)] for e in range(NX)]
    AHEAD = 2

    def makes_parts(c, e):
        if not isinstance(c, int):
            return [], []
        return [e + AHEAD] if e + AHEAD < NX else [], [e] if 1 <= e < NCH else []

    total = carve(k2[0:TT, :], 0, [NTT, D])
    hidden = [carve(k2, NTT * D + CW * i, [CW]) for i in range(HS)]
    gate = [T["ctxT"][:, i, 0:2 * CW].bitcast(F32) for i in range(2)]
    tmp = [T["probs"][0][0:TT, CH * D * i:CH * D * i + CH * D].rearrange("p (t d) -> p t d", t=CH) for i in range(DB)]
    row = T["probs"][1][0:TT, :]
    lg, *r = [row[:, NTT * NE * i:NTT * NE * (i + 1)].rearrange("p (t e) -> p t e", e=NE) for i in range(5)]
    comb = row[:, 640:640 + NTT * (NE + 1)].rearrange("p (t e) -> p t e", e=NE + 1)
    m = row[:, 800:800 + 8 * NTT].rearrange("p (k t) -> p k t", k=8)

    if layer == 0:
        s_mask = sem(n + "mask_loaded")
        s_all = sem(n + "mask_reduced")
    mask_row = T["qstack"][1][0:TT, :].bitcast(U8), T["qstack"][2][0:TT, :].bitcast(U8)
    mask_row = [m[:, SK * i:SK * i + SK] for m in mask_row for i in range(2)]
    keep, keep_scale = T["keep"], QK_UP * L1.hd ** -0.5

    with nc.Block() as block:
        if layer == 0:
            @block.sync
            def _(sp):
                src = a["mask"].rearrange("(t p) k -> p t k", p=TT)
                for c in range(NCH):
                    if c:
                        sp.wait_ge(s_all, c * CH)
                    for t in range(CH):
                        sp.dma_start(mask_row[t], src[:, CH * c + t, :]).then_inc(s_mask, 16)

        def before_hidden(c, u):
            return c * NX + (u - HS) // NF + 1

        def steps(eng, body):
            body(0)
            with eng.Fori(1, NCH) as c:
                body(c)

        @block.tensor
        def _(pe):
            for t in range(NTT):
                last = nc.tensor.matmul(bank[7][0:TT, NE * t:NE * t + NE], XnT[:, TT * t:TT * t + TT],
                                        small[f"routerT{layer}"][:, :], start=True, stop=True)
            last.then_inc(s_lg, 1)
            pe.wait_ge(s_w, 32)

            def project(ps, c, e, row):
                for k, (w, x) in enumerate(((0, 0), (1, 0), (0, 1))):
                    last = nc.tensor.matmul(ps[:, 0:CW], wup_parts[e][w][:, row:row + 128], x_parts[x][:, bass.ds(c * CW, CW)],
                                            start=k == 0, stop=k == 2)
                return last

            def up(c, e):
                if isinstance(c, int):
                    pe.wait_ge(s_wl, e + 1)
                    pe.wait_ge(s_xl, 1)
                elif e == 0:
                    pe.wait_ge(s_xl, NCH)
                for f in range(NF):
                    u = e * NF + f
                    number = c * (NX * NF) + u
                    at_least(pe, s_hid, number - UB + 1)
                    if gated:
                        project(bank[2 * (u % UB)], c, e, 128 * f)
                        last = project(bank[2 * (u % UB) + 1], c, e, FF + 128 * f)
                    else:
                        last = project(bank[u % UB], c, e, 128 * f)
                    last.then_inc(s_up, 1)

            def down(c, e):
                number = c * NX + e
                pe.wait_ge(s_hid, (number + 1) * NF)
                at_least(pe, s_tmp, number - DB + 1)
                for t in range(CH):
                    for f in range(NF):
                        last = nc.tensor.matmul(bank[4 + e % DB - (0 if gated else 1)][0:TT, D * t:D * t + D],
                                                hidden[(e * NF + f) % HS][:, TT * t:TT * t + TT], wdn[:, e, f, :],
                                                start=f == 0, stop=f == NF - 1)
                last.then_inc(s_dn, 1)

            def chunk(c):
                for e in range(NX):
                    up(c, e)
                    if e:
                        down(c, e - 1)
                down(c, NX - 1)
            steps(pe, chunk)

        @block.scalar
        def _(act):
            def token_high(c):
                nc.scalar.activation(x_parts[0][:, CW * c:CW * c + CW], XnT[:, CW * c:CW * c + CW], ACT.Copy).then_inc(s_xh, 1)

            def weight_high(e):
                nc.scalar.activation(wup_parts[e][0], wup[:, e, :], ACT.Copy, scale=QK_UP).then_inc(s_wh, 1)

            token_high(0)
            act.wait_ge(s_w, 32)
            for e in range(AHEAD):
                weight_high(e)
            act.wait_ge(s_d, 1)
            nc.scalar.activation(m[:, 3, :], m[:, 2, :], ACT.Exp).then_inc(s_e, 1)

            def chunk(c):
                for u in range(NX * NF):
                    number = c * (NX * NF) + u
                    experts, chunks = makes_parts(c, u // NF) if u % NF == 0 else ([], [])
                    for e in experts:
                        weight_high(e)
                    for k in chunks:
                        token_high(k)
                    act.wait_ge(s_up, number + 1)
                    if gated:
                        at_least(act, s_hid, number - 1)
                        nc.scalar.activation(gate[u % 2][:, :], bank[2 * (u % UB)][:, 0:CW], ACT.Silu, scale=1.0 / QK_UP).then_inc(s_si, 1)
                    else:
                        if not (isinstance(c, int) and number < HS):
                            act.wait_ge(s_dn, before_hidden(c, u))
                        nc.scalar.activation(hidden[u % HS][:, :], bank[u % UB][:, 0:CW], ACT.Silu, scale=1.0 / QK_UP).then_inc(s_si, 1)
            steps(act, chunk)

        @block.vector
        def _(dve):
            link = chain(dve, sem(n + "chain"))

            def over(v):
                return v.unsqueeze(2).to_broadcast([TT, NTT, NE])

            def token_low(c):
                k = slice(CW * c, CW * c + CW)
                dve.wait_ge(s_xh, c + 1)
                nc.vector.tensor_tensor(x_parts[1][:, k], XnT[:, k], x_parts[0][:, k], ALU.subtract).then_inc(s_xl, 1)

            def weight_low(e):
                dve.wait_ge(s_wh, e + 1)
                nc.vector.scalar_tensor_tensor(wup_parts[e][1], wup[:, e, :], QK_UP, wup_parts[e][0],
                                               ALU.mult, ALU.subtract).then_inc(s_wl, 1)

            token_low(0)
            for e in range(AHEAD):
                weight_low(e)
            dve.wait_ge(s_lg, 1)
            logits = bank[7][0:TT, 0:NTT * NE].rearrange("p (t e) -> p t e", e=NE)
            desc = small["desc"][0:TT, :].unsqueeze(1).to_broadcast([TT, NTT, NE])
            if layer == 0:
                link(nc.vector.tensor_tensor(lg[:, :, :], logits, small["router_b"][0:TT, :].unsqueeze(1).to_broadcast([TT, NTT, NE]), ALU.add))
            else:
                link(nc.vector.tensor_copy(lg[:, :, :], logits))
            cur = lg
            for k in range(2):
                link(nc.vector.reduce_max(m[:, k, :], cur[:, :, :], AX.X))
                link(nc.vector.tensor_tensor(r[2][:, :, :], cur[:, :, :], over(m[:, k, :]), ALU.is_equal))
                link(nc.vector.tensor_tensor(r[2][:, :, :], r[2][:, :, :], desc, ALU.mult))
                link(nc.vector.reduce_max(m[:, 4, :], r[2][:, :, :], AX.X))
                link(nc.vector.tensor_tensor(r[k][:, :, :], r[2][:, :, :], over(m[:, 4, :]), ALU.is_equal))
                if k == 0:
                    link(nc.vector.scalar_tensor_tensor(r[3][:, :, :], r[0][:, :, :], -1e30, lg[:, :, :], ALU.mult, ALU.add))
                    cur = r[3]
            nc.vector.tensor_tensor(m[:, 2, :], m[:, 1, :], m[:, 0, :], ALU.subtract).then_inc(s_d, 1)
            dve.wait_ge(s_e, 1)
            link(nc.vector.tensor_scalar(m[:, 5, :], m[:, 3, :], 1.0, None, ALU.add))
            link(nc.vector.reciprocal(m[:, 6, :], m[:, 5, :]))
            link(nc.vector.tensor_tensor(m[:, 7, :], m[:, 6, :], m[:, 3, :], ALU.mult))
            link(nc.vector.tensor_tensor(r[2][:, :, :], r[0][:, :, :], over(m[:, 6, :]), ALU.mult))
            link(nc.vector.tensor_tensor(r[3][:, :, :], r[1][:, :, :], over(m[:, 7, :]), ALU.mult))
            link(nc.vector.memset(comb[:, :, NE:NE + 1], 1.0))
            link(nc.vector.tensor_tensor(comb[:, :, 0:NE], r[2][:, :, :], r[3][:, :, :], ALU.add))

            def take(c, e):
                number = c * NX + e
                dve.wait_ge(s_dn, number + 1)
                w = comb[:, bass.ds(c * CH, CH), e:e + 1].to_broadcast([TT, CH, D])
                at_least(dve, s_acc, number - DB + 1)
                nc.vector.tensor_tensor(tmp[e % DB][:, :, :],
                                        bank[4 + e % DB - (0 if gated else 1)][0:TT, :].rearrange("p (t d) -> p t d", t=CH),
                                        w, ALU.mult).then_inc(s_tmp, 1)

            def all_masked(c, t):
                if t == 0:
                    dve.wait_ge(s_mask, 16 * CH * (c + 1))
                nc.vector.tensor_reduce(keep[:, bass.ds(CH * c + t, 1)], mask_row[t], AX.X, ALU.min).then_inc(s_all, 1)

            def chunk(c):
                for e in range(NX):
                    experts, chunks = makes_parts(c, e)
                    for k in experts:
                        weight_low(k)
                    for k in chunks:
                        token_low(k)
                    if layer == 0 and e < CH:
                        all_masked(c, e)
                    if gated:
                        for f in range(NF):
                            u = e * NF + f
                            number = c * (NX * NF) + u
                            dve.wait_ge(s_si, number + 1)
                            if not (isinstance(c, int) and number < HS):
                                dve.wait_ge(s_dn, before_hidden(c, u))
                            nc.vector.scalar_tensor_tensor(hidden[u % HS][:, :], bank[2 * (u % UB) + 1][:, 0:CW], 1.0 / QK_UP,
                                                           gate[u % 2][:, :], ALU.mult, ALU.mult).then_inc(s_hid, 1)
                    if e:
                        take(c, e - 1)
                take(c, NX - 1)
            steps(dve, chunk)
            if layer == 0:
                dve.wait_ge(s_all, NTT)
                link(nc.vector.tensor_scalar(keep[:, :], keep[:, :], -keep_scale, keep_scale, ALU.mult, ALU.add))
            g = T["tg"][0:TT, 2 + layer:3 + layer]
            for c in range(NCH):
                dve.wait_ge(s_acc, (c + 1) * NX)
                k = slice(CH * c, CH * c + CH)
                nc.vector.scalar_tensor_tensor(X[:, k, :], total[:, k, :], g, X[:, k, :], ALU.mult, ALU.add)

        @block.gpsimd
        def _(pool):
            nc.gpsimd.memset(total[:, :, :], 0.0).then_inc(s_zero, 1)
            pool.wait_ge(s_zero, 1)

            def chunk(c):
                for e in range(NX):
                    number = c * NX + e
                    pool.wait_ge(s_tmp, number + 1)
                    at_least(pool, s_acc, number)
                    apart(pool)
                    k = total[:, bass.ds(c * CH, CH), :]
                    nc.gpsimd.tensor_tensor(k, k, tmp[e % DB][:, :, :], ALU.add).then_inc(s_acc, 1)
            steps(pool, chunk)


def kernel(**inputs):
    import concourse.bacc as bacc
    from concourse.bass_utils import run_bass_kernel_spmd

    x = {k: np.ascontiguousarray(v) for k, v in inputs.items()}
    arrays = {
        "x": x["x"].reshape(TOKENS, D), "ctx": x["ctx_1024"], "mask": x["mask_BxSxS2_bk1"].reshape(TOKENS, SK),
        "wup0": np.concatenate([x["L0_ffn_w_up"], x["L0_ffn_shared_w_up"]]).transpose(2, 0, 1),
        "wdn0": np.concatenate([x["L0_ffn_w_down"], x["L0_ffn_shared_w_down"]]).reshape(NE + 1, D, FF // 128, 128).transpose(3, 0, 2, 1),
        "wup1": x["L1_ffn_w12"].transpose(2, 0, 1),
        "wdn1": x["L1_ffn_w3"].reshape(NE, D, FF // 128, 128).transpose(3, 0, 2, 1),
        "ones_rows": np.repeat(np.array([[BIG], [1.0]], np.float16), SK, axis=1),
        "big_ident": np.tile(np.eye(SQ) * BIG, L1.group_heads).astype(np.float16),
    }
    parts = {
        "gates": np.concatenate([x["g_xattn"], x["g_ffn"]]),
        "lambdas": np.concatenate([x[f"L0_xattn_{n}"] for n in ("lq1", "lk1", "lq2", "lk2")]),
        "bp0": x["L0_xattn_bp"], "bp1": x["L1_xattn_bo"], "bq1": x["L1_xattn_bq"], "bv1": x["L1_xattn_bv"],
        "router_b": x["L0_ffn_router_b"], "routerT0": x["L0_ffn_router_w"].T, "routerT1": x["L1_ffn_gate_w"].T,
        "WqT0": x["L0_xattn_Wq"].T, "WkT0": x["L0_xattn_Wk"].T, "WvT0": x["L0_xattn_Wv"].T, "WpT0": x["L0_xattn_Wp"].T,
        "WqT1": x["L1_xattn_Wq"].T, "WkT1": x["L1_xattn_Wk"].T, "WvT1": x["L1_xattn_Wv"].T, "WpT1": x["L1_xattn_Wo"].T,
        "ident": np.eye(128, dtype=np.float32), "desc": np.arange(NE, 0, -1).astype(np.float32),
    }
    for i, L in enumerate((L0, L1)):
        own = np.arange(128)[:, None] % L.group_dims // L.hd == np.arange(L.group_heads)
        parts[f"headsel{i}"] = own.astype(np.float32)
    arrays["rows"] = np.concatenate([parts[n] for n in ROWS])
    arrays["wide"] = np.concatenate([parts[n] for n in WIDE], axis=1)
    arrays["columns"] = np.stack([np.tile(x["L0_xattn_subln_w"], VH), x["L1_xattn_bk"]], axis=1)
    nc = bacc.Bacc("TRN2", target_bir_lowering=False, num_devices=1)
    feeds, aps = {}, {}
    for name, array in arrays.items():
        array = np.ascontiguousarray(array)
        feeds[f"in_{name}"] = array
        aps[name] = nc.dram_tensor(f"in_{name}", array.shape, mybir.dt.from_np(array.dtype), kind="ExternalInput").ap()
    out = nc.dram_tensor("result", (TOKENS, D), F32, kind="ExternalOutput").ap()
    build(nc, aps, out)
    got = run_bass_kernel_spmd(nc, [feeds], core_ids=[0])
    return got.results[0]["result"].reshape(B, SQ, D)
```
